# Optimizing a Trainium2 kernel written in Bass

```python
import numpy as np
import jax
import jax.numpy as jnp

def _softmax(x, axis=-1):
    return jax.nn.softmax(x, axis=axis)

def _gelu(x):
    return jax.nn.gelu(x, approximate=True)

def _silu(x):
    return jax.nn.silu(x)

def _sigmoid(x):
    return jax.nn.sigmoid(x)

def _layernorm(x, axis=-1, eps=1e-05):
    m = jnp.mean(x, axis=axis, keepdims=True)
    v = jnp.var(x, axis=axis, keepdims=True)
    return (x - m) / jnp.sqrt(v + eps)

def _scatter_add(tgt, idx, src, axis=0):
    return tgt.at[idx].add(src)

def _segment_sum(src, seg, n):
    return jax.ops.segment_sum(src, seg, n)
kernel_name = 'mk_seq_postln_d1_jaxref_r8_96ee70'

def setup_inputs(seed: int=0):
    np.random.seed(seed)
    _w = jnp.asarray

    def _L0_attn_setup():
        import jax, jax.numpy as jnp
        import numpy as np
        D_MODEL = 128
        D_INNER = 256
        D_STATE = 16
        D_CONV = 4
        DT_RANK = 64
        N_EXPERTS = 8
        TOP_K = 2
        FFN = 512
        EPS = 1e-05

        def rmsnorm(x, w):
            return x * jax.lax.rsqrt(jnp.mean(x * x, axis=-1, keepdims=True) + EPS) * w

        def mamba_block(x, in_proj_w, conv_w, conv_b, x_proj_w, dt_proj_w, dt_proj_b, A_log, D_skip, out_proj_w):
            B, L, _ = x.shape
            xz = x @ in_proj_w
            xi, z = jnp.split(xz, 2, axis=-1)
            xc = jax.lax.conv_general_dilated(xi.transpose(0, 2, 1), conv_w, window_strides=(1,), padding=[(D_CONV - 1, 0)], feature_group_count=D_INNER, dimension_numbers=('NCH', 'OIH', 'NCH'))
            xi = jax.nn.silu(xc.transpose(0, 2, 1) + conv_b)
            dbc = xi @ x_proj_w
            delta = jax.nn.softplus(dbc[..., :DT_RANK] @ dt_proj_w + dt_proj_b)
            Bm = dbc[..., DT_RANK:DT_RANK + D_STATE]
            Cm = dbc[..., DT_RANK + D_STATE:]
            A = -jnp.exp(A_log)

            def step(h, inp):
                d_t, B_t, C_t, x_t = inp
                dA = jnp.exp(d_t[..., None] * A)
                h = dA * h + (d_t * x_t)[..., None] * B_t[:, None, :]
                y = jnp.einsum('ben,bn->be', h, C_t)
                return (h, y)
            h0 = jnp.zeros((B, D_INNER, D_STATE), dtype=x.dtype)
            xs = (delta.transpose(1, 0, 2), Bm.transpose(1, 0, 2), Cm.transpose(1, 0, 2), xi.transpose(1, 0, 2))
            _, ys = jax.lax.scan(step, h0, xs)
            y = ys.transpose(1, 0, 2) + D_skip * xi
            y = y * jax.nn.silu(z)
            return y @ out_proj_w

        def moe_block(x, router_w, Wg, Wu, Wd):
            B, L, D = x.shape
            hs = x.reshape(-1, D)
            router_logits = hs @ router_w
            rw = jax.nn.softmax(router_logits.astype(jnp.float32), axis=-1)
            top_w, sel = jax.lax.top_k(rw, TOP_K)
            top_w = top_w.astype(hs.dtype)
            out = jnp.zeros_like(hs)
            for e in range(N_EXPERTS):
                w_e = jnp.where(sel == e, top_w, 0.0).sum(axis=-1)
                ye = jax.nn.silu(hs @ Wg[e]) * (hs @ Wu[e]) @ Wd[e]
                out = out + w_e[:, None] * ye
            return (out.reshape(B, L, D), router_logits)
        key = jax.random.key(seed)
        ks = jax.random.split(key, 16)
        s = 0.02
        inp = {'hidden_states': jax.random.normal(ks[0], (2, 256, D_MODEL), jnp.float32), 'rms1_w': jnp.ones((D_MODEL,), jnp.float32), 'rms2_w': jnp.ones((D_MODEL,), jnp.float32), 'in_proj_w': jax.random.normal(ks[1], (D_MODEL, 2 * D_INNER), jnp.float32) * s, 'conv_w': jax.random.normal(ks[2], (D_INNER, 1, D_CONV), jnp.float32) * s, 'conv_b': jnp.zeros((D_INNER,), jnp.float32), 'x_proj_w': jax.random.normal(ks[3], (D_INNER, DT_RANK + 2 * D_STATE), jnp.float32) * s, 'dt_proj_w': jax.random.normal(ks[4], (DT_RANK, D_INNER), jnp.float32) * s, 'dt_proj_b': jnp.zeros((D_INNER,), jnp.float32), 'A_log': jnp.log(jnp.tile(jnp.arange(1, D_STATE + 1, dtype=jnp.float32), (D_INNER, 1))), 'D_skip': jnp.ones((D_INNER,), jnp.float32), 'out_proj_w': jax.random.normal(ks[5], (D_INNER, D_MODEL), jnp.float32) * s, 'router_w': jax.random.normal(ks[6], (D_MODEL, N_EXPERTS), jnp.float32) * s, 'Wg': jax.random.normal(ks[7], (N_EXPERTS, D_MODEL, FFN), jnp.float32) * s, 'Wu': jax.random.normal(ks[8], (N_EXPERTS, D_MODEL, FFN), jnp.float32) * s, 'Wd': jax.random.normal(ks[9], (N_EXPERTS, FFN, D_MODEL), jnp.float32) * s}
        return inp
    _L0_attn_in = _L0_attn_setup()

    def _L0_ffn_setup():
        import jax, jax.numpy as jnp
        import numpy as np
        D_MODEL, D_FF, RANK = (128, 512, 32)
        B, S = (4, 512)
        key = jax.random.key(seed)
        ks = jax.random.split(key, 7)
        return {'x': jax.random.normal(ks[0], (B, S, D_MODEL), dtype=jnp.float32), 'U1': jax.random.normal(ks[1], (D_MODEL, RANK), dtype=jnp.float32) * 0.02, 'V1': jax.random.normal(ks[2], (RANK, D_FF), dtype=jnp.float32) * 0.02, 'b1': jnp.zeros((D_FF,), dtype=jnp.float32), 'U2': jax.random.normal(ks[3], (D_FF, RANK), dtype=jnp.float32) * 0.02, 'V2': jax.random.normal(ks[4], (RANK, D_MODEL), dtype=jnp.float32) * 0.02, 'b2': jnp.zeros((D_MODEL,), dtype=jnp.float32)}
    _L0_ffn_in = _L0_ffn_setup()
    _d = {'L0_attn_hidden_states': _L0_attn_in['hidden_states'], 'L0_attn_rms1_w': _L0_attn_in['rms1_w'], 'L0_attn_rms2_w': _L0_attn_in['rms2_w'], 'L0_attn_in_proj_w': _L0_attn_in['in_proj_w'], 'L0_attn_conv_w': _L0_attn_in['conv_w'], 'L0_attn_conv_b': _L0_attn_in['conv_b'], 'L0_attn_x_proj_w': _L0_attn_in['x_proj_w'], 'L0_attn_dt_proj_w': _L0_attn_in['dt_proj_w'], 'L0_attn_dt_proj_b': _L0_attn_in['dt_proj_b'], 'L0_attn_A_log': _L0_attn_in['A_log'], 'L0_attn_D_skip': _L0_attn_in['D_skip'], 'L0_attn_out_proj_w': _L0_attn_in['out_proj_w'], 'L0_attn_router_w': _L0_attn_in['router_w'], 'L0_attn_Wg': _L0_attn_in['Wg'], 'L0_attn_Wu': _L0_attn_in['Wu'], 'L0_attn_Wd': _L0_attn_in['Wd'], 'L0_ffn_U1': _L0_ffn_in['U1'], 'L0_ffn_V1': _L0_ffn_in['V1'], 'L0_ffn_b1': _L0_ffn_in['b1'], 'L0_ffn_U2': _L0_ffn_in['U2'], 'L0_ffn_V2': _L0_ffn_in['V2'], 'L0_ffn_b2': _L0_ffn_in['b2']}
    _x0 = _d['L0_attn_hidden_states']
    _d['L0_attn_hidden_states'] = jax.random.normal(jax.random.fold_in(jax.random.key(seed), 1), (2, 2048, 128), dtype=_x0.dtype)
    del _x0
    return _d

def reference(L0_attn_hidden_states, L0_attn_rms1_w, L0_attn_rms2_w, L0_attn_in_proj_w, L0_attn_conv_w, L0_attn_conv_b, L0_attn_x_proj_w, L0_attn_dt_proj_w, L0_attn_dt_proj_b, L0_attn_A_log, L0_attn_D_skip, L0_attn_out_proj_w, L0_attn_router_w, L0_attn_Wg, L0_attn_Wu, L0_attn_Wd, L0_ffn_U1, L0_ffn_V1, L0_ffn_b1, L0_ffn_U2, L0_ffn_V2, L0_ffn_b2):

    def _L0_attn_ref(hidden_states, rms1_w, rms2_w, in_proj_w, conv_w, conv_b, x_proj_w, dt_proj_w, dt_proj_b, A_log, D_skip, out_proj_w, router_w, Wg, Wu, Wd):
        import jax, jax.numpy as jnp
        import numpy as np
        D_MODEL = 128
        D_INNER = 256
        D_STATE = 16
        D_CONV = 4
        DT_RANK = 64
        N_EXPERTS = 8
        TOP_K = 2
        FFN = 512
        EPS = 1e-05

        def rmsnorm(x, w):
            return x * jax.lax.rsqrt(jnp.mean(x * x, axis=-1, keepdims=True) + EPS) * w

        def mamba_block(x, in_proj_w, conv_w, conv_b, x_proj_w, dt_proj_w, dt_proj_b, A_log, D_skip, out_proj_w):
            B, L, _ = x.shape
            xz = x @ in_proj_w
            xi, z = jnp.split(xz, 2, axis=-1)
            xc = jax.lax.conv_general_dilated(xi.transpose(0, 2, 1), conv_w, window_strides=(1,), padding=[(D_CONV - 1, 0)], feature_group_count=D_INNER, dimension_numbers=('NCH', 'OIH', 'NCH'))
            xi = jax.nn.silu(xc.transpose(0, 2, 1) + conv_b)
            dbc = xi @ x_proj_w
            delta = jax.nn.softplus(dbc[..., :DT_RANK] @ dt_proj_w + dt_proj_b)
            Bm = dbc[..., DT_RANK:DT_RANK + D_STATE]
            Cm = dbc[..., DT_RANK + D_STATE:]
            A = -jnp.exp(A_log)

            def step(h, inp):
                d_t, B_t, C_t, x_t = inp
                dA = jnp.exp(d_t[..., None] * A)
                h = dA * h + (d_t * x_t)[..., None] * B_t[:, None, :]
                y = jnp.einsum('ben,bn->be', h, C_t)
                return (h, y)
            h0 = jnp.zeros((B, D_INNER, D_STATE), dtype=x.dtype)
            xs = (delta.transpose(1, 0, 2), Bm.transpose(1, 0, 2), Cm.transpose(1, 0, 2), xi.transpose(1, 0, 2))
            _, ys = jax.lax.scan(step, h0, xs)
            y = ys.transpose(1, 0, 2) + D_skip * xi
            y = y * jax.nn.silu(z)
            return y @ out_proj_w

        def moe_block(x, router_w, Wg, Wu, Wd):
            B, L, D = x.shape
            hs = x.reshape(-1, D)
            router_logits = hs @ router_w
            rw = jax.nn.softmax(router_logits.astype(jnp.float32), axis=-1)
            top_w, sel = jax.lax.top_k(rw, TOP_K)
            top_w = top_w.astype(hs.dtype)
            out = jnp.zeros_like(hs)
            for e in range(N_EXPERTS):
                w_e = jnp.where(sel == e, top_w, 0.0).sum(axis=-1)
                ye = jax.nn.silu(hs @ Wg[e]) * (hs @ Wu[e]) @ Wd[e]
                out = out + w_e[:, None] * ye
            return (out.reshape(B, L, D), router_logits)
        residual = hidden_states
        h = rmsnorm(hidden_states, rms1_w)
        h = mamba_block(h, in_proj_w, conv_w, conv_b, x_proj_w, dt_proj_w, dt_proj_b, A_log, D_skip, out_proj_w)
        h = residual + h
        residual = h
        h = rmsnorm(h, rms2_w)
        h, router_logits = moe_block(h, router_w, Wg, Wu, Wd)
        h = residual + h
        return h

    def _L0_ffn_ref(x, U1, V1, b1, U2, V2, b2):
        import jax, jax.numpy as jnp
        import numpy as np
        D_MODEL, D_FF, RANK = (128, 512, 32)
        B, S = (4, 512)
        P = jnp.einsum('bsd,dr->bsr', x, U1)
        H = jax.nn.gelu(jnp.einsum('bsr,rf->bsf', P, V1) + b1)
        Q = jnp.einsum('bsf,fr->bsr', H, U2)
        return jnp.einsum('bsr,rd->bsd', Q, V2) + b2
    x = L0_attn_hidden_states
    x = _layernorm(x + _L0_attn_ref(x, L0_attn_rms1_w, L0_attn_rms2_w, L0_attn_in_proj_w, L0_attn_conv_w, L0_attn_conv_b, L0_attn_x_proj_w, L0_attn_dt_proj_w, L0_attn_dt_proj_b, L0_attn_A_log, L0_attn_D_skip, L0_attn_out_proj_w, L0_attn_router_w, L0_attn_Wg, L0_attn_Wu, L0_attn_Wd), axis=-1)
    x = _layernorm(x + _L0_ffn_ref(x, L0_ffn_U1, L0_ffn_V1, L0_ffn_b1, L0_ffn_U2, L0_ffn_V2, L0_ffn_b2), axis=-1)
    return x

_drawn_inputs = setup_inputs


def setup_inputs(seed=0):
    import zlib

    import numpy as np

    out = dict(_drawn_inputs(seed))
    spreads = {'L0_attn_rms1_w': (1.0, 0.6),
     'L0_attn_rms2_w': (1.0, 0.6),
     'L0_attn_conv_b': (0.0, 0.8),
     'L0_attn_dt_proj_b': (0.0, 0.8),
     'L0_attn_D_skip': (1.0, 0.6),
     'L0_ffn_b1': (0.0, 0.8),
     'L0_ffn_b2': (0.0, 0.328)}
    factors = {'L0_attn_in_proj_w': 8.0,
     'L0_attn_conv_w': 8.0,
     'L0_attn_x_proj_w': 8.0,
     'L0_attn_dt_proj_w': 8.0,
     'L0_attn_A_log': 8.0,
     'L0_attn_out_proj_w': 8.0,
     'L0_attn_router_w': 8.0,
     'L0_attn_Wg': 8.0,
     'L0_attn_Wu': 8.0,
     'L0_attn_Wd': 8.0,
     'L0_ffn_U1': 8.0,
     'L0_ffn_V1': 8.0,
     'L0_ffn_U2': 8.0,
     'L0_ffn_V2': 8.0}
    for name, (base, spread) in spreads.items():
        noise = np.random.default_rng([zlib.crc32(name.encode()), seed]).standard_normal(out[name].shape)
        drawn = base * np.exp(spread * noise) if base else spread * noise
        out[name] = jnp.asarray(drawn.astype(out[name].dtype))
    for name, factor in factors.items():
        out[name] = (out[name] * factor).astype(out[name].dtype)
    return out
```

```python
import numpy as np
import concourse.bass as bass
from concourse import mybir
from contextlib import ExitStack

F32 = mybir.dt.float32
BF16 = mybir.dt.bfloat16
ALU = mybir.AluOpType
ACT = mybir.ActivationFunctionType
AX = mybir.AxisListType

P = 128
B, L, D = 2, 2048, 128
DI = 256
NH = DI // P
NS = 16
NTAP = 4
R = 64
NE = 8
FFN = 512
NQ = FFN // P
RANK = 32
T = 512
NJ = T // P
NC = B * L // T
ADDS = NS - 1
UNITS = NE * NQ
LAG = 8
EPS = 1e-5

MISC = {
    "C_out": 2, "C_T": 4, "C_router": 6,
    "E_T": 12, "E_P": 13, "E_H0": 14, "E_H1": 15, "E_H2": 16, "E_H3": 17, "A_T": 18, "E_Q": 19, "E_out": 20,
    "A_xi0": 21, "A_xi1": 22, "A_z0": 23, "A_z1": 24, "A_dt": 26, "A_BC": 27, "A_dd0": 28, "A_dd1": 29,
}
ORDER = sorted(MISC, key=MISC.get)


class Step:

    def __init__(self, i0, j=0):
        self.i0, self.j = i0, j

    def chunk(self, stage):
        return self.i0 + {"A": 1, "B": 0, "C": -1, "D": -1, "tail": -2, "E": -2}[stage]

    def has(self, stage):
        return 0 <= self.chunk(stage) < NC

    def parity(self, stage):
        return self.chunk(stage) % 2

    def time(self, stage):
        return self.chunk(stage) // 2 + self.j

    def count(self, stage, per_chunk, offset):
        return per_chunk * self.chunk(stage) + offset + per_chunk * 2 * self.j

    def misc(self, name):
        before = 0
        for i in range(-1, self.i0):
            before += sum(Step(i).has(n[0]) for n in ORDER)
        here = [n for n in ORDER if self.has(n[0])]
        return before + here.index(name) + len(ORDER) * 2 * self.j


def wait(eng, sem, value):
    if type(value) is int and value <= 0:
        return
    eng.wait_ge(sem, value)


def run_pipeline(eng, iteration):
    for i in (-1, 0, 1):
        iteration(Step(i))
    with eng.Fori(0, 2, 1) as j:
        iteration(Step(2, j))
        iteration(Step(3, j))
    for i in range(6, NC + 2):
        iteration(Step(i))


def build(nc, hidden, rms1_w, rms2_w, in_proj_w, conv_w, conv_b, x_proj_w, dt_proj_w, dt_proj_b, A_log, D_skip,
          out_proj_w, router_w, Wg, Wu, Wd, U1, V1, b1, U2, V2, b2, out):
    ctx = ExitStack()
    with ctx:
        ctx.enter_context(nc.allow_non_contiguous_dma(reason="small per-channel columns"))

        def sb(name, shape, dt=F32):
            return ctx.enter_context(nc.sbuf_tensor(name, shape, dt))

        def sem(name):
            return ctx.enter_context(nc.semaphore(name))

        w_in = sb("w_in", [P, 2 * DI])
        w_conv = sb("w_conv", [P, NH, NTAP])
        b_conv = sb("b_conv", [P, NH])
        w_x = sb("w_x", [P, NH, R + 2 * NS])
        w_bc = sb("w_bc", [P, NH, 3, 2 * NS])
        w_dt = sb("w_dt", [R, DI])
        b_dt = sb("b_dt", [P, NH])
        a_neg = sb("a_neg", [P, NH, NS])
        d_skip = sb("d_skip", [P, NH])
        w_out = sb("w_out", [P, NH, D])
        w_router = sb("w_router", [P, NE])
        w_rms1 = sb("w_rms1", [P, 1])
        w_rms2 = sb("w_rms2", [P, 1])
        w_gate = sb("w_gate", [P, NE, FFN])
        w_up = sb("w_up", [P, NE, FFN])
        w_down = sb("w_down", [P, NE, NQ, D])
        w_u1 = sb("w_u1", [P, RANK])
        w_v1 = sb("w_v1", [RANK, FFN])
        b_v1 = sb("b_v1", [P, NQ])
        w_u2 = sb("w_u2", [P, NQ, RANK])
        w_v2 = sb("w_v2", [RANK + 1, D])
        ident = sb("ident", [P, P])
        pick = sb("pick", [3 * 2 * NS, 2 * NS, P], BF16)
        power = sb("power", [P, NJ])
        per_d, one, eps = sb("per_d", [P, NJ]), sb("one", [P, NJ]), sb("eps", [P, NJ])
        before = sb("before", [P, NE, NE])
        x = [sb(f"x_in{q}", [P, NJ, D]) for q in range(2)]
        ss1 = sb("ss1", [P, NJ])
        ms1 = sb("ms1", [P, NJ])
        rstd1 = sb("rstd1", [P, NJ])
        work = sb("work", [P, 2 * NH, T])
        tokens = sb("tokens", [P, NJ, D])
        columns = sb("columns", [P, T])
        sums = sb("sums", [P, NJ, D])
        narrow = sb("narrow", [R, T])
        xn, xnT = tokens, columns
        xi = sb("xi", [P, NH, NTAP - 1 + T])
        halo = [sb(f"halo{q}", [P, NH, NTAP - 1]) for q in range(2)]
        conv = work[:, 0:NH, :]
        th_conv = work[:, NH:, :]
        th_z = sb("th_z", [P, T])
        act_x = sb("act_x", [P, NH, T])
        gate_z = [sb(f"gate_z{q}", [P, NH, T]) for q in range(2)]
        dt_in = narrow
        bc = [sb(f"bc{q}", [3 * 2 * NS, T], BF16) for q in range(2)]
        bc_rest = th_z[0:3 * 2 * NS, :]
        bc_mid = sb("bc_mid", [3 * 2 * NS, T], BF16)
        bc_rest2 = tokens[0:3 * 2 * NS, :, :].rearrange("p j d -> p (j d)")
        dt_raw = work[:, 0:NH, :]
        dt_soft = work[:, NH:, :]
        delta = [sb(f"delta{q}", [P, NH, T]) for q in range(2)]
        dx = [sb(f"dx{q}", [P, NH, T]) for q in range(2)]
        decay = sb("decay", [P, 3, NH, T])
        h = sb("h", [P, 2, NH, T])
        carry = [sb(f"carry{q}", [P, NS, NH]) for q in range(2)]
        hc = sb("hc", [P, 2, NH, T])
        y_even = [sb(f"y_even{q}", [P, NH, T]) for q in range(2)]
        y_odd = sb("y_odd", [P, NH, T])
        y_gated = work[:, 0:NH, :]
        res = sums
        ss2 = sb("ss2", [P, NJ])
        ms2 = sb("ms2", [P, NJ])
        rstd2 = sb("rstd2", [P, NJ])
        hn = tokens
        hT = [sb(f"hT{q}", [P, T]) for q in range(2)]
        logits = sb("logits", [P, NJ, NE])
        top = sb("top", [P, NJ])
        shifted = sb("shifted", [P, NJ, NE])
        expo = sb("expo", [P, NJ, NE])
        beats = sb("beats", [P, NJ, NE, NE])
        ties = sb("ties", [P, NJ, NE, NE])
        ties2 = sb("ties2", [P, NJ, NE, NE])
        beats2 = sb("beats2", [P, NJ, NE, NE])
        rank = sb("rank", [P, NJ, NE])
        denom = sb("denom", [P, NJ])
        rdenom = sb("rdenom", [P, NJ])
        chosen = sb("chosen", [P, NJ, NE])
        weight = [sb(f"weight{q}", [P, NJ, NE]) for q in range(2)]
        th_gate = sb("th_gate", [P, 2, T])
        hid = sb("hid", [P, 2, NQ, T])
        acc = [sb(f"acc{q}", [P, NJ, D]) for q in range(2)]
        stats = sb("stats", [P, NJ, 6])
        mv = sb("mv", [P, NJ, 2])
        var = sb("var", [P, NJ])
        rstd = sb("rstd", [P, NJ])
        x1 = sb("x_mid", [P, NJ, D])
        x1T = columns
        p_ffn = narrow[0:RANK, :]
        h_ffn = work
        q_ffn = sb("q_ffn", [RANK + 1, T])
        r2 = sums
        stats2 = sb("stats2", [P, NJ, 6])
        mv2 = sb("mv2", [P, NJ, 2])
        var2 = sb("var2", [P, NJ])
        rstd_b = sb("rstd_b", [P, NJ])
        y_out = [sb(f"y_out{q}", [P, NJ, D]) for q in range(2)]

        bank = [ctx.enter_context(nc.psum_tensor(f"bank{i}", [P, T], F32)) for i in range(8)]
        u_bank, b_bank, c_bank, g_bank, up_bank, down_bank, misc = (
            bank[0], bank[1], bank[2], (bank[3], bank[4]), bank[5], bank[6], bank[7])
        misc_tok = misc[:, :].rearrange("p (j d) -> p j d", j=NJ)
        down_tok = down_bank[:, :].rearrange("p (j d) -> p j d", j=NJ)

        mamba_weights, expert_weights, ffn_weights = sem("mamba_weights"), sem("expert_weights"), sem("ffn_weights")
        x_loaded = [sem(f"x_loaded{q}") for q in range(2)]
        stored = [sem(f"stored{q}") for q in range(2)]
        const_made, sel_made, a_exp, prepared, gates_scaled = (
            sem("const_made"), sem("sel_made"), sem("a_exp"), sem("prepared"), sem("gates_scaled"))
        misc_filled, misc_taken = sem("misc_filled"), sem("misc_taken")
        ss1_ready, ms1_ready, rstd1_ready, xn_ready = sem("ss1_ready"), sem("ms1_ready"), sem("rstd1_ready"), sem("xn_ready")
        halo_ready, halo_saved, tap0_ready, tap_done, th_conv_ready, act_x_ready = (
            sem("halo_ready"), sem("halo_saved"), sem("tap0_ready"), sem("tap_done"), sem("th_conv_ready"), sem("act_x_ready"))
        th_z_ready = sem("th_z_ready")
        mid_ready, rest2_ready, bc_ready = sem("mid_ready"), sem("rest2_ready"), sem("bc_ready")
        soft_step, soft_ready, delta_ready, dx_ready, y_init = (
            sem("soft_step"), sem("soft_ready"), sem("delta_ready"), sem("dx_ready"), sem("y_init"))
        b_filled, c_filled, decay_ready, u_ready, scanned, hc_ready, carried, added = (
            sem("b_filled"), sem("c_filled"), sem("decay_ready"), sem("u_ready"), sem("scanned"), sem("hc_ready"),
            sem("carried"), sem("added"))
        y_summed, y_ready, ss2_ready, ms2_ready, rstd2_ready, hn_ready, acc_init = (
            sem("y_summed"), sem("y_ready"), sem("ss2_ready"), sem("ms2_ready"), sem("rstd2_ready"), sem("hn_ready"),
            sem("acc_init"))
        top_ready, shifted_ready, expo_ready, route_step, weight_ready = (
            sem("top_ready"), sem("shifted_ready"), sem("expo_ready"), sem("route_step"), sem("weight_ready"))
        gate_filled, up_filled, th_gate_ready, silu_ready, hid_ready, down_filled, moe_added = (
            sem("gate_filled"), sem("up_filled"), sem("th_gate_ready"), sem("silu_ready"), sem("hid_ready"),
            sem("down_filled"), sem("moe_added"))
        stats_ready, mv_ready, var_ready, rstd_ready, x1_ready, h_act = (
            sem("stats_ready"), sem("mv_ready"), sem("var_ready"), sem("rstd_ready"), sem("x1_ready"), sem("h_act"))
        stats2_ready, mv2_ready, var2_ready, rstd_b_ready, y_out_ready = (
            sem("stats2_ready"), sem("mv2_ready"), sem("var2_ready"), sem("rstd_b_ready"), sem("y_out_ready"))

        block = ctx.enter_context(nc.Block())

        def chunk_rows(dram, s, stage):
            tiles = dram[s.parity(stage), :, :].rearrange("(t j p) d -> t p j d", j=NJ, p=P)
            return tiles[s.time(stage), :, :, :]

        def additions(n):
            return 1 if n < 2 else n

        N_MAMBA, N_EXPERT, N_FFN = 13, 3, 6

        @block.sync
        def _(sp):
            sp.dma_start(w_in[:, :], in_proj_w).then_inc(mamba_weights, 16)
            sp.dma_start(w_rms1[:, :], rms1_w.rearrange("(p a) -> p a", a=1)).then_inc(mamba_weights, 16)
            sp.dma_start(w_conv[:, :, :], conv_w.rearrange("(h p) a k -> p h (a k)", p=P)).then_inc(mamba_weights, 16)
            sp.dma_start(b_conv[:, :], conv_b.rearrange("(h p) -> p h", p=P)).then_inc(mamba_weights, 16)
            sp.dma_start(w_x[:, :, :], x_proj_w.rearrange("(h p) n -> p h n", p=P)).then_inc(mamba_weights, 16)
            sp.dma_start(w_dt[:, :], dt_proj_w).then_inc(mamba_weights, 16)
            sp.dma_start(b_dt[:, :], dt_proj_b.rearrange("(h p) -> p h", p=P)).then_inc(mamba_weights, 16)
            sp.dma_start(a_neg[:, :, :], A_log.rearrange("(h p) n -> p h n", p=P)).then_inc(mamba_weights, 16)
            sp.dma_start(d_skip[:, :], D_skip.rearrange("(h p) -> p h", p=P)).then_inc(mamba_weights, 16)
            sp.dma_start(w_out[:, :, :], out_proj_w.rearrange("(h p) n -> p h n", p=P)).then_inc(mamba_weights, 16)
            sp.dma_start(w_router[:, :], router_w).then_inc(mamba_weights, 16)
            sp.dma_start(w_rms2[:, :], rms2_w.rearrange("(p a) -> p a", a=1)).then_inc(mamba_weights, 16)
            sp.dma_start(w_v2[RANK:RANK + 1, :], b2.rearrange("(a n) -> a n", a=1)).then_inc(mamba_weights, 16)
            sp.dma_start(w_gate[:, :, :], Wg.rearrange("e p n -> p e n")).then_inc(expert_weights, 16)
            sp.dma_start(w_up[:, :, :], Wu.rearrange("e p n -> p e n")).then_inc(expert_weights, 16)
            sp.dma_start(w_down[:, :, :, :], Wd.rearrange("e (q p) n -> p e q n", p=P)).then_inc(expert_weights, 16)
            sp.dma_start(w_u1[:, :], U1).then_inc(ffn_weights, 16)
            sp.dma_start(w_v1[:, :], V1).then_inc(ffn_weights, 16)
            sp.dma_start(b_v1[:, :], b1.rearrange("(q p) -> p q", p=P)).then_inc(ffn_weights, 16)
            sp.dma_start(w_u2[:, :, :], U2.rearrange("(q p) r -> p q r", p=P)).then_inc(ffn_weights, 16)
            sp.dma_start(w_v2[0:RANK, :], V2).then_inc(ffn_weights, 16)

            def iteration(s):
                if s.has("A"):
                    q = s.parity("A")
                    wait(sp, acc_init, s.count("A", 1, -1))
                    sp.dma_start(x[q][:, :, :], chunk_rows(hidden, s, "A")).then_inc(x_loaded[q], 16)
                if s.has("E"):
                    q = s.parity("E")
                    wait(sp, y_out_ready, s.count("E", NJ, NJ))
                    sp.dma_start(chunk_rows(out, s, "E"), y_out[q][:, :, :]).then_inc(stored[q], 16)

            run_pipeline(sp, iteration)
            for q in range(2):
                sp.wait_ge(stored[q], 16 * NC // 2)

        @block.gpsimd
        def _(pool):
            pool.memset(ident[:, :], 0.0).then_inc(sel_made, 1)
            pool.memset(pick[:, :, :], 0.0).then_inc(sel_made, 1)
            pool.memset(before[:, :, :], 1.0).then_inc(sel_made, 1)
            for tile, value in ((power, -0.5), (per_d, 1.0 / D), (one, 1.0), (eps, EPS)):
                pool.memset(tile[:, :], value).then_inc(const_made, 1)
            for q in range(2):
                pool.memset(carry[q][:, :, :], 0.0).then_inc(const_made, 1)
                pool.memset(halo[q][:, :, :], 0.0).then_inc(const_made, 1)
            pool.wait_ge(sel_made, 3)
            pool.affine_select(out=ident[:, :], in_=ident[:, :], compare_op=ALU.not_equal, fill=1.0, base=0,
                               pattern=[[-1, P]], channel_multiplier=1).then_inc(const_made, 1)
            pool.affine_select(out=before[:, :, :], in_=before[:, :, :], compare_op=ALU.is_gt, fill=0.0, base=0,
                               pattern=[[1, NE], [-1, NE]], channel_multiplier=0).then_inc(const_made, 1)
            for term in range(3):
                pool.affine_select(out=pick[:, :, :], in_=pick[:, :, :], compare_op=ALU.not_equal, fill=1.0,
                                   base=-2 * NS * term, pattern=[[-1, 2 * NS], [0, P]],
                                   channel_multiplier=1).then_inc(sel_made, 1)
                pool.wait_ge(sel_made, 4 + term)

            def rstd_of(value, mean_sq, made, result, ready, s, stage, scale):
                pool.tensor_tensor(out=mean_sq[:, :], in0=value, in1=scale[:, :], op=ALU.mult).then_inc(made, 1)
                pool.wait_ge(made, s.count(stage, 2, 1))
                pool.tensor_tensor(out=mean_sq[:, :], in0=mean_sq[:, :], in1=eps[:, :], op=ALU.add).then_inc(made, 1)
                pool.wait_ge(made, s.count(stage, 2, 2))
                pool.tensor_tensor(out=result[:, :], in0=mean_sq[:, :], in1=power[:, :], op=ALU.pow).then_inc(ready, 1)

            def iteration(s):
                for k in range(UNITS):
                    if s.has("C") and k == 0:
                        add_state(s, "C", NS - 1)
                    if s.has("B") and k % 2 == 0 and k > 0 and k // 2 - 1 != 1:
                        add_state(s, "B", k // 2 - 1)
                    if s.has("C") and k == 3:
                        q = s.parity("C")
                        pool.wait_ge(ss2_ready, s.count("C", NJ, NJ))
                        rstd_of(ss2[:, :], ms2, ms2_ready, rstd2, rstd2_ready, s, "C", per_d)
                        pool.wait_ge(rstd2_ready, s.count("C", 1, 1))
                        pool.wait_ge(misc_taken, s.misc("C_out") + 1)
                        wait(pool, misc_taken, s.misc("C_T") - 1)
                        pool.tensor_tensor(out=hn[:, :, :], in0=res[:, :, :],
                                           in1=rstd2[:, :].unsqueeze(2).to_broadcast([P, NJ, D]),
                                           op=ALU.mult).then_inc(hn_ready, 1)
                        wait(pool, x1_ready, s.count("C", NJ, -NJ))
                        pool.tensor_tensor(out=acc[q][:, :, :], in0=res[:, :, :], in1=x[q][:, :, :],
                                           op=ALU.add).then_inc(acc_init, 1)
                    if s.has("E") and k == MISC["E_T"] - 2:
                        pool.wait_ge(mv_ready, s.count("E", NJ, NJ))
                        rstd_of(mv[:, :, 1], var, var_ready, rstd, rstd_ready, s, "E", one)
                    if s.has("A") and k == MISC["A_T"] - 4:
                        pool.wait_ge(ss1_ready, s.count("A", NJ, NJ))
                        rstd_of(ss1[:, :], ms1, ms1_ready, rstd1, rstd1_ready, s, "A", per_d)
                        pool.wait_ge(rstd1_ready, s.count("A", 1, 1))
                        q = s.parity("A")
                        pool.tensor_tensor(out=xn[:, :, :], in0=x[q][:, :, :],
                                           in1=rstd1[:, :].unsqueeze(2).to_broadcast([P, NJ, D]),
                                           op=ALU.mult).then_inc(xn_ready, 1)
                    if s.has("E") and k == MISC["E_out"] + 1:
                        pool.wait_ge(mv2_ready, s.count("E", NJ, NJ))
                        rstd_of(mv2[:, :, 1], var2, var2_ready, rstd_b, rstd_b_ready, s, "E", one)
                if s.has("A"):
                    q = s.parity("A")
                    pool.wait_ge(delta_ready, s.count("A", 1, 1))
                    pool.tensor_tensor(out=dx[q][:, :, :], in0=delta[q][:, :, :], in1=act_x[:, :, :],
                                       op=ALU.mult).then_inc(dx_ready, 1)

            def add_state(s, stage, n):
                q = s.parity(stage)
                y = (y_even[q], y_odd)[n % 2]
                if n == 0:
                    pool.wait_ge(y_init, s.count(stage, NH, NH))
                pool.wait_ge(hc_ready, s.count(stage, NS, n + 1))
                if n >= 2:
                    pool.wait_ge(added, s.count(stage, ADDS, additions(n - 2)))
                pool.tensor_tensor(out=y[:, :, :], in0=y[:, :, :], in1=hc[:, n % 2, :, :],
                                   op=ALU.add).then_inc(added, 1)

            pool.wait_ge(mamba_weights, 16 * N_MAMBA)
            run_pipeline(pool, iteration)

        @block.scalar
        def _(act):
            act.wait_ge(mamba_weights, 16 * N_MAMBA)
            act.activation(a_neg[:, :, :], a_neg[:, :, :], ACT.Exp).then_inc(a_exp, 1)
            act.wait_ge(prepared, 1)

            def take(name, s, out_ap, in_ap, **kw):
                act.wait_ge(misc_filled, s.misc(name) + 1)
                act.activation(out_ap, in_ap, kw.pop("func", ACT.Copy), **kw).then_inc(misc_taken, 1)

            def squares(s, stage, src, dst, ready):
                for j in range(NJ):
                    act.activation(tokens[:, j, :], src[:, j, :], ACT.Square, accum_out=dst[:, j:j + 1]).then_inc(ready, 1)

            def decays(s, n):
                q = s.parity("B")
                for half in range(NH):
                    if n == 0 and half == 0:
                        act.wait_ge(delta_ready, s.count("B", 1, 1))
                    wait(act, scanned, s.count("B", NS * NH, (n - 3) * NH + half + 1))
                    act.activation(decay[:, n % 3, half, :], delta[q][:, half, :], ACT.Exp,
                                   scale=a_neg[:, half, n:n + 1]).then_inc(decay_ready, 1)

            def gate_tanh(s, stage, m):
                act.wait_ge(gate_filled, s.count(stage, UNITS, m + 1))
                wait(act, silu_ready, s.count(stage, UNITS, m - 1))
                act.activation(th_gate[:, m % 2, :], g_bank[m % 2][:, :], ACT.Tanh, scale=0.5).then_inc(th_gate_ready, 1)

            def iteration(s):
                for k in range(UNITS):
                    if s.has("B"):
                        if k == 0:
                            decays(s, 0)
                        if k % 2 == 1 and (k + 1) // 2 < NS:
                            decays(s, (k + 1) // 2)
                    if k >= LAG and s.has("D"):
                        gate_tanh(s, "D", k - LAG)
                    if k < LAG and s.has("tail"):
                        gate_tanh(s, "tail", UNITS - LAG + k)
                    if s.has("C"):
                        q = s.parity("C")
                        if k == MISC["C_out"]:
                            act.wait_ge(misc_taken, s.misc("C_out") + 1)
                            wait(act, rstd2_ready, s.count("C", 1, 0))
                            squares(s, "C", res, ss2, ss2_ready)
                        if k == MISC["C_T"]:
                            wait(act, up_filled, s.count("C", UNITS, -UNITS))
                            take("C_T", s, hT[q][:, :], misc[:, :])
                        if k == MISC["C_router"]:
                            wait(act, weight_ready, s.count("C", 1, 0))
                            take("C_router", s, logits[:, :, :],
                                 misc[:, 0:NJ * NE].rearrange("p (j e) -> p j e", j=NJ))
                            act.wait_ge(shifted_ready, s.count("C", 1, 1))
                            act.activation(expo[:, :, :], shifted[:, :, :], ACT.Exp).then_inc(expo_ready, 1)
                    if s.has("E"):
                        if k == MISC["E_T"]:
                            take("E_T", s, x1T[:, :], misc[:, :])
                        if k == MISC["E_P"]:
                            take("E_P", s, p_ffn[:, :], misc[0:RANK, :])
                        for f in range(NQ):
                            if k == MISC[f"E_H{f}"]:
                                take(f"E_H{f}", s, h_ffn[:, f, :], misc[:, :], func=ACT.Identity,
                                     bias=b_v1[:, f:f + 1])
                        if k == MISC["E_H3"]:
                            act.wait_ge(misc_taken, s.misc("E_H3") + 1)
                            act.activation(h_ffn[:, :, :], h_ffn[:, :, :], ACT.Gelu_apprx_tanh).then_inc(h_act, 1)
                        if k == MISC["E_Q"]:
                            take("E_Q", s, q_ffn[0:RANK, :], misc[0:RANK, :])
                    if s.has("A"):
                        q = s.parity("A")
                        if k == MISC["A_T"] - 5:
                            act.wait_ge(x_loaded[q], 16 * (s.chunk("A") // 2 + 1) + 16 * s.j)
                            wait(act, ms1_ready, s.count("A", 2, 0))
                            squares(s, "A", x[q], ss1, ss1_ready)
                        if k == MISC["A_T"]:
                            take("A_T", s, xnT[:, :], misc[:, :])
                        for half in range(NH):
                            if k == MISC[f"A_xi{half}"]:
                                wait(act, tap_done, s.count("A", NH * 3, 0))
                                wait(act, halo_saved, s.count("A", 1, 0))
                                if half == 0:
                                    act.activation(xi[:, :, 0:NTAP - 1], halo[q][:, :, :], ACT.Copy).then_inc(halo_ready, 1)
                                take(f"A_xi{half}", s, xi[:, half, NTAP - 1:], misc[:, :])
                                act.wait_ge(misc_taken, s.misc(f"A_xi{half}") + 1)
                                act.wait_ge(halo_ready, s.count("A", 1, 1))
                                wait(act, act_x_ready, s.count("A", NH, half + 1 - NH))
                                act.activation(conv[:, half, :], xi[:, half, 0:T], ACT.Identity,
                                               scale=w_conv[:, half, 0:1],
                                               bias=b_conv[:, half:half + 1]).then_inc(tap0_ready, 1)
                                if half == NH - 1:
                                    act.activation(halo[q][:, :, :], xi[:, :, T:], ACT.Copy).then_inc(halo_saved, 1)
                            if k == MISC[f"A_z{half}"]:
                                act.wait_ge(misc_filled, s.misc(f"A_z{half}") + 1)
                                act.activation(th_z[:, :], misc[:, :], ACT.Tanh, scale=0.5).then_inc(th_z_ready, 1)
                            if k == MISC["A_z0"] + 1:
                                act.wait_ge(tap_done, s.count("A", NH * 3, NH * 2 + half + 1))
                                act.activation(th_conv[:, half, :], conv[:, half, :], ACT.Tanh,
                                               scale=0.5).then_inc(th_conv_ready, 1)
                                if half == NH - 1:
                                    y_start(s)
                            if k == MISC[f"A_dd{half}"]:
                                take(f"A_dd{half}", s, dt_raw[:, half, :], misc[:, :], func=ACT.Identity,
                                     bias=b_dt[:, half:half + 1])
                        if k == MISC["A_dt"]:
                            take("A_dt", s, dt_in[:, :], misc[0:R, :])
                        if k == MISC["A_BC"]:
                            wait(act, c_filled, s.count("A", NS, -NS))
                            act.wait_ge(misc_filled, s.misc("A_BC") + 1)
                            act.activation(bc[q][:, :], misc[0:3 * 2 * NS, :], ACT.Copy).then_inc(bc_ready, 1)
                        if k == MISC["A_dd1"]:
                            wait(act, delta_ready, s.count("A", 1, 0))
                            act.wait_ge(misc_taken, s.misc("A_dd1") + 1)
                            act.activation(dt_soft[:, :, :], dt_raw[:, :, :], ACT.Abs).then_inc(soft_step, 1)
                            act.wait_ge(soft_step, s.count("A", 2, 1))
                            act.activation(dt_soft[:, :, :], dt_soft[:, :, :], ACT.Exp, scale=-1.0).then_inc(soft_step, 1)
                            act.wait_ge(soft_step, s.count("A", 2, 2))
                            act.activation(dt_soft[:, :, :], dt_soft[:, :, :], ACT.Ln, bias=1.0).then_inc(soft_ready, 1)

            def y_start(s):
                q = s.parity("A")
                act.wait_ge(act_x_ready, s.count("A", NH, NH))
                wait(act, y_ready, s.count("A", 1, -1))
                for half in range(NH):
                    act.activation(y_even[q][:, half, :], act_x[:, half, :], ACT.Copy,
                                   scale=d_skip[:, half:half + 1]).then_inc(y_init, 1)

            run_pipeline(act, iteration)

        @block.tensor
        def _(pe):
            pe.wait_ge(const_made, 11)
            pe.wait_ge(sel_made, 6)
            pe.wait_ge(prepared, 1)

            def bank_free(name, s):
                wait(pe, misc_taken, s.misc(name))

            def transposes(name, s, src):
                bank_free(name, s)
                for j in range(NJ):
                    last = pe.transpose(misc_tok[:, j, :], src[:, j, :], ident[:, :])
                last.then_inc(misc_filled, 1)

            def broadcast(s, n):
                q = s.parity("B")
                if n == 0:
                    pe.wait_ge(bc_ready, s.count("B", 5, 5))
                wait(pe, scanned, s.count("B", NS * NH, n * NH))
                pe.matmul(b_bank[:, :], pick[:, n, :], bc[q][:, :], start=True, stop=True).then_inc(b_filled, 1)
                wait(pe, hc_ready, s.count("B", NS, n))
                pe.matmul(c_bank[:, :], pick[:, NS + n, :], bc[q][:, :], start=True, stop=True).then_inc(c_filled, 1)

            def expert_unit(s, stage, m):
                q = s.parity(stage)
                e, f = divmod(m, NQ)
                wait(pe, silu_ready, s.count(stage, UNITS, m - 1))
                pe.matmul(g_bank[m % 2][:, :], w_gate[:, e, f * P:(f + 1) * P], hT[q][:, :], start=True,
                          stop=True).then_inc(gate_filled, 1)
                if f == 0 and e > 0:
                    down(s, stage, e - 1)
                wait(pe, hid_ready, s.count(stage, UNITS, m))
                pe.matmul(up_bank[:, :], w_up[:, e, f * P:(f + 1) * P], hT[q][:, :], start=True,
                          stop=True).then_inc(up_filled, 1)

            def down(s, stage, e):
                pe.wait_ge(hid_ready, s.count(stage, UNITS, NQ * (e + 1)))
                wait(pe, moe_added, s.count(stage, NE * NJ, e * NJ))
                for j in range(NJ):
                    for f in range(NQ):
                        last = pe.matmul(down_tok[:, j, :], hid[:, e % 2, f, j * P:(j + 1) * P], w_down[:, e, f, :],
                                         start=(f == 0), stop=(f == NQ - 1))
                last.then_inc(down_filled, 1)

            def iteration(s):
                for k in range(UNITS):
                    if s.has("B") and k % 2 == 0:
                        broadcast(s, k // 2)
                    if s.has("C"):
                        q = s.parity("C")
                        if k == MISC["C_out"]:
                            bank_free("C_out", s)
                            pe.wait_ge(y_ready, s.count("C", 1, 1))
                            for j in range(NJ):
                                for half in range(NH):
                                    last = pe.matmul(misc_tok[:, j, :], y_gated[:, half, j * P:(j + 1) * P],
                                                     w_out[:, half, :], start=(half == 0), stop=(half == NH - 1))
                            last.then_inc(misc_filled, 1)
                        if k == MISC["C_T"]:
                            pe.wait_ge(hn_ready, s.count("C", 1, 1))
                            transposes("C_T", s, hn)
                        if k == MISC["C_router"]:
                            bank_free("C_router", s)
                            for j in range(NJ):
                                last = pe.matmul(misc[:, j * NE:(j + 1) * NE], hT[q][:, j * P:(j + 1) * P],
                                                 w_router[:, :], start=True, stop=True)
                            last.then_inc(misc_filled, 1)
                    if s.has("tail"):
                        if k < LAG:
                            expert_unit(s, "tail", UNITS - LAG + k)
                        if k == LAG:
                            down(s, "tail", NE - 1)
                    if k >= LAG and s.has("D"):
                        if k == LAG:
                            pe.wait_ge(gates_scaled, 2)
                        expert_unit(s, "D", k - LAG)
                    if s.has("E"):
                        if k == MISC["E_T"]:
                            pe.wait_ge(x1_ready, s.count("E", NJ, NJ))
                            pe.wait_ge(ffn_weights, 16 * 5)
                            transposes("E_T", s, x1)
                        if k == MISC["E_P"]:
                            bank_free("E_P", s)
                            pe.matmul(misc[0:RANK, :], w_u1[:, :], x1T[:, :], start=True, stop=True).then_inc(misc_filled, 1)
                        for f in range(NQ):
                            if k == MISC[f"E_H{f}"]:
                                bank_free(f"E_H{f}", s)
                                pe.matmul(misc[:, :], w_v1[:, f * P:(f + 1) * P], p_ffn[:, :], start=True,
                                          stop=True).then_inc(misc_filled, 1)
                        if k == MISC["E_Q"]:
                            bank_free("E_Q", s)
                            pe.wait_ge(h_act, s.count("E", 1, 1))
                            for f in range(NQ):
                                last = pe.matmul(misc[0:RANK, :], w_u2[:, f, :], h_ffn[:, f, :], start=(f == 0),
                                                 stop=(f == NQ - 1))
                            last.then_inc(misc_filled, 1)
                        if k == MISC["E_out"]:
                            bank_free("E_out", s)
                            for j in range(NJ):
                                last = pe.matmul(misc_tok[:, j, :], q_ffn[:, j * P:(j + 1) * P], w_v2[:, :],
                                                 start=True, stop=True)
                            last.then_inc(misc_filled, 1)
                    if s.has("A"):
                        q = s.parity("A")
                        if k == MISC["A_T"]:
                            pe.wait_ge(xn_ready, s.count("A", 1, 1))
                            transposes("A_T", s, xn)
                        for part, name in enumerate(("A_xi0", "A_xi1", "A_z0", "A_z1")):
                            if k == MISC[name]:
                                bank_free(name, s)
                                pe.matmul(misc[:, :], w_in[:, part * P:(part + 1) * P], xnT[:, :], start=True,
                                          stop=True).then_inc(misc_filled, 1)
                        if k == MISC["A_dt"]:
                            bank_free("A_dt", s)
                            pe.wait_ge(act_x_ready, s.count("A", NH, NH))
                            for half in range(NH):
                                last = pe.matmul(misc[0:R, :], w_x[:, half, 0:R], act_x[:, half, :],
                                                 start=(half == 0), stop=(half == NH - 1))
                            last.then_inc(misc_filled, 1)
                        if k == MISC["A_BC"]:
                            bank_free("A_BC", s)
                            for half in range(NH):
                                last = pe.matmul(misc[0:3 * 2 * NS, :], w_bc[:, half, :, :], act_x[:, half, :],
                                                 start=(half == 0), stop=(half == NH - 1))
                            last.then_inc(misc_filled, 1)
                        for half in range(NH):
                            if k == MISC[f"A_dd{half}"]:
                                bank_free(f"A_dd{half}", s)
                                pe.matmul(misc[:, :], w_dt[:, half * P:(half + 1) * P], dt_in[:, :], start=True,
                                          stop=True).then_inc(misc_filled, 1)

            run_pipeline(pe, iteration)

        @block.vector
        def _(dve):
            dve.memset(q_ffn[RANK:RANK + 1, :], 1.0).then_inc(const_made, 1)
            dve.wait_ge(mamba_weights, 16 * N_MAMBA)
            dve.wait_ge(a_exp, 1)
            dve.tensor_scalar(out=a_neg[:, :, :], in0=a_neg[:, :, :], scalar1=-1.0, scalar2=None, op0=ALU.mult)
            dve.tensor_scalar(out=w_in[:, :], in0=w_in[:, :], scalar1=w_rms1[:, 0:1], scalar2=None, op0=ALU.mult)
            dve.tensor_scalar(out=w_router[:, :], in0=w_router[:, :], scalar1=w_rms2[:, 0:1], scalar2=None, op0=ALU.mult)
            for term in range(3):
                dve.tensor_scalar(out=w_bc[:, :, term, :], in0=w_x[:, :, R:], scalar1=0.5, scalar2=None, op0=ALU.mult)
            dve.tensor_scalar(out=w_x[:, :, 0:R], in0=w_x[:, :, 0:R], scalar1=0.5, scalar2=None, op0=ALU.mult)
            dve.tensor_scalar(out=w_out[:, :, :], in0=w_out[:, :, :], scalar1=0.25, scalar2=None,
                              op0=ALU.mult).then_inc(prepared, 1)
            dve.wait_ge(const_made, 11)

            def multiply_b(s, n):
                q = s.parity("B")
                if n == 0:
                    dve.wait_ge(dx_ready, s.count("B", 1, 1))
                dve.wait_ge(b_filled, s.count("B", NS, n + 1))
                for half, dst in enumerate((u_bank, b_bank)):
                    dve.tensor_tensor(out=dst[:, :], in0=dx[q][:, half, :], in1=b_bank[:, :],
                                      op=ALU.mult).then_inc(u_ready, 1)

            def scan(s, n):
                q = s.parity("B")
                for half, src in enumerate((u_bank, b_bank)):
                    dve.wait_ge(decay_ready, s.count("B", NS * NH, n * NH + half + 1))
                    dve.wait_ge(u_ready, s.count("B", NS * NH, n * NH + half + 1))
                    if half == 0 and s.chunk("B") >= 2:
                        dve.wait_ge(carried, s.count("B", NS, n + 1 - 2 * NS))
                    dve.tensor_tensor_scan(out=h[:, n % 2, half, :], data0=decay[:, n % 3, half, :], data1=src[:, :],
                                           initial=carry[q][:, n, half:half + 1], op0=ALU.mult,
                                           op1=ALU.add).then_inc(scanned, 1)

            def multiply_c(s, stage, n):
                q = s.parity(stage)
                dve.wait_ge(scanned, s.count(stage, NS * NH, (n + 1) * NH))
                dve.wait_ge(c_filled, s.count(stage, NS, n + 1))
                if n >= 2:
                    dve.wait_ge(added, s.count(stage, ADDS, additions(n - 2)))
                else:
                    wait(dve, added, s.count(stage, ADDS, 0))
                if n == 1:
                    wait(dve, y_summed, s.count(stage, 1, 0))
                dst = y_odd[:, :, :] if n == 1 else hc[:, n % 2, :, :]
                dve.tensor_tensor(out=dst, in0=h[:, n % 2, :, :],
                                  in1=c_bank[:, :].unsqueeze(1).to_broadcast([P, NH, T]),
                                  op=ALU.mult).then_inc(hc_ready, 1)
                dve.tensor_copy(carry[q][:, n, :], h[:, n % 2, :, T - 1]).then_inc(carried, 1)

            def hidden_unit(s, stage, m):
                e, f = divmod(m, NQ)
                dve.wait_ge(th_gate_ready, s.count(stage, UNITS, m + 1))
                dve.scalar_tensor_tensor(out=th_gate[:, m % 2, :], in0=th_gate[:, m % 2, :], scalar=1.0,
                                         in1=g_bank[m % 2][:, :], op0=ALU.add, op1=ALU.mult).then_inc(silu_ready, 1)
                dve.wait_ge(up_filled, s.count(stage, UNITS, m + 1))
                dve.wait_ge(silu_ready, s.count(stage, UNITS, m + 1))
                if f == 0:
                    wait(dve, down_filled, s.count(stage, NE, e - 1))
                dve.tensor_tensor(out=hid[:, e % 2, f, :], in0=th_gate[:, m % 2, :], in1=up_bank[:, :],
                                  op=ALU.mult).then_inc(hid_ready, 1)

            def add_expert(s, stage, e):
                q = s.parity(stage)
                if e == 0:
                    dve.wait_ge(acc_init, s.count(stage, 1, 1))
                    dve.wait_ge(weight_ready, s.count(stage, 1, 1))
                else:
                    dve.wait_ge(moe_added, s.count(stage, NE * NJ, e * NJ))
                dve.wait_ge(down_filled, s.count(stage, NE, e + 1))
                for j in range(NJ):
                    dve.scalar_tensor_tensor(out=acc[q][:, j, :], in0=down_tok[:, j, :], scalar=weight[q][:, j, e:e + 1],
                                             in1=acc[q][:, j, :], op0=ALU.mult, op1=ALU.add).then_inc(moe_added, 1)

            def layer_norm_stats(src, st, st_ready):
                for j in range(NJ):
                    dve.bn_stats(out=st[:, j, :], in_=src[:, j, :]).then_inc(st_ready, 1)

            def layer_norm_aggregate(st, mean_var, mv_done):
                for j in range(NJ):
                    dve.bn_aggr(out=mean_var[:, j, :], in_=st[:, j, :]).then_inc(mv_done, 1)

            def normalize(s, src, mean_var, rs, dst, done):
                for j in range(NJ):
                    dve.tensor_scalar(out=dst[:, j, :], in0=src[:, j, :], scalar1=mean_var[:, j, 0:1],
                                      scalar2=rs[:, j:j + 1], op0=ALU.subtract, op1=ALU.mult).then_inc(done, 1)

            def route(s):
                q = s.parity("C")
                dve.wait_ge(misc_taken, s.misc("C_router") + 1)
                dve.tensor_reduce(out=top[:, :], in_=logits[:, :, :], axis=AX.X, op=ALU.max).then_inc(top_ready, 1)
                mine = logits[:, :, :].unsqueeze(3).to_broadcast([P, NJ, NE, NE])
                other = logits[:, :, :].unsqueeze(2).to_broadcast([P, NJ, NE, NE])
                flat = lambda a: a[:, :, :, :].rearrange("p j e f -> p j (e f)")
                tie_order = before[:, :, :].rearrange("p e f -> p (e f)").unsqueeze(1).to_broadcast([P, NJ, NE * NE])
                dve.wait_ge(top_ready, s.count("C", 1, 1))
                dve.tensor_tensor(out=shifted[:, :, :], in0=logits[:, :, :],
                                  in1=top[:, :].unsqueeze(2).to_broadcast([P, NJ, NE]),
                                  op=ALU.subtract).then_inc(shifted_ready, 1)
                dve.tensor_tensor(out=ties[:, :, :, :], in0=other, in1=mine, op=ALU.is_equal).then_inc(route_step, 1)
                dve.tensor_tensor(out=beats[:, :, :, :], in0=other, in1=mine, op=ALU.is_gt).then_inc(route_step, 1)
                dve.wait_ge(route_step, s.count("C", 7, 1))
                dve.tensor_tensor(out=flat(ties2), in0=flat(ties), in1=tie_order, op=ALU.mult).then_inc(route_step, 1)
                dve.wait_ge(route_step, s.count("C", 7, 3))
                dve.tensor_tensor(out=flat(beats2), in0=flat(beats), in1=flat(ties2), op=ALU.add).then_inc(route_step, 1)
                dve.wait_ge(route_step, s.count("C", 7, 4))
                dve.tensor_reduce(out=rank[:, :, :], in_=beats2[:, :, :, :], axis=AX.X, op=ALU.add).then_inc(route_step, 1)
                dve.wait_ge(expo_ready, s.count("C", 1, 1))
                dve.tensor_reduce(out=denom[:, :], in_=expo[:, :, :], axis=AX.X, op=ALU.add).then_inc(route_step, 1)
                dve.wait_ge(route_step, s.count("C", 7, 6))
                dve.scalar_tensor_tensor(out=chosen[:, :, :], in0=rank[:, :, :], scalar=1.5, in1=expo[:, :, :],
                                         op0=ALU.is_lt, op1=ALU.mult)
                dve.reciprocal(rdenom[:, :], denom[:, :]).then_inc(route_step, 1)
                dve.wait_ge(route_step, s.count("C", 7, 7))
                dve.tensor_tensor(out=weight[q][:, :, :], in0=chosen[:, :, :],
                                  in1=rdenom[:, :].unsqueeze(2).to_broadcast([P, NJ, NE]),
                                  op=ALU.mult).then_inc(weight_ready, 1)

            def stage_a(s, k):
                q = s.parity("A")
                if k == MISC["A_z0"]:
                    for tap in range(1, NTAP):
                        for half in range(NH):
                            if tap == 1:
                                dve.wait_ge(tap0_ready, s.count("A", NH, half + 1))
                            else:
                                dve.wait_ge(tap_done, s.count("A", NH * 3, NH * (tap - 2) + half + 1))
                            dve.scalar_tensor_tensor(out=conv[:, half, :], in0=xi[:, half, tap:tap + T],
                                                     scalar=w_conv[:, half, tap:tap + 1], in1=conv[:, half, :],
                                                     op0=ALU.mult, op1=ALU.add).then_inc(tap_done, 1)
                for half in range(NH):
                    if k == MISC[f"A_z{half}"]:
                        dve.wait_ge(th_z_ready, s.count("A", NH, half + 1))
                        dve.scalar_tensor_tensor(out=gate_z[q][:, half, :], in0=th_z[:, :], scalar=1.0, in1=misc[:, :],
                                                 op0=ALU.add, op1=ALU.mult).then_inc(misc_taken, 1)
                if k == MISC["A_z0"] + 1:
                    for half in range(NH):
                        dve.wait_ge(th_conv_ready, s.count("A", NH, half + 1))
                        dve.scalar_tensor_tensor(out=act_x[:, half, :], in0=th_conv[:, half, :], scalar=1.0,
                                                 in1=conv[:, half, :], op0=ALU.add, op1=ALU.mult).then_inc(act_x_ready, 1)
                if k == MISC["A_BC"]:
                    dve.wait_ge(bc_ready, s.count("A", 5, 1))
                    dve.tensor_tensor(out=bc_rest[:, :], in0=misc[0:3 * 2 * NS, :], in1=bc[q][:, :],
                                      op=ALU.subtract).then_inc(misc_taken, 1)
                    dve.wait_ge(misc_taken, s.misc("A_BC") + 1)
                    dve.tensor_copy(bc_mid[:, :], bc_rest[:, :]).then_inc(mid_ready, 1)
                    dve.wait_ge(mid_ready, s.count("A", 1, 1))
                    dve.tensor_tensor(out=bc_rest2[:, :], in0=bc_rest[:, :], in1=bc_mid[:, :],
                                      op=ALU.subtract).then_inc(rest2_ready, 1)
                    dve.tensor_copy(bc[q][2 * NS:4 * NS, :], bc_mid[2 * NS:4 * NS, :]).then_inc(bc_ready, 1)
                    dve.wait_ge(rest2_ready, s.count("A", 1, 1))
                    dve.tensor_copy(bc[q][4 * NS:6 * NS, :], bc_rest2[4 * NS:6 * NS, :]).then_inc(bc_ready, 3)
                if k == UNITS - 1:
                    dve.wait_ge(soft_ready, s.count("A", 1, 1))
                    wait(dve, decay_ready, s.count("A", NS * NH, -NS * NH))
                    dve.scalar_tensor_tensor(out=delta[q][:, :, :], in0=dt_raw[:, :, :], scalar=0.0, in1=dt_soft[:, :, :],
                                             op0=ALU.max, op1=ALU.add).then_inc(delta_ready, 1)

            def iteration(s):
                for k in range(UNITS):
                    if s.has("E") and k == MISC["E_T"] - 2:
                        dve.wait_ge(stats_ready, s.count("E", NJ, NJ))
                    if s.has("E") and k == MISC["E_out"] + 1:
                        dve.wait_ge(stats2_ready, s.count("E", NJ, NJ))
                    if s.has("B") and k % 2 == 0:
                        multiply_b(s, k // 2)
                        scan(s, k // 2)
                    if s.has("B") and k % 2 == 1 and k < UNITS - 1:
                        multiply_c(s, "B", k // 2)
                    if s.has("C") and k == 0:
                        multiply_c(s, "C", NS - 1)
                    if s.has("C") and k == 1:
                        q = s.parity("C")
                        dve.wait_ge(added, s.count("C", ADDS, ADDS))
                        dve.tensor_tensor(out=y_even[q][:, :, :], in0=y_even[q][:, :, :], in1=y_odd[:, :, :],
                                          op=ALU.add).then_inc(y_summed, 1)
                        dve.wait_ge(y_summed, s.count("C", 1, 1))
                        dve.tensor_tensor(out=y_gated[:, :, :], in0=y_even[q][:, :, :], in1=gate_z[q][:, :, :],
                                          op=ALU.mult).then_inc(y_ready, 1)
                    if s.has("C") and k == MISC["C_out"]:
                        q = s.parity("C")
                        dve.wait_ge(misc_filled, s.misc("C_out") + 1)
                        dve.tensor_tensor(out=res[:, :, :], in0=misc_tok, in1=x[q][:, :, :], op=ALU.add).then_inc(misc_taken, 1)
                    if s.has("C") and k == MISC["C_router"]:
                        route(s)
                    if k < LAG and s.has("tail"):
                        hidden_unit(s, "tail", UNITS - LAG + k)
                        if k % NQ == 0:
                            add_expert(s, "tail", (UNITS - LAG + k) // NQ - 1)
                    if k == LAG and s.has("tail"):
                        add_expert(s, "tail", NE - 1)
                    if k >= LAG and s.has("D"):
                        hidden_unit(s, "D", k - LAG)
                        if k % NQ == 0 and k > LAG:
                            add_expert(s, "D", (k - LAG) // NQ - 1)
                    if s.has("E"):
                        q = s.parity("E")
                        if k == MISC["E_T"] - 3:
                            dve.wait_ge(moe_added, s.count("E", NE * NJ, NE * NJ))
                            layer_norm_stats(acc[q], stats, stats_ready)
                        if k == MISC["E_T"] - 2:
                            layer_norm_aggregate(stats, mv, mv_ready)
                        if k == MISC["E_out"] + 1:
                            layer_norm_aggregate(stats2, mv2, mv2_ready)
                        if k == MISC["E_T"] - 1:
                            dve.wait_ge(rstd_ready, s.count("E", 1, 1))
                            normalize(s, acc[q], mv, rstd, x1, x1_ready)
                        if k == MISC["E_out"]:
                            dve.wait_ge(misc_filled, s.misc("E_out") + 1)
                            dve.tensor_tensor(out=r2[:, :, :], in0=misc_tok, in1=x1[:, :, :], op=ALU.add).then_inc(misc_taken, 1)
                            dve.wait_ge(misc_taken, s.misc("E_out") + 1)
                            layer_norm_stats(r2, stats2, stats2_ready)
                        if k == MISC["E_out"] + 2:
                            dve.wait_ge(rstd_b_ready, s.count("E", 1, 1))
                            if s.chunk("E") >= 2:
                                dve.wait_ge(stored[q], 16 * (s.chunk("E") // 2) + 16 * s.j)
                            normalize(s, r2, mv2, rstd_b, y_out[q], y_out_ready)
                    if s.has("A"):
                        stage_a(s, k)
                    if s.i0 == 0 and k in (4, 12):
                        w, half = ((w_gate, 1.0), (w_up, 0.5))[k == 12]
                        dve.wait_ge(expert_weights, 16 * N_EXPERT)
                        dve.tensor_scalar(out=w[:, :, :], in0=w[:, :, :], scalar1=w_rms2[:, 0:1], scalar2=half,
                                          op0=ALU.mult, op1=ALU.mult).then_inc(gates_scaled, 1)

            run_pipeline(dve, iteration)


_INS = ["L0_attn_hidden_states", "L0_attn_rms1_w", "L0_attn_rms2_w", "L0_attn_in_proj_w", "L0_attn_conv_w",
        "L0_attn_conv_b", "L0_attn_x_proj_w", "L0_attn_dt_proj_w", "L0_attn_dt_proj_b", "L0_attn_A_log",
        "L0_attn_D_skip", "L0_attn_out_proj_w", "L0_attn_router_w", "L0_attn_Wg", "L0_attn_Wu", "L0_attn_Wd",
        "L0_ffn_U1", "L0_ffn_V1", "L0_ffn_b1", "L0_ffn_U2", "L0_ffn_V2", "L0_ffn_b2"]


def kernel(**inputs):
    import concourse.bacc as bacc
    from concourse.bass_utils import run_bass_kernel_spmd

    nc = bacc.Bacc("TRN2", target_bir_lowering=False, num_devices=1)
    arrays, args = {}, []
    for name in _INS:
        a = np.ascontiguousarray(inputs[name])
        arrays[f"in_{name}"] = a
        args.append(nc.dram_tensor(f"in_{name}", a.shape, mybir.dt.from_np(a.dtype), kind="ExternalInput").ap())
    args.append(nc.dram_tensor("out_0", (B, L, D), F32, kind="ExternalOutput").ap())
    build(nc, *args)
    r = run_bass_kernel_spmd(nc, [arrays], core_ids=[0])
    return r.results[0]["out_0"]
```

```python
import numpy as np
import concourse.bass as bass
from concourse import mybir
from contextlib import ExitStack

F32 = mybir.dt.float32
BF16 = mybir.dt.bfloat16
I32 = mybir.dt.int32
U32 = mybir.dt.uint32
ALU = mybir.AluOpType
ACT = mybir.ActivationFunctionType
AX = mybir.AxisListType

P = 128
B, L, D = 2, 2048, 128
DI = 256
NH = DI // P
NS = 16
NTAP = 4
R = 64
NE = 8
FFN = 512
NQ = FFN // P
RANK = 32
T = 512
NJ = T // P
NC = B * L // T
ADDS = NS - 1
UNITS = 2 * NS
TOPK = 2
ND = 4
NT = NJ * TOPK + NE - 1
NB = 5
LAG = 18
EPS = 1e-5

MISC = {
    "F_out": 0, "C_out": 2, "C_T": 4, "C_router": 6, "C_rank": 8,
    "A_T": 10, "A_xi0": 11, "A_xi1": 12, "A_z0": 13, "A_z1": 14, "A_dt": 16, "A_BC": 17, "A_dd0": 18, "A_dd1": 19,
    "E_T": 24, "E_P": 25, "E_H0": 26, "E_H1": 27, "E_H2": 28, "E_H3": 29, "E_Q": 31,
}
ORDER = sorted(MISC, key=MISC.get)


class Step:

    def __init__(self, i0, j=0):
        self.i0, self.j = i0, j

    def chunk(self, stage):
        return self.i0 + {"A": 1, "B": 0, "C": -1, "D": -1, "tail": -2, "E": -2, "F": -3}[stage]

    def has(self, stage):
        return 0 <= self.chunk(stage) < NC

    def parity(self, stage):
        return self.chunk(stage) % 2

    def time(self, stage):
        return self.chunk(stage) // 2 + self.j

    def count(self, stage, per_chunk, offset):
        return per_chunk * self.chunk(stage) + offset + per_chunk * 2 * self.j

    def misc(self, name):
        before = 0
        for i in range(-1, self.i0):
            before += sum(Step(i).has(n[0]) for n in ORDER)
        here = [n for n in ORDER if self.has(n[0])]
        return before + here.index(name) + len(ORDER) * 2 * self.j


def wait(eng, sem, value):
    if type(value) is int and value <= 0:
        return
    eng.wait_ge(sem, value)


def small_use(what, i):
    if what == "x":
        return max(0, 2 * i - 1)
    return min(2 * i + 2, 2 * NT - 2) + (i == NT - 1)


def run_pipeline(eng, iteration):
    for i in (-1, 0, 1, 2):
        iteration(Step(i))
    with eng.Fori(0, 2, 1) as j:
        iteration(Step(3, j))
        iteration(Step(4, j))
    for i in range(7, NC + 3):
        iteration(Step(i))


def build(nc, hidden, rms1_w, rms2_w, in_proj_w, conv_w, conv_b, x_proj_w, dt_proj_w, dt_proj_b, A_log, D_skip,
          out_proj_w, router_w, Wg, Wu, Wd, U1, V1, b1, U2, V2, b2, out):
    ctx = ExitStack()
    with ctx:
        ctx.enter_context(nc.allow_non_contiguous_dma(reason="small per-channel columns"))

        def sb(name, shape, dt=F32):
            return ctx.enter_context(nc.sbuf_tensor(name, shape, dt))

        def sem(name):
            return ctx.enter_context(nc.semaphore(name))

        w_in = sb("w_in", [P, 2 * DI])
        w_conv = sb("w_conv", [P, NH, NTAP])
        b_conv = sb("b_conv", [P, NH])
        w_x = sb("w_x", [P, NH, R + 2 * NS])
        w_bc = sb("w_bc", [P, NH, 3, 2 * NS])
        w_dt = sb("w_dt", [R, DI])
        b_dt = sb("b_dt", [P, NH])
        a_neg = sb("a_neg", [P, NH, NS])
        d_skip = sb("d_skip", [P, NH])
        w_out = sb("w_out", [P, NH, D])
        w_router = sb("w_router", [P, NE])
        w_rms1 = sb("w_rms1", [P, 1])
        w_rms2 = sb("w_rms2", [P, 1])
        w_gate = sb("w_gate", [P, NE, FFN])
        w_up = sb("w_up", [P, NE, FFN])
        w_down = sb("w_down", [P, NE, NQ, D])
        w_u1 = sb("w_u1", [P, RANK])
        w_v1 = sb("w_v1", [RANK, FFN])
        b_v1 = sb("b_v1", [P, NQ])
        w_u2 = sb("w_u2", [P, NQ, RANK])
        w_v2 = sb("w_v2", [RANK + 1, D])
        ident = sb("ident", [P, P])
        pick = sb("pick", [3 * 2 * NS, 2 * NS], BF16)
        power = sb("power", [P, NJ])
        per_d, one, eps = sb("per_d", [P, NJ]), sb("one", [P, NJ]), sb("eps", [P, NJ])
        earlier = sb("earlier", [P, P], BF16)
        all_ones = sb("all_ones", [P, P], BF16)
        whole = sb("whole", [P, NJ])
        tile_no = sb("tile_no", [1, NT])
        before = sb("before", [P, NE, NE])
        x = [sb(f"x_in{q}", [P, NJ, D]) for q in range(2)]
        ss1 = sb("ss1", [P, NJ])
        ms1 = sb("ms1", [P, NJ])
        rstd1 = sb("rstd1", [P, NJ])
        work = sb("work", [P, 2 * NH, T])
        tokens = sb("tokens", [P, NJ, D])
        columns = sb("columns", [P, T])
        sums = sb("sums", [P, NJ, D])
        narrow = sb("narrow", [R, T])
        xn, xnT = tokens, columns
        xi = sb("xi", [P, NH, NTAP - 1 + T])
        halo = [sb(f"halo{q}", [P, NH, NTAP - 1]) for q in range(2)]
        conv = work[:, 0:NH, :]
        th_conv = work[:, NH:, :]
        th_z = sb("th_z", [P, T])
        act_x = sb("act_x", [P, NH, T])
        gate_z = [sb(f"gate_z{q}", [P, NH, T]) for q in range(2)]
        dt_in = narrow
        bc = [sb(f"bc{q}", [3 * 2 * NS, T], BF16) for q in range(2)]
        bc_rest = th_z[0:3 * 2 * NS, :]
        bc_mid = sb("bc_mid", [3 * 2 * NS, T], BF16)
        bc_rest2 = tokens[0:3 * 2 * NS, :, :].rearrange("p j d -> p (j d)")
        dt_raw = work[:, 0:NH, :]
        dt_soft = work[:, NH:, :]
        delta = [sb(f"delta{q}", [P, NH, T]) for q in range(2)]
        dx = [sb(f"dx{q}", [P, NH, T]) for q in range(2)]
        decay = sb("decay", [P, ND, NH, T])
        h = sb("h", [P, 2, NH, T])
        carry = [sb(f"carry{q}", [P, NS, NH]) for q in range(2)]
        hc = sb("hc", [P, 2, NH, T])
        y_even = [sb(f"y_even{q}", [P, NH, T]) for q in range(2)]
        y_odd = sb("y_odd", [P, NH, T])
        y_gated = work[:, 0:NH, :]
        res = sums
        ss2 = sb("ss2", [P, NJ])
        ms2 = sb("ms2", [P, NJ])
        rstd2 = sb("rstd2", [P, NJ])
        hn = sb("hn", [P, NJ, D])
        hT = sb("hT", [P, T])
        logits = sb("logits", [P, NJ, NE])
        top = sb("top", [P, NJ])
        shifted = sb("shifted", [P, NJ, NE])
        expo = sb("expo", [P, NJ, NE])
        beats = sb("beats", [P, NJ, NE, NE])
        ties = sb("ties", [P, NJ, NE, NE])
        ties2 = sb("ties2", [P, NJ, NE, NE])
        beats2 = sb("beats2", [P, NJ, NE, NE])
        rank = sb("rank", [P, NJ, NE])
        denom = sb("denom", [P, NJ])
        rdenom = sb("rdenom", [P, NJ])
        mask = sb("mask", [P, NJ, NE], BF16)
        choice = sb("choice", [P, TOPK, NJ, NE])
        chosen = sb("chosen", [P, TOPK, NJ, NE])
        chosen_w = sb("chosen_w", [P, TOPK, NJ])
        weight = [sb(f"weight{q}", [P, TOPK, NJ]) for q in range(2)]
        place = sb("place", [P, NJ + 1, NE])
        over = sb("over", [P, NE, NJ])
        tiles = sb("tiles", [P, NE])
        tiles_b = sb("tiles_b", [P, NE, NE])
        first_tile = sb("first_tile", [P, NE])
        end_tile = sb("end_tile", [P, NE])
        passed = sb("passed", [1, NT, NE])
        passed_n = sb("passed_n", [1, NT])
        place2 = sb("place2", [P, NJ, NE])
        picked = sb("picked", [P, TOPK, NJ, NE])
        slot_f = sb("slot_f", [P, TOPK, NJ])
        slot = [sb(f"slot{q}", [P, TOPK, NJ], U32) for q in range(2)]
        tile_expert = [sb(f"tile_expert{q}", [1, NT], I32) for q in range(2)]
        xs = sb("xs", [P, NB, D])
        xsT = sb("xsT", [P, 2, P])
        th_gate = sb("th_gate", [P, 2, FFN])
        hid = sb("hid", [P, 2, FFN])
        hidT = sb("hidT", [P, 2, NQ, P])
        ys = sb("ys", [P, NB, D])
        y_sel = sb("y_sel", [P, TOPK, NJ, D])
        acc = [sb(f"acc{q}", [P, NJ, D]) for q in range(2)]
        xs_dram = [nc.dram_tensor(f"xs_dram{q}", (NT * P, D), F32, kind="Internal").ap() for q in range(2)]
        ys_dram = [nc.dram_tensor(f"ys_dram{q}", (NT * P, D), F32, kind="Internal").ap() for q in range(2)]
        stats = sb("stats", [P, NJ, 6])
        mv = sb("mv", [P, NJ, 2])
        var = sb("var", [P, NJ])
        rstd = sb("rstd", [P, NJ])
        x1 = sb("x_mid", [P, NJ, D])
        x1T = columns
        p_ffn = narrow[0:RANK, :]
        h_ffn = work
        q_ffn = sb("q_ffn", [RANK + 1, T])
        r2 = sb("r2", [P, NJ, D])
        stats2 = sb("stats2", [P, NJ, 6])
        mv2 = sb("mv2", [P, NJ, 2])
        var2 = sb("var2", [P, NJ])
        rstd_b = sb("rstd_b", [P, NJ])
        y_out = [sb(f"y_out{q}", [P, NJ, D]) for q in range(2)]

        bank = [ctx.enter_context(nc.psum_tensor(f"bank{i}", [P, T], F32)) for i in range(8)]
        u_bank, b_bank, c_bank, g_bank, up_bank, turn_bank, small, misc = bank
        misc_tok = misc[:, :].rearrange("p (j d) -> p j d", j=NJ)

        mamba_weights, expert_weights, ffn_weights = sem("mamba_weights"), sem("expert_weights"), sem("ffn_weights")
        x_loaded = [sem(f"x_loaded{q}") for q in range(2)]
        stored = [sem(f"stored{q}") for q in range(2)]
        const_made, sel_made, a_exp, prepared, gates_scaled = (
            sem("const_made"), sem("sel_made"), sem("a_exp"), sem("prepared"), sem("gates_scaled"))
        misc_filled, misc_taken = sem("misc_filled"), sem("misc_taken")
        ss1_ready, ms1_ready, rstd1_ready, xn_ready = sem("ss1_ready"), sem("ms1_ready"), sem("rstd1_ready"), sem("xn_ready")
        halo_ready, halo_saved, tap0_ready, tap_done, th_conv_ready, act_x_ready = (
            sem("halo_ready"), sem("halo_saved"), sem("tap0_ready"), sem("tap_done"), sem("th_conv_ready"), sem("act_x_ready"))
        th_z_ready = sem("th_z_ready")
        mid_ready, rest2_ready, bc_ready = sem("mid_ready"), sem("rest2_ready"), sem("bc_ready")
        soft_step, soft_ready, delta_ready, dx_ready, y_init = (
            sem("soft_step"), sem("soft_ready"), sem("delta_ready"), sem("dx_ready"), sem("y_init"))
        b_filled, c_filled, decay_ready, u_ready, scanned, hc_ready, carried, added = (
            sem("b_filled"), sem("c_filled"), sem("decay_ready"), sem("u_ready"), sem("scanned"), sem("hc_ready"),
            sem("carried"), sem("added"))
        y_summed, y_ready, ss2_ready, ms2_ready, rstd2_ready, hn_ready, acc_init = (
            sem("y_summed"), sem("y_ready"), sem("ss2_ready"), sem("ms2_ready"), sem("rstd2_ready"), sem("hn_ready"),
            sem("acc_init"))
        top_ready, shifted_ready, expo_ready, route_step, mask_ready, weight_ready = (
            sem("top_ready"), sem("shifted_ready"), sem("expo_ready"), sem("route_step"), sem("mask_ready"),
            sem("weight_ready"))
        tiles_step, slot_f_ready, passed_ready, weight_step, expert_ready, slot_ready, cleared, slots_zero = (
            sem("tiles_step"), sem("slot_f_ready"), sem("passed_ready"), sem("weight_step"), sem("expert_ready"), sem("slot_ready"), sem("cleared"), sem("slots_zero"))
        scattered, gathered, combined = sem("scattered"), sem("gathered"), sem("combined")
        tile_loaded = [sem(f"tile_loaded{b}") for b in range(NB)]
        tile_stored = [sem(f"tile_stored{b}") for b in range(NB)]
        small_filled, small_taken, gate_filled, up_filled, turned, turn_taken = (
            sem("small_filled"), sem("small_taken"), sem("gate_filled"), sem("up_filled"), sem("turned"),
            sem("turn_taken"))
        th_gate_ready, silu_ready, hid_ready = sem("th_gate_ready"), sem("silu_ready"), sem("hid_ready")
        stats_ready, mv_ready, var_ready, rstd_ready, x1_ready, h_act = (
            sem("stats_ready"), sem("mv_ready"), sem("var_ready"), sem("rstd_ready"), sem("x1_ready"), sem("h_act"))
        stats2_ready, mv2_ready, var2_ready, rstd_b_ready, y_out_ready = (
            sem("stats2_ready"), sem("mv2_ready"), sem("var2_ready"), sem("rstd_b_ready"), sem("y_out_ready"))

        block = ctx.enter_context(nc.Block())

        def chunk_rows(dram, s, stage):
            tiles = dram[s.parity(stage), :, :].rearrange("(t j p) d -> t p j d", j=NJ, p=P)
            return tiles[s.time(stage), :, :, :]

        def tile_at(g, offset):
            i, odd = divmod(g - LAG - offset, 2)
            return i if not odd and 0 <= i < NT else None

        def additions(n):
            return 1 if n < 2 else n

        N_MAMBA, N_EXPERT, N_FFN = 13, 3, 6

        @block.sync
        def _(sp):
            sp.dma_start(w_in[:, :], in_proj_w).then_inc(mamba_weights, 16)
            sp.dma_start(w_rms1[:, :], rms1_w.rearrange("(p a) -> p a", a=1)).then_inc(mamba_weights, 16)
            sp.dma_start(w_conv[:, :, :], conv_w.rearrange("(h p) a k -> p h (a k)", p=P)).then_inc(mamba_weights, 16)
            sp.dma_start(b_conv[:, :], conv_b.rearrange("(h p) -> p h", p=P)).then_inc(mamba_weights, 16)
            sp.dma_start(w_x[:, :, :], x_proj_w.rearrange("(h p) n -> p h n", p=P)).then_inc(mamba_weights, 16)
            sp.dma_start(w_dt[:, :], dt_proj_w).then_inc(mamba_weights, 16)
            sp.dma_start(b_dt[:, :], dt_proj_b.rearrange("(h p) -> p h", p=P)).then_inc(mamba_weights, 16)
            sp.dma_start(a_neg[:, :, :], A_log.rearrange("(h p) n -> p h n", p=P)).then_inc(mamba_weights, 16)
            sp.dma_start(d_skip[:, :], D_skip.rearrange("(h p) -> p h", p=P)).then_inc(mamba_weights, 16)
            sp.dma_start(w_out[:, :, :], out_proj_w.rearrange("(h p) n -> p h n", p=P)).then_inc(mamba_weights, 16)
            sp.dma_start(w_router[:, :], router_w).then_inc(mamba_weights, 16)
            sp.dma_start(w_rms2[:, :], rms2_w.rearrange("(p a) -> p a", a=1)).then_inc(mamba_weights, 16)
            sp.dma_start(w_v2[RANK:RANK + 1, :], b2.rearrange("(a n) -> a n", a=1)).then_inc(mamba_weights, 16)
            sp.dma_start(w_gate[:, :, :], Wg.rearrange("e p n -> p e n")).then_inc(expert_weights, 16)
            sp.dma_start(w_up[:, :, :], Wu.rearrange("e p n -> p e n")).then_inc(expert_weights, 16)
            sp.dma_start(w_down[:, :, :, :], Wd.rearrange("e (q p) n -> p e q n", p=P)).then_inc(expert_weights, 16)
            sp.dma_start(w_u1[:, :], U1).then_inc(ffn_weights, 16)
            sp.dma_start(w_v1[:, :], V1).then_inc(ffn_weights, 16)
            sp.dma_start(b_v1[:, :], b1.rearrange("(q p) -> p q", p=P)).then_inc(ffn_weights, 16)
            sp.dma_start(w_u2[:, :, :], U2.rearrange("(q p) r -> p q r", p=P)).then_inc(ffn_weights, 16)
            sp.dma_start(w_v2[0:RANK, :], V2).then_inc(ffn_weights, 16)

            sp.wait_ge(slots_zero, 1)
            for q in range(2):
                sp.dma_start(xs_dram[q].rearrange("(i p) d -> p i d", p=P),
                             h[:, :, :, :].rearrange("p a b t -> p (a b t)")[:, 0:NT * D]
                             .rearrange("p (i d) -> p i d", i=NT)).then_inc(cleared, 16)

            def iteration(s):
                for k in range(UNITS):
                    if s.has("A") and k == 3:
                        q = s.parity("A")
                        wait(sp, acc_init, s.count("A", 1, -1))
                        sp.dma_start(x[q][:, :, :], chunk_rows(hidden, s, "A")).then_inc(x_loaded[q], 16)
                    if s.has("F") and k == 4:
                        q = s.parity("F")
                        sp.wait_ge(y_out_ready, s.count("F", NJ, NJ))
                        sp.dma_start(chunk_rows(out, s, "F"), y_out[q][:, :, :]).then_inc(stored[q], 16)
                    for stage, g in (("tail", k + UNITS), ("D", k)):
                        if not s.has(stage):
                            continue
                        q = s.parity(stage)
                        i = tile_at(g, -5)
                        if i is not None:
                            if i == 0:
                                sp.wait_ge(scattered, s.count(stage, 16 * TOPK * NJ, 16 * TOPK * NJ))
                            if i >= NB:
                                sp.wait_ge(small_filled, s.count(stage, 2 * NT, small_use("x", i - NB) + 1))
                            sp.dma_start(xs[:, i % NB, :], xs_dram[q][i * P:(i + 1) * P, :]).then_inc(tile_loaded[i % NB], 16)
                        i = tile_at(g, 2)
                        if i is not None:
                            sp.wait_ge(small_taken, s.count(stage, 2 * NT, small_use("y", i) + 1))
                            sp.dma_start(ys_dram[q][i * P:(i + 1) * P, :], ys[:, i % NB, :]).then_inc(tile_stored[i % NB], 16)

            run_pipeline(sp, iteration)
            for q in range(2):
                sp.wait_ge(stored[q], 16 * NC // 2)

        @block.gpsimd
        def _(pool):
            pool.memset(ident[:, :], 0.0).then_inc(sel_made, 1)
            pool.memset(pick[:, :], 0.0).then_inc(sel_made, 1)
            pool.memset(before[:, :, :], 1.0).then_inc(sel_made, 1)
            for tile, value in ((power, -0.5), (per_d, 1.0 / D), (one, 1.0), (eps, EPS)):
                pool.memset(tile[:, :], value).then_inc(const_made, 1)
            pool.memset(all_ones[:, :], 1.0).then_inc(const_made, 1)
            pool.memset(earlier[:, :], 1.0).then_inc(sel_made, 1)
            pool.iota(whole[:, :], pattern=[[P, NJ]], base=0, channel_multiplier=0,
                      allow_small_or_imprecise_dtypes=True).then_inc(const_made, 1)
            pool.iota(tile_no[:, :], pattern=[[1, NT]], base=0, channel_multiplier=0,
                      allow_small_or_imprecise_dtypes=True).then_inc(const_made, 1)
            for q in range(2):
                pool.memset(carry[q][:, :, :], 0.0).then_inc(const_made, 1)
                pool.memset(halo[q][:, :, :], 0.0).then_inc(const_made, 1)
            pool.wait_ge(sel_made, 4)
            pool.affine_select(out=ident[:, :], in_=ident[:, :], compare_op=ALU.not_equal, fill=1.0, base=0,
                               pattern=[[-1, P]], channel_multiplier=1).then_inc(const_made, 1)
            pool.affine_select(out=before[:, :, :], in_=before[:, :, :], compare_op=ALU.is_gt, fill=0.0, base=0,
                               pattern=[[1, NE], [-1, NE]], channel_multiplier=0).then_inc(const_made, 1)
            pool.affine_select(out=earlier[:, :], in_=earlier[:, :], compare_op=ALU.is_gt, fill=0.0, base=0,
                               pattern=[[1, P]], channel_multiplier=-1).then_inc(const_made, 1)
            for term in range(3):
                pool.affine_select(out=pick[:, :], in_=pick[:, :], compare_op=ALU.not_equal, fill=1.0,
                                   base=-2 * NS * term, pattern=[[-1, 2 * NS]],
                                   channel_multiplier=1).then_inc(sel_made, 1)
                pool.wait_ge(sel_made, 5 + term)

            def rstd_of(value, mean_sq, made, result, ready, s, stage, scale):
                pool.tensor_tensor(out=mean_sq[:, :], in0=value, in1=scale[:, :], op=ALU.mult).then_inc(made, 1)
                pool.wait_ge(made, s.count(stage, 2, 1))
                pool.tensor_tensor(out=mean_sq[:, :], in0=mean_sq[:, :], in1=eps[:, :], op=ALU.add).then_inc(made, 1)
                pool.wait_ge(made, s.count(stage, 2, 2))
                pool.tensor_tensor(out=result[:, :], in0=mean_sq[:, :], in1=power[:, :], op=ALU.pow).then_inc(ready, 1)

            def iteration(s):
                for k in range(UNITS):
                    if s.has("C") and k == 0:
                        add_state(s, "C", NS - 1)
                    if s.has("C") and k == MISC["C_rank"] + 2:
                        pool.wait_ge(slot_ready, s.count("C", 1, 1))
                        if s.chunk("C") == 0:
                            pool.wait_ge(cleared, 16 * 2)
                        wait(pool, small_filled, s.count("C", 2 * NT, -2 * NT))
                    if s.has("E") and k == LAG:
                        for b in range(NB):
                            pool.wait_ge(tile_stored[b], s.count("E", 16 * NT // NB, 16 * NT // NB))
                        wait(pool, combined, s.count("E", TOPK * NJ, 0))
                    if s.has("B") and k % 2 == 0 and k > 0 and k // 2 - 1 != 1:
                        add_state(s, "B", k // 2 - 1)
                    if s.has("C") and k == 3:
                        q = s.parity("C")
                        pool.wait_ge(ss2_ready, s.count("C", NJ, NJ))
                        rstd_of(ss2[:, :], ms2, ms2_ready, rstd2, rstd2_ready, s, "C", per_d)
                        pool.wait_ge(rstd2_ready, s.count("C", 1, 1))
                        pool.wait_ge(misc_taken, s.misc("C_out") + 1)
                        wait(pool, scattered, s.count("C", 16 * TOPK * NJ, 0))
                        pool.tensor_tensor(out=hn[:, :, :], in0=res[:, :, :],
                                           in1=rstd2[:, :].unsqueeze(2).to_broadcast([P, NJ, D]),
                                           op=ALU.mult).then_inc(hn_ready, 1)
                        wait(pool, x1_ready, s.count("C", NJ, -NJ))
                        pool.tensor_tensor(out=acc[q][:, :, :], in0=res[:, :, :], in1=x[q][:, :, :],
                                           op=ALU.add).then_inc(acc_init, 1)
                    if s.has("C") and k == MISC["C_rank"] + 2:
                        q = s.parity("C")
                        for c in range(TOPK):
                            for j in range(NJ):
                                pool.indirect_dma_start(
                                    xs_dram[q], bass.IndirectOffsetOnAxis(ap=slot[q][:, c, j:j + 1], axis=0),
                                    hn[:, j, :], None).then_inc(scattered, 16)
                    if s.has("E") and k == LAG:
                        q = s.parity("E")
                        for c in range(TOPK):
                            for j in range(NJ):
                                pool.indirect_dma_start(
                                    y_sel[:, c, j, :], None, ys_dram[q],
                                    bass.IndirectOffsetOnAxis(ap=slot[q][:, c, j:j + 1], axis=0)).then_inc(gathered, 16)
                    if s.has("E") and k == MISC["E_T"] - 2:
                        pool.wait_ge(mv_ready, s.count("E", NJ, NJ))
                        rstd_of(mv[:, :, 1], var, var_ready, rstd, rstd_ready, s, "E", one)
                    if s.has("A") and k == MISC["A_T"] - 4:
                        pool.wait_ge(ss1_ready, s.count("A", NJ, NJ))
                        rstd_of(ss1[:, :], ms1, ms1_ready, rstd1, rstd1_ready, s, "A", per_d)
                        pool.wait_ge(rstd1_ready, s.count("A", 1, 1))
                        q = s.parity("A")
                        pool.tensor_tensor(out=xn[:, :, :], in0=x[q][:, :, :],
                                           in1=rstd1[:, :].unsqueeze(2).to_broadcast([P, NJ, D]),
                                           op=ALU.mult).then_inc(xn_ready, 1)
                    if s.has("F") and k == MISC["F_out"] + 1:
                        pool.wait_ge(mv2_ready, s.count("F", NJ, NJ))
                        rstd_of(mv2[:, :, 1], var2, var2_ready, rstd_b, rstd_b_ready, s, "F", one)
                    if s.has("A") and k == MISC["A_dd1"] + 2:
                        q = s.parity("A")
                        pool.wait_ge(delta_ready, s.count("A", 1, 1))
                        pool.tensor_tensor(out=dx[q][:, :, :], in0=delta[q][:, :, :], in1=act_x[:, :, :],
                                           op=ALU.mult).then_inc(dx_ready, 1)

            def add_state(s, stage, n):
                q = s.parity(stage)
                y = (y_even[q], y_odd)[n % 2]
                if n == 0:
                    pool.wait_ge(y_init, s.count(stage, NH, NH))
                pool.wait_ge(hc_ready, s.count(stage, NS, n + 1))
                if n >= 2:
                    pool.wait_ge(added, s.count(stage, ADDS, additions(n - 2)))
                pool.tensor_tensor(out=y[:, :, :], in0=y[:, :, :], in1=hc[:, n % 2, :, :],
                                   op=ALU.add).then_inc(added, 1)

            pool.wait_ge(mamba_weights, 16 * N_MAMBA)
            run_pipeline(pool, iteration)

        @block.scalar
        def _(act):
            act.wait_ge(mamba_weights, 16 * N_MAMBA)
            act.activation(a_neg[:, :, :], a_neg[:, :, :], ACT.Exp).then_inc(a_exp, 1)
            act.wait_ge(prepared, 1)

            def take(name, s, out_ap, in_ap, **kw):
                act.wait_ge(misc_filled, s.misc(name) + 1)
                act.activation(out_ap, in_ap, kw.pop("func", ACT.Copy), **kw).then_inc(misc_taken, 1)

            def squares(s, stage, src, scratch, dst, ready):
                for j in range(NJ):
                    act.activation(scratch[:, j, :], src[:, j, :], ACT.Square, accum_out=dst[:, j:j + 1]).then_inc(ready, 1)

            def decays(s, n):
                q = s.parity("B")
                for half in range(NH):
                    if n == 0 and half == 0:
                        act.wait_ge(delta_ready, s.count("B", 1, 1))
                    wait(act, scanned, s.count("B", NS * NH, (n - ND) * NH + half + 1))
                    act.activation(decay[:, n % ND, half, :], delta[q][:, half, :], ACT.Exp,
                                   scale=a_neg[:, half, n:n + 1]).then_inc(decay_ready, 1)

            def tile_steps(s, stage, g):
                i = tile_at(g, -1)
                if i is not None:
                    wait(act, up_filled, s.count(stage, NT, i - 1))
                    act.wait_ge(small_filled, s.count(stage, 2 * NT, small_use("x", i) + 1))
                    act.activation(xsT[:, i % 2, :], small[:, 0:P], ACT.Copy).then_inc(small_taken, 1)
                i = tile_at(g, 0)
                if i is not None:
                    wait(act, silu_ready, s.count(stage, NT, i - 1))
                    act.wait_ge(gate_filled, s.count(stage, NT, i + 1))
                    act.activation(th_gate[:, i % 2, :], g_bank[:, :], ACT.Tanh, scale=0.5).then_inc(th_gate_ready, 1)
                i = tile_at(g, 1)
                if i is not None:
                    if i >= 2:
                        act.wait_ge(small_filled, s.count(stage, 2 * NT, small_use("y", i - 2) + 1))
                    act.wait_ge(turned, s.count(stage, NT, i + 1))
                    act.activation(hidT[:, i % 2, :, :].rearrange("p q t -> p (q t)"), turn_bank[:, :],
                                   ACT.Copy).then_inc(turn_taken, 1)
                i = tile_at(g, 2)
                if i is not None:
                    wait(act, tile_stored[i % NB], s.count(stage, 16 * NT // NB, 16 * (i // NB)))
                    act.wait_ge(small_filled, s.count(stage, 2 * NT, small_use("y", i) + 1))
                    act.activation(ys[:, i % NB, :], small[:, 0:D], ACT.Copy).then_inc(small_taken, 1)

            def iteration(s):
                for k in range(UNITS):
                    if s.has("B"):
                        if k == 0:
                            decays(s, 0)
                        if k % 2 == 1 and (k + 1) // 2 < NS:
                            decays(s, (k + 1) // 2)
                    if s.has("tail"):
                        tile_steps(s, "tail", k + UNITS)
                    if s.has("D"):
                        tile_steps(s, "D", k)
                    if s.has("C"):
                        q = s.parity("C")
                        if k == MISC["C_out"]:
                            act.wait_ge(misc_taken, s.misc("C_out") + 1)
                            wait(act, rstd2_ready, s.count("C", 1, 0))
                            wait(act, scattered, s.count("C", 16 * TOPK * NJ, 0))
                            squares(s, "C", res, hn, ss2, ss2_ready)
                        if k == MISC["C_T"]:
                            take("C_T", s, hT[:, :], misc[:, :])
                        if k == MISC["C_router"]:
                            wait(act, weight_ready, s.count("C", 1, 0))
                            take("C_router", s, logits[:, :, :],
                                 misc[:, 0:NJ * NE].rearrange("p (j e) -> p j e", j=NJ))
                            act.wait_ge(shifted_ready, s.count("C", 1, 1))
                            act.activation(expo[:, :, :], shifted[:, :, :], ACT.Exp).then_inc(expo_ready, 1)
                        if k == MISC["C_rank"]:
                            wait(act, slot_ready, s.count("C", 1, 0))
                            take("C_rank", s, place[:, :, :],
                                 misc[:, 0:(NJ + 1) * NE].rearrange("p (j e) -> p j e", j=NJ + 1))
                    if s.has("E"):
                        if k == MISC["E_T"]:
                            take("E_T", s, x1T[:, :], misc[:, :])
                        if k == MISC["E_P"]:
                            take("E_P", s, p_ffn[:, :], misc[0:RANK, :])
                        for f in range(NQ):
                            if k == MISC[f"E_H{f}"]:
                                take(f"E_H{f}", s, h_ffn[:, f, :], misc[:, :], func=ACT.Identity,
                                     bias=b_v1[:, f:f + 1])
                        if k == MISC["E_H3"]:
                            act.wait_ge(misc_taken, s.misc("E_H3") + 1)
                            act.activation(h_ffn[:, :, :], h_ffn[:, :, :], ACT.Gelu_apprx_tanh).then_inc(h_act, 1)
                        if k == MISC["E_Q"]:
                            take("E_Q", s, q_ffn[0:RANK, :], misc[0:RANK, :])
                    if s.has("A"):
                        q = s.parity("A")
                        if k == MISC["A_T"] - 5:
                            act.wait_ge(x_loaded[q], 16 * (s.chunk("A") // 2 + 1) + 16 * s.j)
                            wait(act, ms1_ready, s.count("A", 2, 0))
                            squares(s, "A", x[q], tokens, ss1, ss1_ready)
                        if k == MISC["A_T"]:
                            take("A_T", s, xnT[:, :], misc[:, :])
                        for half in range(NH):
                            if k == MISC[f"A_xi{half}"]:
                                wait(act, tap_done, s.count("A", NH * 3, 0))
                                wait(act, halo_saved, s.count("A", 1, 0))
                                if half == 0:
                                    act.activation(xi[:, :, 0:NTAP - 1], halo[q][:, :, :], ACT.Copy).then_inc(halo_ready, 1)
                                take(f"A_xi{half}", s, xi[:, half, NTAP - 1:], misc[:, :])
                                act.wait_ge(misc_taken, s.misc(f"A_xi{half}") + 1)
                                act.wait_ge(halo_ready, s.count("A", 1, 1))
                                wait(act, act_x_ready, s.count("A", NH, half + 1 - NH))
                                act.activation(conv[:, half, :], xi[:, half, 0:T], ACT.Identity,
                                               scale=w_conv[:, half, 0:1],
                                               bias=b_conv[:, half:half + 1]).then_inc(tap0_ready, 1)
                                if half == NH - 1:
                                    act.activation(halo[q][:, :, :], xi[:, :, T:], ACT.Copy).then_inc(halo_saved, 1)
                            if k == MISC[f"A_z{half}"]:
                                act.wait_ge(misc_filled, s.misc(f"A_z{half}") + 1)
                                act.activation(th_z[:, :], misc[:, :], ACT.Tanh, scale=0.5).then_inc(th_z_ready, 1)
                            if k == MISC["A_z0"] + 1:
                                act.wait_ge(tap_done, s.count("A", NH * 3, NH * 2 + half + 1))
                                act.activation(th_conv[:, half, :], conv[:, half, :], ACT.Tanh,
                                               scale=0.5).then_inc(th_conv_ready, 1)
                                if half == NH - 1:
                                    y_start(s)
                            if k == MISC[f"A_dd{half}"]:
                                take(f"A_dd{half}", s, dt_raw[:, half, :], misc[:, :], func=ACT.Identity,
                                     bias=b_dt[:, half:half + 1])
                        if k == MISC["A_dt"]:
                            take("A_dt", s, dt_in[:, :], misc[0:R, :])
                        if k == MISC["A_BC"]:
                            wait(act, c_filled, s.count("A", NS, -NS))
                            act.wait_ge(misc_filled, s.misc("A_BC") + 1)
                            act.activation(bc[q][:, :], misc[0:3 * 2 * NS, :], ACT.Copy).then_inc(bc_ready, 1)
                        if k == MISC["A_dd1"]:
                            wait(act, delta_ready, s.count("A", 1, 0))
                            act.wait_ge(misc_taken, s.misc("A_dd1") + 1)
                            act.activation(dt_soft[:, :, :], dt_raw[:, :, :], ACT.Abs).then_inc(soft_step, 1)
                            act.wait_ge(soft_step, s.count("A", 2, 1))
                            act.activation(dt_soft[:, :, :], dt_soft[:, :, :], ACT.Exp, scale=-1.0).then_inc(soft_step, 1)
                            act.wait_ge(soft_step, s.count("A", 2, 2))
                            act.activation(dt_soft[:, :, :], dt_soft[:, :, :], ACT.Ln, bias=1.0).then_inc(soft_ready, 1)

            def y_start(s):
                q = s.parity("A")
                act.wait_ge(act_x_ready, s.count("A", NH, NH))
                wait(act, y_ready, s.count("A", 1, -1))
                for half in range(NH):
                    act.activation(y_even[q][:, half, :], act_x[:, half, :], ACT.Copy,
                                   scale=d_skip[:, half:half + 1]).then_inc(y_init, 1)

            run_pipeline(act, iteration)

        @block.tensor
        def _(pe):
            pe.wait_ge(const_made, 15)
            pe.wait_ge(sel_made, 7)
            pe.wait_ge(prepared, 1)

            def bank_free(name, s):
                wait(pe, misc_taken, s.misc(name))

            def transposes(name, s, src):
                bank_free(name, s)
                for j in range(NJ):
                    last = pe.transpose(misc_tok[:, j, :], src[:, j, :], ident[:, :])
                last.then_inc(misc_filled, 1)

            def broadcast(s, n):
                q = s.parity("B")
                if n == 0:
                    pe.wait_ge(bc_ready, s.count("B", 5, 5))
                wait(pe, scanned, s.count("B", NS * NH, n * NH))
                pe.matmul(b_bank[:, :], pick[:, n:n + 1].to_broadcast([3 * 2 * NS, P]), bc[q][:, :], start=True, stop=True).then_inc(b_filled, 1)
                wait(pe, hc_ready, s.count("B", NS, n))
                pe.matmul(c_bank[:, :], pick[:, NS + n:NS + n + 1].to_broadcast([3 * 2 * NS, P]), bc[q][:, :], start=True, stop=True).then_inc(c_filled, 1)

            def tile_steps(s, stage, g):
                q = s.parity(stage)
                i = tile_at(g, -1)
                if i is not None:
                    if i == 0:
                        pe.wait_ge(expert_ready, s.count(stage, 1, 1))
                    pe.wait_ge(tile_loaded[i % NB], s.count(stage, 16 * NT // NB, 16 * (i // NB + 1)))
                    wait(pe, small_taken, s.count(stage, 2 * NT, small_use("x", i)))
                    pe.transpose(small[:, 0:P], xs[:, i % NB, :], ident[:, :]).then_inc(small_filled, 1)
                i = tile_at(g, 0)
                if i is not None:
                    if i == 0:
                        pe.wait_ge(gates_scaled, 2)
                    e = pe.value_load(tile_expert[q][0:1, i:i + 1], min_val=0, max_val=NE - 1)
                    pe.wait_ge(small_taken, s.count(stage, 2 * NT, small_use("x", i) + 1))
                    wait(pe, silu_ready, s.count(stage, NT, i))
                    pe.matmul(g_bank[:, :], xsT[:, i % 2, :], w_gate[:, bass.ds(e, 1), :], start=True,
                              stop=True).then_inc(gate_filled, 1)
                    wait(pe, hid_ready, s.count(stage, NT, i))
                    pe.matmul(up_bank[:, :], xsT[:, i % 2, :], w_up[:, bass.ds(e, 1), :], start=True,
                              stop=True).then_inc(up_filled, 1)
                i = tile_at(g, 1)
                if i is not None:
                    pe.wait_ge(hid_ready, s.count(stage, NT, i + 1))
                    wait(pe, turn_taken, s.count(stage, NT, i))
                    for f in range(NQ):
                        last = pe.transpose(turn_bank[:, f * P:(f + 1) * P], hid[:, i % 2, f * P:(f + 1) * P], ident[:, :])
                    last.then_inc(turned, 1)
                i = tile_at(g, 2)
                if i is not None:
                    e = pe.value_load(tile_expert[q][0:1, i:i + 1], min_val=0, max_val=NE - 1)
                    pe.wait_ge(turn_taken, s.count(stage, NT, i + 1))
                    pe.wait_ge(small_taken, s.count(stage, 2 * NT, small_use("y", i)))
                    for f in range(NQ):
                        last = pe.matmul(small[:, 0:D], hidT[:, i % 2, f, :], w_down[:, bass.ds(e, 1), f, :],
                                         start=(f == 0), stop=(f == NQ - 1))
                    last.then_inc(small_filled, 1)

            def iteration(s):
                for k in range(UNITS):
                    if s.has("B") and k % 2 == 0:
                        broadcast(s, k // 2)
                    if s.has("C"):
                        q = s.parity("C")
                        if k == MISC["C_out"]:
                            bank_free("C_out", s)
                            pe.wait_ge(y_ready, s.count("C", 1, 1))
                            for j in range(NJ):
                                for half in range(NH):
                                    last = pe.matmul(misc_tok[:, j, :], y_gated[:, half, j * P:(j + 1) * P],
                                                     w_out[:, half, :], start=(half == 0), stop=(half == NH - 1))
                            last.then_inc(misc_filled, 1)
                        if k == MISC["C_T"]:
                            pe.wait_ge(hn_ready, s.count("C", 1, 1))
                            transposes("C_T", s, hn)
                        if k == MISC["C_router"]:
                            bank_free("C_router", s)
                            for j in range(NJ):
                                last = pe.matmul(misc[:, j * NE:(j + 1) * NE], hT[:, j * P:(j + 1) * P],
                                                 w_router[:, :], start=True, stop=True)
                            last.then_inc(misc_filled, 1)
                        if k == MISC["C_rank"]:
                            bank_free("C_rank", s)
                            pe.wait_ge(mask_ready, s.count("C", 1, 1))
                            pe.matmul(misc[:, 0:NJ * NE], earlier[:, :], mask[:, :, :].rearrange("p j e -> p (j e)"),
                                      start=True, stop=False)
                            for j in range(NJ - 1):
                                pe.matmul(misc[:, (j + 1) * NE:NJ * NE].rearrange("p (j e) -> p j e", e=NE), all_ones[:, :],
                                          mask[:, j, :].unsqueeze(1).to_broadcast([P, NJ - 1 - j, NE]),
                                          start=False, stop=(j == NJ - 2))
                            for j in range(NJ):
                                last = pe.matmul(misc[:, NJ * NE:(NJ + 1) * NE], all_ones[:, :], mask[:, j, :],
                                                 start=(j == 0), stop=(j == NJ - 1))
                            last.then_inc(misc_filled, 1)
                    if s.has("tail"):
                        tile_steps(s, "tail", k + UNITS)
                    if s.has("D"):
                        tile_steps(s, "D", k)
                    if s.has("E"):
                        if k == MISC["E_T"]:
                            pe.wait_ge(x1_ready, s.count("E", NJ, NJ))
                            pe.wait_ge(ffn_weights, 16 * 5)
                            transposes("E_T", s, x1)
                        if k == MISC["E_P"]:
                            bank_free("E_P", s)
                            pe.matmul(misc[0:RANK, :], w_u1[:, :], x1T[:, :], start=True, stop=True).then_inc(misc_filled, 1)
                        for f in range(NQ):
                            if k == MISC[f"E_H{f}"]:
                                bank_free(f"E_H{f}", s)
                                pe.matmul(misc[:, :], w_v1[:, f * P:(f + 1) * P], p_ffn[:, :], start=True,
                                          stop=True).then_inc(misc_filled, 1)
                        if k == MISC["E_Q"]:
                            bank_free("E_Q", s)
                            pe.wait_ge(h_act, s.count("E", 1, 1))
                            for f in range(NQ):
                                last = pe.matmul(misc[0:RANK, :], w_u2[:, f, :], h_ffn[:, f, :], start=(f == 0),
                                                 stop=(f == NQ - 1))
                            last.then_inc(misc_filled, 1)
                    if s.has("F") and k == MISC["F_out"]:
                        bank_free("F_out", s)
                        for j in range(NJ):
                            last = pe.matmul(misc_tok[:, j, :], q_ffn[:, j * P:(j + 1) * P], w_v2[:, :],
                                             start=True, stop=True)
                        last.then_inc(misc_filled, 1)
                    if s.has("A"):
                        q = s.parity("A")
                        if k == MISC["A_T"]:
                            pe.wait_ge(xn_ready, s.count("A", 1, 1))
                            transposes("A_T", s, xn)
                        for part, name in enumerate(("A_xi0", "A_xi1", "A_z0", "A_z1")):
                            if k == MISC[name]:
                                bank_free(name, s)
                                pe.matmul(misc[:, :], w_in[:, part * P:(part + 1) * P], xnT[:, :], start=True,
                                          stop=True).then_inc(misc_filled, 1)
                        if k == MISC["A_dt"]:
                            bank_free("A_dt", s)
                            pe.wait_ge(act_x_ready, s.count("A", NH, NH))
                            for half in range(NH):
                                last = pe.matmul(misc[0:R, :], w_x[:, half, 0:R], act_x[:, half, :],
                                                 start=(half == 0), stop=(half == NH - 1))
                            last.then_inc(misc_filled, 1)
                        if k == MISC["A_BC"]:
                            bank_free("A_BC", s)
                            for half in range(NH):
                                last = pe.matmul(misc[0:3 * 2 * NS, :], w_bc[:, half, :, :], act_x[:, half, :],
                                                 start=(half == 0), stop=(half == NH - 1))
                            last.then_inc(misc_filled, 1)
                        for half in range(NH):
                            if k == MISC[f"A_dd{half}"]:
                                bank_free(f"A_dd{half}", s)
                                pe.matmul(misc[:, :], w_dt[:, half * P:(half + 1) * P], dt_in[:, :], start=True,
                                          stop=True).then_inc(misc_filled, 1)

            run_pipeline(pe, iteration)

        @block.vector
        def _(dve):
            dve.memset(q_ffn[RANK:RANK + 1, :], 1.0).then_inc(const_made, 1)
            dve.memset(h[:, :, :, :], 0.0).then_inc(slots_zero, 1)
            dve.wait_ge(mamba_weights, 16 * N_MAMBA)
            dve.wait_ge(a_exp, 1)
            dve.tensor_scalar(out=a_neg[:, :, :], in0=a_neg[:, :, :], scalar1=-1.0, scalar2=None, op0=ALU.mult)
            dve.tensor_scalar(out=w_in[:, :], in0=w_in[:, :], scalar1=w_rms1[:, 0:1], scalar2=None, op0=ALU.mult)
            dve.tensor_scalar(out=w_router[:, :], in0=w_router[:, :], scalar1=w_rms2[:, 0:1], scalar2=None, op0=ALU.mult)
            for term in range(3):
                dve.tensor_scalar(out=w_bc[:, :, term, :], in0=w_x[:, :, R:], scalar1=0.5, scalar2=None, op0=ALU.mult)
            dve.tensor_scalar(out=w_x[:, :, 0:R], in0=w_x[:, :, 0:R], scalar1=0.5, scalar2=None, op0=ALU.mult)
            dve.tensor_scalar(out=w_out[:, :, :], in0=w_out[:, :, :], scalar1=0.25, scalar2=None,
                              op0=ALU.mult).then_inc(prepared, 1)
            dve.wait_ge(const_made, 15)

            def multiply_b(s, n):
                q = s.parity("B")
                if n == 0:
                    dve.wait_ge(dx_ready, s.count("B", 1, 1))
                    if s.chunk("B") == 0:
                        dve.wait_ge(cleared, 16 * 2)
                dve.wait_ge(b_filled, s.count("B", NS, n + 1))
                for half, dst in enumerate((u_bank, b_bank)):
                    dve.tensor_tensor(out=dst[:, :], in0=dx[q][:, half, :], in1=b_bank[:, :],
                                      op=ALU.mult).then_inc(u_ready, 1)

            def scan(s, n):
                q = s.parity("B")
                for half, src in enumerate((u_bank, b_bank)):
                    dve.wait_ge(decay_ready, s.count("B", NS * NH, n * NH + half + 1))
                    dve.wait_ge(u_ready, s.count("B", NS * NH, n * NH + half + 1))
                    if half == 0 and s.chunk("B") >= 2:
                        dve.wait_ge(carried, s.count("B", NS, n + 1 - 2 * NS))
                    dve.tensor_tensor_scan(out=h[:, n % 2, half, :], data0=decay[:, n % ND, half, :], data1=src[:, :],
                                           initial=carry[q][:, n, half:half + 1], op0=ALU.mult,
                                           op1=ALU.add).then_inc(scanned, 1)

            def multiply_c(s, stage, n):
                q = s.parity(stage)
                dve.wait_ge(scanned, s.count(stage, NS * NH, (n + 1) * NH))
                dve.wait_ge(c_filled, s.count(stage, NS, n + 1))
                if n >= 2:
                    dve.wait_ge(added, s.count(stage, ADDS, additions(n - 2)))
                else:
                    wait(dve, added, s.count(stage, ADDS, 0))
                if n == 1:
                    wait(dve, y_summed, s.count(stage, 1, 0))
                dst = y_odd[:, :, :] if n == 1 else hc[:, n % 2, :, :]
                dve.tensor_tensor(out=dst, in0=h[:, n % 2, :, :],
                                  in1=c_bank[:, :].unsqueeze(1).to_broadcast([P, NH, T]),
                                  op=ALU.mult).then_inc(hc_ready, 1)
                dve.tensor_copy(carry[q][:, n, :], h[:, n % 2, :, T - 1]).then_inc(carried, 1)

            def tile_steps(s, stage, g):
                i = tile_at(g, 0)
                if i is not None:
                    dve.wait_ge(th_gate_ready, s.count(stage, NT, i + 1))
                    dve.scalar_tensor_tensor(out=th_gate[:, i % 2, :], in0=th_gate[:, i % 2, :], scalar=1.0,
                                             in1=g_bank[:, :], op0=ALU.add, op1=ALU.mult).then_inc(silu_ready, 1)
                    dve.wait_ge(up_filled, s.count(stage, NT, i + 1))
                    dve.wait_ge(silu_ready, s.count(stage, NT, i + 1))
                    wait(dve, turned, s.count(stage, NT, i - 1))
                    dve.tensor_tensor(out=hid[:, i % 2, :], in0=th_gate[:, i % 2, :], in1=up_bank[:, :],
                                      op=ALU.mult).then_inc(hid_ready, 1)

            def combine(s):
                q = s.parity("E")
                dve.wait_ge(gathered, s.count("E", 16 * TOPK * NJ, 16 * TOPK * NJ))
                dve.wait_ge(acc_init, s.count("E", 1, 1))
                for c in range(TOPK):
                    if c > 0:
                        dve.wait_ge(combined, s.count("E", TOPK * NJ, c * NJ))
                    for j in range(NJ):
                        dve.scalar_tensor_tensor(out=acc[q][:, j, :], in0=y_sel[:, c, j, :], scalar=weight[q][:, c, j:j + 1],
                                                 in1=acc[q][:, j, :], op0=ALU.mult, op1=ALU.add).then_inc(combined, 1)

            def layer_norm_stats(src, st, st_ready):
                for j in range(NJ):
                    dve.bn_stats(out=st[:, j, :], in_=src[:, j, :]).then_inc(st_ready, 1)

            def layer_norm_aggregate(st, mean_var, mv_done):
                for j in range(NJ):
                    dve.bn_aggr(out=mean_var[:, j, :], in_=st[:, j, :]).then_inc(mv_done, 1)

            def normalize(s, src, mean_var, rs, dst, done):
                for j in range(NJ):
                    dve.tensor_scalar(out=dst[:, j, :], in0=src[:, j, :], scalar1=mean_var[:, j, 0:1],
                                      scalar2=rs[:, j:j + 1], op0=ALU.subtract, op1=ALU.mult).then_inc(done, 1)

            def route(s):
                q = s.parity("C")
                dve.wait_ge(misc_taken, s.misc("C_router") + 1)
                dve.tensor_reduce(out=top[:, :], in_=logits[:, :, :], axis=AX.X, op=ALU.max).then_inc(top_ready, 1)
                mine = logits[:, :, :].unsqueeze(3).to_broadcast([P, NJ, NE, NE])
                other = logits[:, :, :].unsqueeze(2).to_broadcast([P, NJ, NE, NE])
                flat = lambda a: a[:, :, :, :].rearrange("p j e f -> p j (e f)")
                tie_order = before[:, :, :].rearrange("p e f -> p (e f)").unsqueeze(1).to_broadcast([P, NJ, NE * NE])
                dve.tensor_tensor(out=ties[:, :, :, :], in0=other, in1=mine, op=ALU.is_equal).then_inc(route_step, 1)
                dve.tensor_tensor(out=beats[:, :, :, :], in0=other, in1=mine, op=ALU.is_gt).then_inc(route_step, 1)
                dve.wait_ge(top_ready, s.count("C", 1, 1))
                dve.tensor_tensor(out=shifted[:, :, :], in0=logits[:, :, :],
                                  in1=top[:, :].unsqueeze(2).to_broadcast([P, NJ, NE]),
                                  op=ALU.subtract).then_inc(shifted_ready, 1)
                dve.wait_ge(route_step, s.count("C", 5, 2))
                dve.tensor_tensor(out=flat(ties2), in0=flat(ties), in1=tie_order, op=ALU.mult).then_inc(route_step, 1)
                dve.wait_ge(route_step, s.count("C", 5, 3))
                dve.tensor_tensor(out=flat(beats2), in0=flat(beats), in1=flat(ties2), op=ALU.add).then_inc(route_step, 1)
                dve.wait_ge(route_step, s.count("C", 5, 4))
                dve.tensor_reduce(out=rank[:, :, :], in_=beats2[:, :, :, :], axis=AX.X, op=ALU.add).then_inc(route_step, 1)
                dve.wait_ge(route_step, s.count("C", 5, 5))
                dve.tensor_scalar(out=mask[:, :, :], in0=rank[:, :, :], scalar1=1.5, scalar2=None,
                                  op0=ALU.is_lt).then_inc(mask_ready, 1)

            def weigh(s):
                q = s.parity("C")
                for c in range(TOPK):
                    dve.tensor_scalar(out=choice[:, c, :, :], in0=rank[:, :, :], scalar1=float(c), scalar2=None,
                                      op0=ALU.is_equal).then_inc(weight_step, 1)
                dve.wait_ge(expo_ready, s.count("C", 1, 1))
                dve.tensor_reduce(out=denom[:, :], in_=expo[:, :, :], axis=AX.X, op=ALU.add).then_inc(weight_step, 1)
                dve.wait_ge(weight_step, s.count("C", 6, 2))
                dve.tensor_tensor(out=chosen[:, :, :, :], in0=choice[:, :, :, :],
                                  in1=expo[:, :, :].unsqueeze(1).to_broadcast([P, TOPK, NJ, NE]),
                                  op=ALU.mult).then_inc(weight_step, 1)
                dve.wait_ge(weight_step, s.count("C", 6, 3))
                dve.reciprocal(rdenom[:, :], denom[:, :]).then_inc(weight_step, 1)
                dve.wait_ge(weight_step, s.count("C", 6, 4))
                dve.tensor_reduce(out=chosen_w[:, :, :], in_=chosen[:, :, :, :], axis=AX.X, op=ALU.add).then_inc(weight_step, 1)
                dve.wait_ge(weight_step, s.count("C", 6, 6))
                dve.tensor_tensor(out=weight[q][:, :, :], in0=chosen_w[:, :, :],
                                  in1=rdenom[:, :].unsqueeze(1).to_broadcast([P, TOPK, NJ]),
                                  op=ALU.mult).then_inc(weight_ready, 1)

            def slots(s):
                q = s.parity("C")

                def step(n):
                    dve.wait_ge(tiles_step, s.count("C", 8, n))

                dve.wait_ge(misc_taken, s.misc("C_rank") + 1)
                dve.tensor_tensor(out=over[:, :, :], in0=place[:, NJ, :].unsqueeze(2).to_broadcast([P, NE, NJ]),
                                  in1=whole[:, :].unsqueeze(1).to_broadcast([P, NE, NJ]), op=ALU.is_gt).then_inc(tiles_step, 1)
                step(1)
                dve.tensor_reduce(out=tiles[:, :], in_=over[:, :, :], axis=AX.X, op=ALU.add).then_inc(tiles_step, 1)
                step(2)
                dve.tensor_tensor(out=tiles_b[:, :, :], in0=tiles[:, :].unsqueeze(1).to_broadcast([P, NE, NE]),
                                  in1=before[:, :, :], op=ALU.mult).then_inc(tiles_step, 1)
                step(3)
                dve.tensor_reduce(out=first_tile[:, :], in_=tiles_b[:, :, :], axis=AX.X, op=ALU.add).then_inc(tiles_step, 1)
                step(4)
                dve.scalar_tensor_tensor(out=place2[:, :, :], in0=first_tile[:, :].unsqueeze(1).to_broadcast([P, NJ, NE]),
                                         scalar=float(P), in1=place[:, 0:NJ, :], op0=ALU.mult,
                                         op1=ALU.add).then_inc(tiles_step, 1)
                dve.tensor_tensor(out=end_tile[:, :], in0=first_tile[:, :], in1=tiles[:, :],
                                  op=ALU.add).then_inc(tiles_step, 1)
                step(5)
                dve.tensor_tensor(out=picked[:, :, :, :], in0=choice[:, :, :, :],
                                  in1=place2[:, :, :].unsqueeze(1).to_broadcast([P, TOPK, NJ, NE]),
                                  op=ALU.mult).then_inc(tiles_step, 1)
                step(7)
                dve.tensor_reduce(out=slot_f[:, :, :], in_=picked[:, :, :, :], axis=AX.X, op=ALU.add).then_inc(slot_f_ready, 1)
                dve.wait_ge(slot_f_ready, s.count("C", 1, 1))
                dve.tensor_copy(slot[q][:, :, :], slot_f[:, :, :]).then_inc(slot_ready, 1)
                dve.tensor_tensor(out=passed[:, :, :], in0=tile_no[:, :].unsqueeze(2).to_broadcast([1, NT, NE]),
                                  in1=end_tile[0:1, :].unsqueeze(1).to_broadcast([1, NT, NE]),
                                  op=ALU.is_ge).then_inc(passed_ready, 1)
                dve.wait_ge(passed_ready, s.count("C", 1, 1))
                dve.tensor_reduce(out=passed_n[:, :], in_=passed[:, :, :], axis=AX.X, op=ALU.add).then_inc(tiles_step, 1)
                step(8)
                dve.tensor_scalar(out=tile_expert[q][:, :], in0=passed_n[:, :], scalar1=float(NE - 1), scalar2=None,
                                  op0=ALU.min).then_inc(expert_ready, 1)

            def stage_a(s, k):
                q = s.parity("A")
                if k == MISC["A_z0"]:
                    for tap in range(1, NTAP):
                        for half in range(NH):
                            if tap == 1:
                                dve.wait_ge(tap0_ready, s.count("A", NH, half + 1))
                            else:
                                dve.wait_ge(tap_done, s.count("A", NH * 3, NH * (tap - 2) + half + 1))
                            dve.scalar_tensor_tensor(out=conv[:, half, :], in0=xi[:, half, tap:tap + T],
                                                     scalar=w_conv[:, half, tap:tap + 1], in1=conv[:, half, :],
                                                     op0=ALU.mult, op1=ALU.add).then_inc(tap_done, 1)
                for half in range(NH):
                    if k == MISC[f"A_z{half}"]:
                        dve.wait_ge(th_z_ready, s.count("A", NH, half + 1))
                        dve.scalar_tensor_tensor(out=gate_z[q][:, half, :], in0=th_z[:, :], scalar=1.0, in1=misc[:, :],
                                                 op0=ALU.add, op1=ALU.mult).then_inc(misc_taken, 1)
                if k == MISC["A_z0"] + 1:
                    for half in range(NH):
                        dve.wait_ge(th_conv_ready, s.count("A", NH, half + 1))
                        dve.scalar_tensor_tensor(out=act_x[:, half, :], in0=th_conv[:, half, :], scalar=1.0,
                                                 in1=conv[:, half, :], op0=ALU.add, op1=ALU.mult).then_inc(act_x_ready, 1)
                if k == MISC["A_BC"]:
                    dve.wait_ge(bc_ready, s.count("A", 5, 1))
                    dve.tensor_tensor(out=bc_rest[:, :], in0=misc[0:3 * 2 * NS, :], in1=bc[q][:, :],
                                      op=ALU.subtract).then_inc(misc_taken, 1)
                    dve.wait_ge(misc_taken, s.misc("A_BC") + 1)
                    dve.tensor_copy(bc_mid[:, :], bc_rest[:, :]).then_inc(mid_ready, 1)
                    dve.wait_ge(mid_ready, s.count("A", 1, 1))
                    dve.tensor_tensor(out=bc_rest2[:, :], in0=bc_rest[:, :], in1=bc_mid[:, :],
                                      op=ALU.subtract).then_inc(rest2_ready, 1)
                    dve.tensor_copy(bc[q][2 * NS:4 * NS, :], bc_mid[2 * NS:4 * NS, :]).then_inc(bc_ready, 1)
                    dve.wait_ge(rest2_ready, s.count("A", 1, 1))
                    dve.tensor_copy(bc[q][4 * NS:6 * NS, :], bc_rest2[4 * NS:6 * NS, :]).then_inc(bc_ready, 3)
                if k == MISC["A_dd1"] + 1:
                    dve.wait_ge(soft_ready, s.count("A", 1, 1))
                    wait(dve, decay_ready, s.count("A", NS * NH, -NS * NH))
                    dve.scalar_tensor_tensor(out=delta[q][:, :, :], in0=dt_raw[:, :, :], scalar=0.0, in1=dt_soft[:, :, :],
                                             op0=ALU.max, op1=ALU.add).then_inc(delta_ready, 1)

            def iteration(s):
                for k in range(UNITS):
                    if s.has("E") and k == MISC["E_T"] - 2:
                        dve.wait_ge(stats_ready, s.count("E", NJ, NJ))
                    if s.has("F") and k == MISC["F_out"] + 1:
                        dve.wait_ge(stats2_ready, s.count("F", NJ, NJ))
                    if s.has("B") and k % 2 == 0:
                        multiply_b(s, k // 2)
                        scan(s, k // 2)
                    if s.has("B") and k % 2 == 1 and k < UNITS - 1:
                        multiply_c(s, "B", k // 2)
                    if s.has("C") and k == 0:
                        multiply_c(s, "C", NS - 1)
                    if s.has("C") and k == 1:
                        q = s.parity("C")
                        dve.wait_ge(added, s.count("C", ADDS, ADDS))
                        dve.tensor_tensor(out=y_even[q][:, :, :], in0=y_even[q][:, :, :], in1=y_odd[:, :, :],
                                          op=ALU.add).then_inc(y_summed, 1)
                        dve.wait_ge(y_summed, s.count("C", 1, 1))
                        dve.tensor_tensor(out=y_gated[:, :, :], in0=y_even[q][:, :, :], in1=gate_z[q][:, :, :],
                                          op=ALU.mult).then_inc(y_ready, 1)
                    if s.has("C") and k == MISC["C_out"]:
                        q = s.parity("C")
                        dve.wait_ge(misc_filled, s.misc("C_out") + 1)
                        dve.tensor_tensor(out=res[:, :, :], in0=misc_tok, in1=x[q][:, :, :], op=ALU.add).then_inc(misc_taken, 1)
                    if s.has("C") and k == MISC["C_router"]:
                        route(s)
                    if s.has("C") and k == MISC["C_router"] + 1:
                        weigh(s)
                    if s.has("C") and k == MISC["C_rank"] + 1:
                        slots(s)
                    if s.has("tail"):
                        tile_steps(s, "tail", k + UNITS)
                    if s.has("D"):
                        tile_steps(s, "D", k)
                    if s.has("E"):
                        q = s.parity("E")
                        if k == MISC["E_T"] - 3:
                            combine(s)
                            dve.wait_ge(combined, s.count("E", TOPK * NJ, TOPK * NJ))
                            layer_norm_stats(acc[q], stats, stats_ready)
                        if k == MISC["E_T"] - 2:
                            layer_norm_aggregate(stats, mv, mv_ready)
                        if k == MISC["E_T"] - 1:
                            dve.wait_ge(rstd_ready, s.count("E", 1, 1))
                            normalize(s, acc[q], mv, rstd, x1, x1_ready)
                    if s.has("F"):
                        q = s.parity("F")
                        if k == MISC["F_out"]:
                            dve.wait_ge(misc_filled, s.misc("F_out") + 1)
                            dve.tensor_tensor(out=r2[:, :, :], in0=misc_tok, in1=x1[:, :, :], op=ALU.add).then_inc(misc_taken, 1)
                            dve.wait_ge(misc_taken, s.misc("F_out") + 1)
                            layer_norm_stats(r2, stats2, stats2_ready)
                        if k == MISC["F_out"] + 1:
                            layer_norm_aggregate(stats2, mv2, mv2_ready)
                        if k == MISC["F_out"] + 3:
                            dve.wait_ge(rstd_b_ready, s.count("F", 1, 1))
                            if s.chunk("F") >= 2:
                                dve.wait_ge(stored[q], 16 * (s.chunk("F") // 2) + 16 * s.j)
                            normalize(s, r2, mv2, rstd_b, y_out[q], y_out_ready)
                    if s.has("A"):
                        stage_a(s, k)
                    if s.i0 == 0 and k in (22, 26):
                        w, half = ((w_gate, 1.0), (w_up, 0.5))[k == 26]
                        dve.wait_ge(expert_weights, 16 * N_EXPERT)
                        dve.tensor_scalar(out=w[:, :, :], in0=w[:, :, :], scalar1=w_rms2[:, 0:1], scalar2=half,
                                          op0=ALU.mult, op1=ALU.mult).then_inc(gates_scaled, 1)

            run_pipeline(dve, iteration)


_INS = ["L0_attn_hidden_states", "L0_attn_rms1_w", "L0_attn_rms2_w", "L0_attn_in_proj_w", "L0_attn_conv_w",
        "L0_attn_conv_b", "L0_attn_x_proj_w", "L0_attn_dt_proj_w", "L0_attn_dt_proj_b", "L0_attn_A_log",
        "L0_attn_D_skip", "L0_attn_out_proj_w", "L0_attn_router_w", "L0_attn_Wg", "L0_attn_Wu", "L0_attn_Wd",
        "L0_ffn_U1", "L0_ffn_V1", "L0_ffn_b1", "L0_ffn_U2", "L0_ffn_V2", "L0_ffn_b2"]


def kernel(**inputs):
    import concourse.bacc as bacc
    from concourse.bass_utils import run_bass_kernel_spmd

    nc = bacc.Bacc("TRN2", target_bir_lowering=False, num_devices=1)
    arrays, args = {}, []
    for name in _INS:
        a = np.ascontiguousarray(inputs[name])
        arrays[f"in_{name}"] = a
        args.append(nc.dram_tensor(f"in_{name}", a.shape, mybir.dt.from_np(a.dtype), kind="ExternalInput").ap())
    args.append(nc.dram_tensor("out_0", (B, L, D), F32, kind="ExternalOutput").ap())
    build(nc, *args)
    r = run_bass_kernel_spmd(nc, [arrays], core_ids=[0])
    return r.results[0]["out_0"]
```

```python
import numpy as np
import concourse.bass as bass
from concourse import mybir
from contextlib import ExitStack

F32 = mybir.dt.float32
BF16 = mybir.dt.bfloat16
I32 = mybir.dt.int32
U32 = mybir.dt.uint32
ALU = mybir.AluOpType
ACT = mybir.ActivationFunctionType
AX = mybir.AxisListType

P = 128
B, L, D = 2, 2048, 128
DI = 256
NH = DI // P
NS = 16
NTAP = 4
R = 64
NE = 8
FFN = 512
NQ = FFN // P
RANK = 32
T = 512
NJ = T // P
NC = B * L // T
ADDS = NS - 1
UNITS = 2 * NS
TOPK = 2
ND = 4
NT = NJ * TOPK + NE - 1
NB = 5
LAG = 20
EPS = 1e-5

MISC = {
    "F_T": 0, "F_P": 1, "F_H0": 2, "C_out": 3, "F_H1": 4, "F_H2": 5, "F_H3": 6, "C_T": 7, "C_router": 8,
    "C_rank": 10, "F_Q": 11, "A_T": 13, "A_xi0": 14, "A_xi1": 15, "A_z0": 16, "A_z1": 17, "F_out": 19, "A_dt": 21, "A_BC": 22,
    "A_dd0": 23, "A_dd1": 24,
}
TAKE = {name: unit + 1 for name, unit in MISC.items()}
WHEN = {
    "C_last": 0, "C_gate": 2, "C_squares": 5, "C_norm": 6, "C_route": 9, "C_choose": 10, "C_expo": 10, "C_slots": 11,
    "C_weigh": 12, "C_scatter": 12,
    "E_gather": 22, "E_combine": 28,
    "F_act": 8, "F_norm": 21,
    "A_load": 7, "A_squares": 10, "A_norm": 11, "A_tap1": 17, "A_taps": 18, "A_tanh": 19, "A_silu": 20, "A_one": 19, "A_gate": 20,
    "A_start": 22, "A_split": 24, "A_soft": 25, "A_delta": 27, "A_dx": 27,
}
ORDER = sorted(MISC, key=MISC.get)


class Step:

    def __init__(self, i0, j=0):
        self.i0, self.j = i0, j

    def chunk(self, stage):
        return self.i0 + {"A": 1, "B": 0, "C": -1, "D": -1, "tail": -2, "E": -2, "F": -3}[stage]

    def has(self, stage):
        return 0 <= self.chunk(stage) < NC

    def parity(self, stage):
        return self.chunk(stage) % 2

    def time(self, stage):
        return self.chunk(stage) // 2 + self.j

    def count(self, stage, per_chunk, offset):
        return per_chunk * self.chunk(stage) + offset + per_chunk * 2 * self.j

    def misc(self, name):
        before = 0
        for i in range(-1, self.i0):
            before += sum(Step(i).has(n[0]) for n in ORDER)
        here = [n for n in ORDER if self.has(n[0])]
        return before + here.index(name) + len(ORDER) * 2 * self.j


def wait(eng, sem, value):
    if type(value) is int and value <= 0:
        return
    eng.wait_ge(sem, value)


def run_pipeline(eng, iteration):
    for i in (-1, 0, 1, 2):
        iteration(Step(i))
    with eng.Fori(0, 2, 1) as j:
        iteration(Step(3, j))
        iteration(Step(4, j))
    for i in range(7, NC + 3):
        iteration(Step(i))


def build(nc, hidden, rms1_w, rms2_w, in_proj_w, conv_w, conv_b, x_proj_w, dt_proj_w, dt_proj_b, A_log, D_skip,
          out_proj_w, router_w, Wg, Wu, Wd, U1, V1, b1, U2, V2, b2, out):
    ctx = ExitStack()
    with ctx:
        ctx.enter_context(nc.allow_non_contiguous_dma(reason="small per-channel columns"))

        def sb(name, shape, dt=F32):
            return ctx.enter_context(nc.sbuf_tensor(name, shape, dt))

        def sem(name):
            return ctx.enter_context(nc.semaphore(name))

        w_in = sb("w_in", [P, 2 * DI])
        w_conv = sb("w_conv", [P, NH, NTAP])
        b_conv = sb("b_conv", [P, NH])
        w_x = sb("w_x", [P, NH, R + 2 * NS])
        w_bc = sb("w_bc", [P, NH, 3, 2 * NS])
        w_dt = sb("w_dt", [R, DI])
        b_dt = sb("b_dt", [P, NH])
        a_neg = sb("a_neg", [P, NH, NS])
        d_skip = sb("d_skip", [P, NH])
        w_out = sb("w_out", [P, NH, D])
        w_router = sb("w_router", [P, NE])
        w_rms1 = sb("w_rms1", [P, 1])
        w_rms2 = sb("w_rms2", [P, 1])
        w_gate = sb("w_gate", [P, NE, FFN])
        w_up = sb("w_up", [P, NE, FFN])
        w_down = sb("w_down", [P, NE, NQ, D])
        w_u1 = sb("w_u1", [P, RANK])
        w_v1 = sb("w_v1", [RANK, FFN])
        b_v1 = sb("b_v1", [P, NQ])
        w_u2 = sb("w_u2", [P, NQ, RANK])
        w_v2 = sb("w_v2", [RANK + 1, D])
        ident = sb("ident", [P, P])
        pick = sb("pick", [3 * 2 * NS, 2 * NS], BF16)
        power = sb("power", [P, NJ])
        per_d, one, eps = sb("per_d", [P, NJ]), sb("one", [P, NJ]), sb("eps", [P, NJ])
        earlier = sb("earlier", [P, P], BF16)
        all_ones = sb("all_ones", [P, P], BF16)
        whole = sb("whole", [P, NJ])
        tile_no = sb("tile_no", [1, NT])
        before = sb("before", [P, NE, NE])
        x = [sb(f"x_in{q}", [P, NJ, D]) for q in range(2)]
        ss1 = sb("ss1", [P, NJ])
        ms1 = sb("ms1", [P, NJ])
        rstd1 = sb("rstd1", [P, NJ])
        work = sb("work", [P, 2 * NH, T])
        tokens = sb("tokens", [P, NJ, D])
        columns = sb("columns", [P, T])
        sums = sb("sums", [P, NJ, D])
        narrow = sb("narrow", [R, T])
        xn, xnT = tokens, columns
        xi = sb("xi", [P, NH, NTAP - 1 + T])
        halo = [sb(f"halo{q}", [P, NH, NTAP - 1]) for q in range(2)]
        conv = work[:, 0:NH, :]
        th_conv = work[:, NH:, :]
        th_z = sb("th_z", [P, NH, T])
        act_x = sb("act_x", [P, NH, T])
        gate_z = [sb(f"gate_z{q}", [P, NH, T]) for q in range(2)]
        dt_in = narrow
        bc = [sb(f"bc{q}", [3 * 2 * NS, T], BF16) for q in range(2)]
        bc_full = th_z[0:3 * 2 * NS, 0, :]
        bc_rest = th_z[0:3 * 2 * NS, 1, :]
        bc_mid = sb("bc_mid", [3 * 2 * NS, T], BF16)
        bc_rest2 = tokens[0:3 * 2 * NS, :, :].rearrange("p j d -> p (j d)")
        dt_raw = work[:, 0:NH, :]
        dt_soft = work[:, NH:, :]
        delta = [sb(f"delta{q}", [P, NH, T]) for q in range(2)]
        dx = [sb(f"dx{q}", [P, NH, T]) for q in range(2)]
        decay = sb("decay", [P, ND, NH, T])
        u = sb("u", [P, NH, T])
        h = sb("h", [P, 2, NH, T])
        carry = [sb(f"carry{q}", [P, NS, NH]) for q in range(2)]
        hc = sb("hc", [P, 2, NH, T])
        y_even = [sb(f"y_even{q}", [P, NH, T]) for q in range(2)]
        y_odd = sb("y_odd", [P, NH, T])
        res = sums
        ss2 = sb("ss2", [P, NJ])
        ms2 = sb("ms2", [P, NJ])
        rstd2 = sb("rstd2", [P, NJ])
        hn = sb("hn", [P, NJ, D])
        hT = sb("hT", [P, T])
        logits = sb("logits", [P, NJ, NE])
        top = sb("top", [P, NJ])
        shifted = sb("shifted", [P, NJ, NE])
        expo = sb("expo", [P, NJ, NE])
        beats = sb("beats", [P, NJ, NE, NE])
        ties = sb("ties", [P, NJ, NE, NE])
        rank = sb("rank", [P, NJ, NE])
        denom = sb("denom", [P, NJ])
        rdenom = sb("rdenom", [P, NJ])
        mask = sb("mask", [P, NJ, NE], BF16)
        choice = sb("choice", [P, TOPK, NJ, NE])
        chosen = sb("chosen", [P, TOPK, NJ, NE])
        chosen_w = sb("chosen_w", [P, TOPK, NJ])
        weight = [sb(f"weight{q}", [P, TOPK, NJ]) for q in range(2)]
        place = sb("place", [P, NJ + 1, NE])
        over = sb("over", [P, NE, NJ])
        tiles = sb("tiles", [P, NE])
        tiles_b = sb("tiles_b", [P, NE, NE])
        first_tile = sb("first_tile", [P, NE])
        end_tile = sb("end_tile", [P, NE])
        passed = sb("passed", [1, NT, NE])
        passed_n = sb("passed_n", [1, NT])
        place2 = sb("place2", [P, NJ, NE])
        picked = sb("picked", [P, TOPK, NJ, NE])
        slot_f = sb("slot_f", [P, TOPK, NJ])
        slot = [sb(f"slot{q}", [P, TOPK, NJ], U32) for q in range(2)]
        tile_expert = [sb(f"tile_expert{q}", [1, NT], I32) for q in range(2)]
        xs = sb("xs", [P, NB, D])
        xsT = sb("xsT", [P, 2, P])
        th_gate = sb("th_gate", [P, 2, FFN])
        hid = sb("hid", [P, 2, FFN])
        hidT = sb("hidT", [P, 2, NQ, P])
        ys = sb("ys", [P, NB, D])
        y_sel = sb("y_sel", [P, TOPK, NJ, D])
        acc = [sb(f"acc{q}", [P, NJ, D]) for q in range(2)]
        xs_dram = [nc.dram_tensor(f"xs_dram{q}", (NT * P, D), F32, kind="Internal").ap() for q in range(2)]
        ys_dram = [nc.dram_tensor(f"ys_dram{q}", (NT * P, D), F32, kind="Internal").ap() for q in range(2)]
        stats = sb("stats", [P, NJ, 6])
        mv = sb("mv", [P, NJ, 2])
        var = sb("var", [P, NJ])
        rstd = sb("rstd", [P, NJ])
        x1 = sb("x_mid", [P, NJ, D])
        x1T = columns
        p_ffn = narrow[0:RANK, :]
        h_ffn = work
        q_ffn = sb("q_ffn", [RANK + 1, T])
        y_out = sb("y_out", [P, NJ, D])
        stats2 = sb("stats2", [P, NJ, 6])
        mv2 = sb("mv2", [P, NJ, 2])
        var2 = sb("var2", [P, NJ])
        rstd_b = sb("rstd_b", [P, NJ])

        bank = [ctx.enter_context(nc.psum_tensor(f"bank{i}", [P, T], F32)) for i in range(8)]
        b_bank, c_bank, x_bank, g_bank, up_bank, turn_bank, y_bank, misc = bank
        misc_tok = misc[:, :].rearrange("p (j d) -> p j d", j=NJ)

        mamba_weights, expert_weights, ffn_weights = sem("mamba_weights"), sem("expert_weights"), sem("ffn_weights")
        x_loaded = [sem(f"x_loaded{q}") for q in range(2)]
        stored = sem("stored")
        const_made, sel_made, a_exp, prepared, gates_scaled = (
            sem("const_made"), sem("sel_made"), sem("a_exp"), sem("prepared"), sem("gates_scaled"))
        misc_filled, misc_taken = sem("misc_filled"), sem("misc_taken")
        ss1_ready, ms1_ready, rstd1_ready, xn_ready = sem("ss1_ready"), sem("ms1_ready"), sem("rstd1_ready"), sem("xn_ready")
        halo_ready, halo_saved, tap0_ready, tap_done, th_conv_ready, act_x_ready = (
            sem("halo_ready"), sem("halo_saved"), sem("tap0_ready"), sem("tap_done"), sem("th_conv_ready"), sem("act_x_ready"))
        centred, centred2 = sem("centred"), sem("centred2")
        th_z_ready, th_one_ready, gate_z_ready = sem("th_z_ready"), sem("th_one_ready"), sem("gate_z_ready")
        rest_ready, mid_ready, rest2_ready, bc_ready = sem("rest_ready"), sem("mid_ready"), sem("rest2_ready"), sem("bc_ready")
        soft_step, soft_ready, delta_ready, dx_ready, y_init = (
            sem("soft_step"), sem("soft_ready"), sem("delta_ready"), sem("dx_ready"), sem("y_init"))
        b_filled, c_filled, decay_ready, u_ready, scanned, hc_ready, carried, added = (
            sem("b_filled"), sem("c_filled"), sem("decay_ready"), sem("u_ready"), sem("scanned"), sem("hc_ready"),
            sem("carried"), sem("added"))
        y_summed, y_ready, ss2_ready, ms2_ready, rstd2_ready, hn_ready, acc_init = (
            sem("y_summed"), sem("y_ready"), sem("ss2_ready"), sem("ms2_ready"), sem("rstd2_ready"), sem("hn_ready"),
            sem("acc_init"))
        top_ready, shifted_ready, expo_ready, route_step, mask_ready, weight_ready = (
            sem("top_ready"), sem("shifted_ready"), sem("expo_ready"), sem("route_step"), sem("mask_ready"),
            sem("weight_ready"))
        tiles_step, slot_f_ready, passed_ready, weight_step, expert_ready, slot_ready, cleared, slots_zero = (
            sem("tiles_step"), sem("slot_f_ready"), sem("passed_ready"), sem("weight_step"), sem("expert_ready"), sem("slot_ready"), sem("cleared"), sem("slots_zero"))
        scattered, gathered, combined = sem("scattered"), sem("gathered"), sem("combined")
        tile_loaded = [sem(f"tile_loaded{b}") for b in range(NB)]
        tile_stored = [sem(f"tile_stored{b}") for b in range(NB)]
        x_turned, xT_taken, y_filled, y_taken, gate_filled, up_filled, turned, turn_taken = (
            sem("x_turned"), sem("xT_taken"), sem("y_filled"), sem("y_taken"), sem("gate_filled"), sem("up_filled"), sem("turned"),
            sem("turn_taken"))
        th_gate_ready, silu_ready, hid_ready = sem("th_gate_ready"), sem("silu_ready"), sem("hid_ready")
        stats_ready, mv_ready, var_ready, rstd_ready, x1_ready, h_act = (
            sem("stats_ready"), sem("mv_ready"), sem("var_ready"), sem("rstd_ready"), sem("x1_ready"), sem("h_act"))
        stats2_ready, mv2_ready, var2_ready, rstd_b_ready, y_out_ready = (
            sem("stats2_ready"), sem("mv2_ready"), sem("var2_ready"), sem("rstd_b_ready"), sem("y_out_ready"))

        block = ctx.enter_context(nc.Block())

        def chunk_rows(dram, s, stage):
            tiles = dram[s.parity(stage), :, :].rearrange("(t j p) d -> t p j d", j=NJ, p=P)
            return tiles[s.time(stage), :, :, :]

        def tile_at(g, offset):
            i, odd = divmod(g - LAG - offset, 2)
            return i if not odd and 0 <= i < NT else None

        def additions(n):
            return 1 if n < 2 else n

        N_MAMBA, N_EXPERT, N_FFN = 13, 3, 6

        @block.sync
        def _(sp):
            def load_x(s):
                q = s.parity("A")
                wait(sp, acc_init, s.count("A", 1, -1))
                sp.dma_start(x[q][:, :, :], chunk_rows(hidden, s, "A")).then_inc(x_loaded[q], 16)

            load_x(Step(-1))
            sp.dma_start(w_in[:, :], in_proj_w).then_inc(mamba_weights, 16)
            sp.dma_start(w_rms1[:, :], rms1_w.rearrange("(p a) -> p a", a=1)).then_inc(mamba_weights, 16)
            sp.dma_start(w_conv[:, :, :], conv_w.rearrange("(h p) a k -> p h (a k)", p=P)).then_inc(mamba_weights, 16)
            sp.dma_start(b_conv[:, :], conv_b.rearrange("(h p) -> p h", p=P)).then_inc(mamba_weights, 16)
            sp.dma_start(w_x[:, :, :], x_proj_w.rearrange("(h p) n -> p h n", p=P)).then_inc(mamba_weights, 16)
            sp.dma_start(w_dt[:, :], dt_proj_w).then_inc(mamba_weights, 16)
            sp.dma_start(b_dt[:, :], dt_proj_b.rearrange("(h p) -> p h", p=P)).then_inc(mamba_weights, 16)
            sp.dma_start(a_neg[:, :, :], A_log.rearrange("(h p) n -> p h n", p=P)).then_inc(mamba_weights, 16)
            sp.dma_start(d_skip[:, :], D_skip.rearrange("(h p) -> p h", p=P)).then_inc(mamba_weights, 16)
            sp.dma_start(w_out[:, :, :], out_proj_w.rearrange("(h p) n -> p h n", p=P)).then_inc(mamba_weights, 16)
            sp.dma_start(w_router[:, :], router_w).then_inc(mamba_weights, 16)
            sp.dma_start(w_rms2[:, :], rms2_w.rearrange("(p a) -> p a", a=1)).then_inc(mamba_weights, 16)
            sp.dma_start(w_v2[RANK:RANK + 1, :], b2.rearrange("(a n) -> a n", a=1)).then_inc(mamba_weights, 16)
            sp.dma_start(w_gate[:, :, :], Wg.rearrange("e p n -> p e n")).then_inc(expert_weights, 16)
            sp.dma_start(w_up[:, :, :], Wu.rearrange("e p n -> p e n")).then_inc(expert_weights, 16)
            sp.dma_start(w_down[:, :, :, :], Wd.rearrange("e (q p) n -> p e q n", p=P)).then_inc(expert_weights, 16)
            sp.dma_start(w_u1[:, :], U1).then_inc(ffn_weights, 16)
            sp.dma_start(w_v1[:, :], V1).then_inc(ffn_weights, 16)
            sp.dma_start(b_v1[:, :], b1.rearrange("(q p) -> p q", p=P)).then_inc(ffn_weights, 16)
            sp.dma_start(w_u2[:, :, :], U2.rearrange("(q p) r -> p q r", p=P)).then_inc(ffn_weights, 16)
            sp.dma_start(w_v2[0:RANK, :], V2).then_inc(ffn_weights, 16)

            sp.wait_ge(slots_zero, 1)
            for q in range(2):
                sp.dma_start(xs_dram[q].rearrange("(i p) d -> p i d", p=P),
                             h[:, :, :, :].rearrange("p a b t -> p (a b t)")[:, 0:NT * D]
                             .rearrange("p (i d) -> p i d", i=NT)).then_inc(cleared, 16)

            def iteration(s):
                for k in range(UNITS):
                    if s.has("A") and s.i0 >= 0 and k == WHEN["A_load"]:
                        load_x(s)
                    if s.has("F") and k == WHEN["F_norm"] + 1:
                        sp.wait_ge(y_out_ready, s.count("F", NJ, NJ))
                        sp.dma_start(chunk_rows(out, s, "F"), y_out[:, :, :]).then_inc(stored, 16)
                    for stage, g in (("tail", k + UNITS), ("D", k)):
                        if not s.has(stage):
                            continue
                        q = s.parity(stage)
                        i = tile_at(g, -4)
                        if i is not None:
                            if i == 0:
                                sp.wait_ge(scattered, s.count(stage, 16 * TOPK * NJ, 16 * TOPK * NJ))
                            if i >= NB:
                                sp.wait_ge(x_turned, s.count(stage, NT, i - NB + 1))
                            sp.dma_start(xs[:, i % NB, :], xs_dram[q][i * P:(i + 1) * P, :]).then_inc(tile_loaded[i % NB], 16)
                        i = tile_at(g, 3)
                        if i is not None:
                            sp.wait_ge(y_taken, s.count(stage, NT, i + 1))
                            sp.dma_start(ys_dram[q][i * P:(i + 1) * P, :], ys[:, i % NB, :]).then_inc(tile_stored[i % NB], 16)

            run_pipeline(sp, iteration)
            sp.wait_ge(stored, 16 * NC)

        @block.gpsimd
        def _(pool):
            pool.memset(ident[:, :], 0.0).then_inc(sel_made, 1)
            pool.memset(pick[:, :], 0.0).then_inc(sel_made, 1)
            pool.memset(before[:, :, :], 1.0).then_inc(sel_made, 1)
            for tile, value in ((power, -0.5), (per_d, 1.0 / D), (one, 1.0), (eps, EPS)):
                pool.memset(tile[:, :], value).then_inc(const_made, 1)
            pool.memset(all_ones[:, :], 1.0).then_inc(const_made, 1)
            pool.memset(earlier[:, :], 1.0).then_inc(sel_made, 1)
            pool.iota(whole[:, :], pattern=[[P, NJ]], base=0, channel_multiplier=0,
                      allow_small_or_imprecise_dtypes=True).then_inc(const_made, 1)
            pool.iota(tile_no[:, :], pattern=[[1, NT]], base=0, channel_multiplier=0,
                      allow_small_or_imprecise_dtypes=True).then_inc(const_made, 1)
            for q in range(2):
                pool.memset(carry[q][:, :, :], 0.0).then_inc(const_made, 1)
                pool.memset(halo[q][:, :, :], 0.0).then_inc(const_made, 1)
            pool.wait_ge(sel_made, 4)
            pool.affine_select(out=ident[:, :], in_=ident[:, :], compare_op=ALU.not_equal, fill=1.0, base=0,
                               pattern=[[-1, P]], channel_multiplier=1).then_inc(const_made, 1)
            pool.affine_select(out=before[:, :, :], in_=before[:, :, :], compare_op=ALU.is_gt, fill=0.0, base=0,
                               pattern=[[1, NE], [-1, NE]], channel_multiplier=0).then_inc(const_made, 1)
            pool.affine_select(out=earlier[:, :], in_=earlier[:, :], compare_op=ALU.is_gt, fill=0.0, base=0,
                               pattern=[[1, P]], channel_multiplier=-1).then_inc(const_made, 1)
            for term in range(3):
                pool.affine_select(out=pick[:, :], in_=pick[:, :], compare_op=ALU.not_equal, fill=1.0,
                                   base=-2 * NS * term, pattern=[[-1, 2 * NS]],
                                   channel_multiplier=1).then_inc(sel_made, 1)
                pool.wait_ge(sel_made, 5 + term)

            def rstd_of(value, mean_sq, made, result, ready, s, stage, scale):
                pool.tensor_tensor(out=mean_sq[:, :], in0=value, in1=scale[:, :], op=ALU.mult).then_inc(made, 1)
                pool.wait_ge(made, s.count(stage, 2, 1))
                pool.tensor_tensor(out=mean_sq[:, :], in0=mean_sq[:, :], in1=eps[:, :], op=ALU.add).then_inc(made, 1)
                pool.wait_ge(made, s.count(stage, 2, 2))
                pool.tensor_tensor(out=result[:, :], in0=mean_sq[:, :], in1=power[:, :], op=ALU.pow).then_inc(ready, 1)

            def normalize(s, stage, src, mean_var, rs, rs_ready, dst, middle, done):
                pool.tensor_tensor(out=dst[:, :, :], in0=src[:, :, :], in1=mean_var[:, :, 0:1].to_broadcast([P, NJ, D]),
                                   op=ALU.subtract).then_inc(middle, 1)
                pool.wait_ge(middle, s.count(stage, 1, 1))
                pool.wait_ge(rs_ready, s.count(stage, 1, 1))
                pool.tensor_tensor(out=dst[:, :, :], in0=dst[:, :, :], in1=rs[:, :].unsqueeze(2).to_broadcast([P, NJ, D]),
                                   op=ALU.mult).then_inc(done, NJ)

            def iteration(s):
                for k in range(UNITS):
                    if s.has("C") and k == WHEN["C_last"]:
                        add_state(s, "C", NS - 1)
                        q = s.parity("C")
                        pool.wait_ge(added, s.count("C", ADDS, ADDS))
                        pool.tensor_tensor(out=y_even[q][:, :, :], in0=y_even[q][:, :, :], in1=y_odd[:, :, :],
                                           op=ALU.add).then_inc(y_summed, 1)
                    if s.has("C") and k == WHEN["C_scatter"]:
                        pool.wait_ge(slot_ready, s.count("C", 1, 1))
                        if s.chunk("C") == 0:
                            pool.wait_ge(cleared, 16 * 2)
                        wait(pool, x_turned, s.count("C", NT, -NT))
                    if s.has("E") and k == WHEN["E_gather"]:
                        for b in range(NB):
                            pool.wait_ge(tile_stored[b], s.count("E", 16 * NT // NB, 16 * NT // NB))
                        wait(pool, combined, s.count("E", TOPK * NJ, 0))
                    if s.has("B") and k % 2 == 0 and k > 0 and k // 2 - 1 != 1:
                        add_state(s, "B", k // 2 - 1)
                    if s.has("C") and k == WHEN["C_norm"]:
                        q = s.parity("C")
                        pool.wait_ge(ss2_ready, s.count("C", NJ, NJ))
                        rstd_of(ss2[:, :], ms2, ms2_ready, rstd2, rstd2_ready, s, "C", per_d)
                        pool.wait_ge(rstd2_ready, s.count("C", 1, 1))
                        pool.wait_ge(misc_taken, s.misc("C_out") + 1)
                        wait(pool, scattered, s.count("C", 16 * TOPK * NJ, 0))
                        pool.tensor_tensor(out=hn[:, :, :], in0=res[:, :, :],
                                           in1=rstd2[:, :].unsqueeze(2).to_broadcast([P, NJ, D]),
                                           op=ALU.mult).then_inc(hn_ready, 1)
                    if s.has("C") and k == WHEN["C_norm"] + 1:
                        q = s.parity("C")
                        wait(pool, x1_ready, s.count("C", NJ, -NJ))
                        pool.tensor_tensor(out=acc[q][:, :, :], in0=res[:, :, :], in1=x[q][:, :, :],
                                           op=ALU.add).then_inc(acc_init, 1)
                    if s.has("C") and 0 <= k - WHEN["C_scatter"] < NJ:
                        q, j = s.parity("C"), k - WHEN["C_scatter"]
                        for c in range(TOPK):
                            pool.indirect_dma_start(
                                xs_dram[q], bass.IndirectOffsetOnAxis(ap=slot[q][:, c, j:j + 1], axis=0),
                                hn[:, j, :], None).then_inc(scattered, 16)
                    if s.has("E") and 0 <= k - WHEN["E_gather"] < NJ:
                        q, j = s.parity("E"), k - WHEN["E_gather"]
                        for c in range(TOPK):
                            pool.indirect_dma_start(
                                y_sel[:, c, j, :], None, ys_dram[q],
                                bass.IndirectOffsetOnAxis(ap=slot[q][:, c, j:j + 1], axis=0)).then_inc(gathered, 16)
                    if s.has("E") and k == WHEN["E_combine"] + 1:
                        pool.wait_ge(mv_ready, s.count("E", NJ, NJ))
                        rstd_of(mv[:, :, 1], var, var_ready, rstd, rstd_ready, s, "E", one)
                        normalize(s, "E", acc[s.parity("E")], mv, rstd, rstd_ready, x1, centred, x1_ready)
                    if s.has("A") and k == WHEN["A_norm"]:
                        pool.wait_ge(ss1_ready, s.count("A", NJ, NJ))
                        rstd_of(ss1[:, :], ms1, ms1_ready, rstd1, rstd1_ready, s, "A", per_d)
                        pool.wait_ge(rstd1_ready, s.count("A", 1, 1))
                        q = s.parity("A")
                        pool.tensor_tensor(out=xn[:, :, :], in0=x[q][:, :, :],
                                           in1=rstd1[:, :].unsqueeze(2).to_broadcast([P, NJ, D]),
                                           op=ALU.mult).then_inc(xn_ready, 1)
                    if s.has("F") and k == TAKE["F_out"] + 1:
                        pool.wait_ge(mv2_ready, s.count("F", NJ, NJ))
                        rstd_of(mv2[:, :, 1], var2, var2_ready, rstd_b, rstd_b_ready, s, "F", one)
                        normalize(s, "F", y_out, mv2, rstd_b, rstd_b_ready, y_out, centred2, y_out_ready)
                    if s.has("A") and k == WHEN["A_gate"]:
                        q = s.parity("A")
                        pool.wait_ge(th_one_ready, s.count("A", 1, 1))
                        pool.tensor_tensor(out=gate_z[q][:, :, :], in0=th_z[:, :, :], in1=gate_z[q][:, :, :],
                                           op=ALU.mult).then_inc(gate_z_ready, 1)
                    if s.has("A") and k == WHEN["A_dx"]:
                        q = s.parity("A")
                        pool.wait_ge(delta_ready, s.count("A", 1, 1))
                        pool.tensor_tensor(out=dx[q][:, :, :], in0=delta[q][:, :, :], in1=act_x[:, :, :],
                                           op=ALU.mult).then_inc(dx_ready, 1)

            def add_state(s, stage, n):
                q = s.parity(stage)
                y = (y_even[q], y_odd)[n % 2]
                if n == 0:
                    pool.wait_ge(y_init, s.count(stage, NH, NH))
                pool.wait_ge(hc_ready, s.count(stage, NS, n + 1))
                if n >= 2:
                    pool.wait_ge(added, s.count(stage, ADDS, additions(n - 2)))
                pool.tensor_tensor(out=y[:, :, :], in0=y[:, :, :], in1=hc[:, n % 2, :, :],
                                   op=ALU.add).then_inc(added, 1)

            pool.wait_ge(mamba_weights, 16 * N_MAMBA)
            run_pipeline(pool, iteration)

        @block.scalar
        def _(act):
            act.wait_ge(mamba_weights, 16 * N_MAMBA)
            act.activation(a_neg[:, :, :], a_neg[:, :, :], ACT.Exp).then_inc(a_exp, 1)
            act.wait_ge(prepared, 1)

            def take(name, s, out_ap, in_ap, **kw):
                act.wait_ge(misc_filled, s.misc(name) + 1)
                act.activation(out_ap, in_ap, kw.pop("func", ACT.Copy), **kw).then_inc(misc_taken, 1)

            def squares(s, stage, src, scratch, dst, ready):
                for j in range(NJ):
                    act.activation(scratch[:, j, :], src[:, j, :], ACT.Square, accum_out=dst[:, j:j + 1]).then_inc(ready, 1)

            def decays(s, stage, n):
                q = s.parity(stage)
                for half in range(NH):
                    if n == 0 and half == 0:
                        act.wait_ge(delta_ready, s.count(stage, 1, 1))
                    wait(act, scanned, s.count(stage, NS * NH, (n - ND) * NH + half + 1))
                    act.activation(decay[:, n % ND, half, :], delta[q][:, half, :], ACT.Exp,
                                   scale=a_neg[:, half, n:n + 1]).then_inc(decay_ready, 1)

            def tile_input(s, stage, g):
                i = tile_at(g, -1)
                if i is not None:
                    wait(act, up_filled, s.count(stage, NT, i - 1))
                    act.wait_ge(x_turned, s.count(stage, NT, i + 1))
                    act.activation(xsT[:, i % 2, :], x_bank[:, 0:P], ACT.Copy).then_inc(xT_taken, 1)

            def tile_output(s, stage, g):
                i = tile_at(g, 3)
                if i is not None:
                    wait(act, tile_stored[i % NB], s.count(stage, 16 * NT // NB, 16 * (i // NB)))
                    act.wait_ge(y_filled, s.count(stage, NT, i + 1))
                    act.activation(ys[:, i % NB, :], y_bank[:, 0:D], ACT.Copy).then_inc(y_taken, 1)

            def tile_middle(s, stage, g):
                i = tile_at(g, 0)
                if i is not None:
                    wait(act, hid_ready, s.count(stage, NT, i - 1))
                    act.wait_ge(gate_filled, s.count(stage, NT, i + 1))
                    act.activation(th_gate[:, i % 2, :], g_bank[:, :], ACT.Tanh, scale=0.5).then_inc(th_gate_ready, 1)
                i = tile_at(g, 2)
                if i is not None:
                    if i >= 2:
                        act.wait_ge(y_filled, s.count(stage, NT, i - 1))
                    act.wait_ge(turned, s.count(stage, NT, i + 1))
                    act.activation(hidT[:, i % 2, :, :].rearrange("p q t -> p (q t)"), turn_bank[:, :],
                                   ACT.Copy).then_inc(turn_taken, 1)
            def stage_c(s, k):
                if k == TAKE["C_T"]:
                    take("C_T", s, hT[:, :], misc[:, :])
                if k == TAKE["C_router"]:
                    wait(act, weight_ready, s.count("C", 1, 0))
                    take("C_router", s, logits[:, :, :], misc[:, 0:NJ * NE].rearrange("p (j e) -> p j e", j=NJ))
                if k == TAKE["C_rank"]:
                    wait(act, slot_ready, s.count("C", 1, 0))
                    take("C_rank", s, place[:, :, :], misc[:, 0:(NJ + 1) * NE].rearrange("p (j e) -> p j e", j=NJ + 1))

            def stage_f(s, k):
                if k == TAKE["F_T"]:
                    take("F_T", s, x1T[:, :], misc[:, :])
                if k == TAKE["F_P"]:
                    take("F_P", s, p_ffn[:, :], misc[0:RANK, :])
                for f in range(NQ):
                    if k == TAKE[f"F_H{f}"]:
                        take(f"F_H{f}", s, h_ffn[:, f, :], misc[:, :], func=ACT.Identity, bias=b_v1[:, f:f + 1])
                if k == TAKE["F_Q"]:
                    take("F_Q", s, q_ffn[0:RANK, :], misc[0:RANK, :])

            def stage_a(s, k):
                q = s.parity("A")
                if k == TAKE["A_T"]:
                    take("A_T", s, xnT[:, :], misc[:, :])
                for half in range(NH):
                    if k == TAKE[f"A_xi{half}"]:
                        wait(act, tap_done, s.count("A", NH * 3, 0))
                        wait(act, halo_saved, s.count("A", 1, 0))
                        if half == 0:
                            act.activation(xi[:, :, 0:NTAP - 1], halo[q][:, :, :], ACT.Copy).then_inc(halo_ready, 1)
                        take(f"A_xi{half}", s, xi[:, half, NTAP - 1:], misc[:, :])
                        act.wait_ge(misc_taken, s.misc(f"A_xi{half}") + 1)
                        act.wait_ge(halo_ready, s.count("A", 1, 1))
                        wait(act, act_x_ready, s.count("A", NH, half + 1 - NH))
                        act.activation(conv[:, half, :], xi[:, half, 0:T], ACT.Identity, scale=w_conv[:, half, 0:1],
                                       bias=b_conv[:, half:half + 1]).then_inc(tap0_ready, 1)
                        if half == NH - 1:
                            act.activation(halo[q][:, :, :], xi[:, :, T:], ACT.Copy).then_inc(halo_saved, 1)
                    if k == TAKE[f"A_z{half}"]:
                        wait(act, y_ready, s.count("A", 1, -1))
                        take(f"A_z{half}", s, gate_z[q][:, half, :], misc[:, :])
                        act.wait_ge(misc_taken, s.misc(f"A_z{half}") + 1)
                        wait(act, rest2_ready, s.count("A", 1, 0))
                        act.activation(th_z[:, half, :], gate_z[q][:, half, :], ACT.Tanh, scale=0.5).then_inc(th_z_ready, 1)
                    if k == WHEN["A_tanh"]:
                        act.wait_ge(tap_done, s.count("A", NH * 3, NH * 2 + half + 1))
                        act.activation(th_conv[:, half, :], conv[:, half, :], ACT.Tanh, scale=0.5).then_inc(th_conv_ready, 1)
                    if k == TAKE[f"A_dd{half}"]:
                        take(f"A_dd{half}", s, dt_raw[:, half, :], misc[:, :], func=ACT.Identity,
                             bias=b_dt[:, half:half + 1])
                if k == TAKE["A_dt"]:
                    take("A_dt", s, dt_in[:, :], misc[0:R, :])
                if k == TAKE["A_BC"]:
                    act.wait_ge(gate_z_ready, s.count("A", 1, 1))
                    take("A_BC", s, bc_full, misc[0:3 * 2 * NS, :])
                    act.wait_ge(misc_taken, s.misc("A_BC") + 1)
                    wait(act, c_filled, s.count("A", NS, -NS))
                    act.activation(bc[q][:, :], bc_full, ACT.Copy).then_inc(bc_ready, 1)
            def late_steps(s, k):
                if s.has("C"):
                    if k == WHEN["C_squares"]:
                        act.wait_ge(misc_taken, s.misc("C_out") + 1)
                        wait(act, rstd2_ready, s.count("C", 1, 0))
                        wait(act, scattered, s.count("C", 16 * TOPK * NJ, 0))
                        squares(s, "C", res, hn, ss2, ss2_ready)
                    if k == WHEN["C_expo"]:
                        act.wait_ge(shifted_ready, s.count("C", 1, 1))
                        act.activation(expo[:, :, :], shifted[:, :, :], ACT.Exp).then_inc(expo_ready, 1)
                if s.has("F"):
                    if k == WHEN["F_act"]:
                        act.wait_ge(misc_taken, s.misc("F_H3") + 1)
                        act.activation(h_ffn[:, :, :], h_ffn[:, :, :], ACT.Gelu_apprx_tanh).then_inc(h_act, 1)
                if s.has("A"):
                    q = s.parity("A")
                    if k == WHEN["A_squares"]:
                        act.wait_ge(x_loaded[q], 16 * (s.chunk("A") // 2 + 1) + 16 * s.j)
                        wait(act, ms1_ready, s.count("A", 2, 0))
                        squares(s, "A", x[q], tokens, ss1, ss1_ready)
                    if k == WHEN["A_one"]:
                        act.wait_ge(th_z_ready, s.count("A", NH, NH))
                        act.activation(th_z[:, :, :], th_z[:, :, :], ACT.Identity, bias=1.0).then_inc(th_one_ready, 1)
                    if k == WHEN["A_soft"]:
                        wait(act, delta_ready, s.count("A", 1, 0))
                        act.wait_ge(misc_taken, s.misc("A_dd1") + 1)
                        act.activation(dt_soft[:, :, :], dt_raw[:, :, :], ACT.Abs).then_inc(soft_step, 1)
                        act.wait_ge(soft_step, s.count("A", 2, 1))
                        act.activation(dt_soft[:, :, :], dt_soft[:, :, :], ACT.Exp, scale=-1.0).then_inc(soft_step, 1)
                    if k == WHEN["A_soft"] + 1:
                        act.wait_ge(soft_step, s.count("A", 2, 2))
                        act.activation(dt_soft[:, :, :], dt_soft[:, :, :], ACT.Ln, bias=1.0).then_inc(soft_ready, 1)
                    if k == WHEN["A_start"]:
                        act.wait_ge(act_x_ready, s.count("A", NH, NH))
                        for half in range(NH):
                            act.activation(y_even[q][:, half, :], act_x[:, half, :], ACT.Copy,
                                           scale=d_skip[:, half:half + 1]).then_inc(y_init, 1)

            def iteration(s):
                for k in range(UNITS):
                    for stage, g in (("tail", k + UNITS), ("D", k)):
                        if s.has(stage):
                            tile_input(s, stage, g)
                    if s.has("C"):
                        stage_c(s, k)
                    if s.has("F"):
                        stage_f(s, k)
                    if s.has("A"):
                        stage_a(s, k)
                    for stage, g in (("tail", k + UNITS), ("D", k)):
                        if s.has(stage):
                            tile_middle(s, stage, g)
                    n = k // 2 + 2
                    if k % 2 == 1 and s.has("B") and n < NS:
                        decays(s, "B", n)
                    if k % 2 == 1 and s.has("A") and n >= NS:
                        decays(s, "A", n - NS)
                    for stage, g in (("tail", k + UNITS), ("D", k)):
                        if s.has(stage):
                            tile_output(s, stage, g)
                    late_steps(s, k)

            run_pipeline(act, iteration)

        @block.tensor
        def _(pe):
            pe.wait_ge(const_made, 15)
            pe.wait_ge(sel_made, 7)
            pe.wait_ge(prepared, 1)

            def bank_free(name, s):
                wait(pe, misc_taken, s.misc(name))

            def transposes(name, s, src):
                bank_free(name, s)
                for j in range(NJ):
                    last = pe.transpose(misc_tok[:, j, :], src[:, j, :], ident[:, :])
                last.then_inc(misc_filled, 1)

            def spread(s, stage, n, row, dst, filled):
                pe.matmul(dst[:, :], pick[:, row:row + 1].to_broadcast([3 * 2 * NS, P]), bc[s.parity(stage)][:, :],
                          start=True, stop=True).then_inc(filled, 1)

            def spread_b(s, stage, n):
                if n == 0:
                    pe.wait_ge(bc_ready, s.count(stage, 5, 5))
                wait(pe, u_ready, s.count(stage, NS * NH, n * NH))
                spread(s, stage, n, n, b_bank, b_filled)

            def spread_c(s, stage, n):
                wait(pe, hc_ready, s.count(stage, NS, n))
                spread(s, stage, n, NS + n, c_bank, c_filled)

            def expert_of(s, stage, i, known):
                if (stage, i) not in known:
                    known[stage, i] = pe.value_load(tile_expert[s.parity(stage)][0:1, i:i + 1], min_val=0, max_val=NE - 1)
                return known[stage, i]

            def tile_first(s, stage, g, known):
                i = tile_at(g, -1)
                if i is not None:
                    if i == 0:
                        pe.wait_ge(expert_ready, s.count(stage, 1, 1))
                    pe.wait_ge(tile_loaded[i % NB], s.count(stage, 16 * NT // NB, 16 * (i // NB + 1)))
                    wait(pe, xT_taken, s.count(stage, NT, i))
                    pe.transpose(x_bank[:, 0:P], xs[:, i % NB, :], ident[:, :]).then_inc(x_turned, 1)
                    expert_of(s, stage, i, known)
                i = tile_at(g, 3)
                if i is not None:
                    e = expert_of(s, stage, i, known)
                    pe.wait_ge(turn_taken, s.count(stage, NT, i + 1))
                    wait(pe, y_taken, s.count(stage, NT, i))
                    for f in range(NQ):
                        last = pe.matmul(y_bank[:, 0:D], hidT[:, i % 2, f, :], w_down[:, bass.ds(e, 1), f, :],
                                         start=(f == 0), stop=(f == NQ - 1))
                    last.then_inc(y_filled, 1)
                i = tile_at(g, 0)
                if i is not None:
                    e = expert_of(s, stage, i, known)
                    if i == 0:
                        pe.wait_ge(gates_scaled, 2)
                    pe.wait_ge(xT_taken, s.count(stage, NT, i + 1))
                    wait(pe, silu_ready, s.count(stage, NT, i))
                    pe.matmul(g_bank[:, :], xsT[:, i % 2, :], w_gate[:, bass.ds(e, 1), :], start=True,
                              stop=True).then_inc(gate_filled, 1)

            def tile_second(s, stage, g, known):
                i = tile_at(g, 2)
                if i is not None:
                    pe.wait_ge(hid_ready, s.count(stage, NT, i + 1))
                    wait(pe, turn_taken, s.count(stage, NT, i))
                    for f in range(NQ):
                        last = pe.transpose(turn_bank[:, f * P:(f + 1) * P], hid[:, i % 2, f * P:(f + 1) * P], ident[:, :])
                    last.then_inc(turned, 1)
                i = tile_at(g, 0)
                if i is not None:
                    wait(pe, hid_ready, s.count(stage, NT, i))
                    e = expert_of(s, stage, i, known)
                    pe.matmul(up_bank[:, :], xsT[:, i % 2, :], w_up[:, bass.ds(e, 1), :], start=True,
                              stop=True).then_inc(up_filled, 1)

            def iteration(s):
                known = {}
                for k in range(UNITS):
                    for stage, g in (("tail", k + UNITS), ("D", k)):
                        if s.has(stage):
                            tile_first(s, stage, g, known)
                    if s.has("B"):
                        if k % 2 == 0:
                            spread_c(s, "B", k // 2)
                        elif k < UNITS - 1:
                            spread_b(s, "B", (k + 1) // 2)
                    if s.has("A") and k == UNITS - 1:
                        spread_b(s, "A", 0)
                    for stage, g in (("tail", k + UNITS), ("D", k)):
                        if s.has(stage):
                            tile_second(s, stage, g, known)
                    if s.has("C"):
                        q = s.parity("C")
                        if k == MISC["C_out"]:
                            bank_free("C_out", s)
                            pe.wait_ge(y_ready, s.count("C", 1, 1))
                            for j in range(NJ):
                                for half in range(NH):
                                    last = pe.matmul(misc_tok[:, j, :], y_even[q][:, half, j * P:(j + 1) * P],
                                                     w_out[:, half, :], start=(half == 0), stop=(half == NH - 1))
                            last.then_inc(misc_filled, 1)
                        if k == MISC["C_T"]:
                            pe.wait_ge(hn_ready, s.count("C", 1, 1))
                            transposes("C_T", s, hn)
                        if k == MISC["C_router"]:
                            bank_free("C_router", s)
                            for j in range(NJ):
                                last = pe.matmul(misc[:, j * NE:(j + 1) * NE], hT[:, j * P:(j + 1) * P],
                                                 w_router[:, :], start=True, stop=True)
                            last.then_inc(misc_filled, 1)
                        if k == MISC["C_rank"]:
                            bank_free("C_rank", s)
                            pe.wait_ge(mask_ready, s.count("C", 1, 1))
                            pe.matmul(misc[:, 0:NJ * NE], earlier[:, :], mask[:, :, :].rearrange("p j e -> p (j e)"),
                                      start=True, stop=False)
                            for j in range(NJ - 1):
                                pe.matmul(misc[:, (j + 1) * NE:NJ * NE].rearrange("p (j e) -> p j e", e=NE), all_ones[:, :],
                                          mask[:, j, :].unsqueeze(1).to_broadcast([P, NJ - 1 - j, NE]),
                                          start=False, stop=(j == NJ - 2))
                            for j in range(NJ):
                                last = pe.matmul(misc[:, NJ * NE:(NJ + 1) * NE], all_ones[:, :], mask[:, j, :],
                                                 start=(j == 0), stop=(j == NJ - 1))
                            last.then_inc(misc_filled, 1)
                    if s.has("F"):
                        if k == MISC["F_T"]:
                            pe.wait_ge(x1_ready, s.count("F", NJ, NJ))
                            pe.wait_ge(ffn_weights, 16 * 5)
                            transposes("F_T", s, x1)
                        if k == MISC["F_P"]:
                            bank_free("F_P", s)
                            pe.matmul(misc[0:RANK, :], w_u1[:, :], x1T[:, :], start=True, stop=True).then_inc(misc_filled, 1)
                        for f in range(NQ):
                            if k == MISC[f"F_H{f}"]:
                                bank_free(f"F_H{f}", s)
                                pe.matmul(misc[:, :], w_v1[:, f * P:(f + 1) * P], p_ffn[:, :], start=True,
                                          stop=True).then_inc(misc_filled, 1)
                        if k == MISC["F_Q"]:
                            bank_free("F_Q", s)
                            pe.wait_ge(h_act, s.count("F", 1, 1))
                            for f in range(NQ):
                                last = pe.matmul(misc[0:RANK, :], w_u2[:, f, :], h_ffn[:, f, :], start=(f == 0),
                                                 stop=(f == NQ - 1))
                            last.then_inc(misc_filled, 1)
                    if s.has("F") and k == MISC["F_out"]:
                        bank_free("F_out", s)
                        for j in range(NJ):
                            last = pe.matmul(misc_tok[:, j, :], q_ffn[:, j * P:(j + 1) * P], w_v2[:, :],
                                             start=True, stop=True)
                        last.then_inc(misc_filled, 1)
                    if s.has("A"):
                        q = s.parity("A")
                        if k == MISC["A_T"]:
                            pe.wait_ge(xn_ready, s.count("A", 1, 1))
                            transposes("A_T", s, xn)
                        for part, name in enumerate(("A_xi0", "A_xi1", "A_z0", "A_z1")):
                            if k == MISC[name]:
                                bank_free(name, s)
                                pe.matmul(misc[:, :], w_in[:, part * P:(part + 1) * P], xnT[:, :], start=True,
                                          stop=True).then_inc(misc_filled, 1)
                        if k == MISC["A_dt"]:
                            bank_free("A_dt", s)
                            pe.wait_ge(act_x_ready, s.count("A", NH, NH))
                            for half in range(NH):
                                last = pe.matmul(misc[0:R, :], w_x[:, half, 0:R], act_x[:, half, :],
                                                 start=(half == 0), stop=(half == NH - 1))
                            last.then_inc(misc_filled, 1)
                        if k == MISC["A_BC"]:
                            bank_free("A_BC", s)
                            for half in range(NH):
                                last = pe.matmul(misc[0:3 * 2 * NS, :], w_bc[:, half, :, :], act_x[:, half, :],
                                                 start=(half == 0), stop=(half == NH - 1))
                            last.then_inc(misc_filled, 1)
                        for half in range(NH):
                            if k == MISC[f"A_dd{half}"]:
                                bank_free(f"A_dd{half}", s)
                                pe.matmul(misc[:, :], w_dt[:, half * P:(half + 1) * P], dt_in[:, :], start=True,
                                          stop=True).then_inc(misc_filled, 1)


            run_pipeline(pe, iteration)

        @block.vector
        def _(dve):
            dve.memset(q_ffn[RANK:RANK + 1, :], 1.0).then_inc(const_made, 1)
            dve.memset(h[:, :, :, :], 0.0).then_inc(slots_zero, 1)
            dve.wait_ge(mamba_weights, 16 * N_MAMBA)
            dve.wait_ge(a_exp, 1)
            dve.tensor_scalar(out=a_neg[:, :, :], in0=a_neg[:, :, :], scalar1=-1.0, scalar2=None, op0=ALU.mult)
            dve.tensor_scalar(out=w_in[:, :], in0=w_in[:, :], scalar1=w_rms1[:, 0:1], scalar2=None, op0=ALU.mult)
            dve.tensor_scalar(out=w_router[:, :], in0=w_router[:, :], scalar1=w_rms2[:, 0:1], scalar2=None, op0=ALU.mult)
            for term in range(3):
                dve.tensor_scalar(out=w_bc[:, :, term, :], in0=w_x[:, :, R:], scalar1=0.5, scalar2=None, op0=ALU.mult)
            dve.tensor_scalar(out=w_x[:, :, 0:R], in0=w_x[:, :, 0:R], scalar1=0.5, scalar2=None, op0=ALU.mult)
            dve.tensor_scalar(out=w_out[:, :, :], in0=w_out[:, :, :], scalar1=0.25, scalar2=None,
                              op0=ALU.mult).then_inc(prepared, 1)
            dve.wait_ge(const_made, 15)

            def multiply_b(s, n):
                q = s.parity("B")
                if n == 0:
                    dve.wait_ge(dx_ready, s.count("B", 1, 1))
                    if s.chunk("B") == 0:
                        dve.wait_ge(cleared, 16 * 2)
                dve.wait_ge(b_filled, s.count("B", NS, n + 1))
                for half in range(NH):
                    dve.tensor_tensor(out=u[:, half, :], in0=dx[q][:, half, :], in1=b_bank[:, :],
                                      op=ALU.mult).then_inc(u_ready, 1)

            def scan(s, n):
                q = s.parity("B")
                for half in range(NH):
                    dve.wait_ge(decay_ready, s.count("B", NS * NH, n * NH + half + 1))
                    dve.wait_ge(u_ready, s.count("B", NS * NH, n * NH + half + 1))
                    if half == 0 and s.chunk("B") >= 2:
                        dve.wait_ge(carried, s.count("B", NS, n + 1 - 2 * NS))
                    dve.tensor_tensor_scan(out=h[:, n % 2, half, :], data0=decay[:, n % ND, half, :], data1=u[:, half, :],
                                           initial=carry[q][:, n, half:half + 1], op0=ALU.mult,
                                           op1=ALU.add).then_inc(scanned, 1)

            def multiply_c(s, stage, n):
                q = s.parity(stage)
                dve.wait_ge(scanned, s.count(stage, NS * NH, (n + 1) * NH))
                dve.wait_ge(c_filled, s.count(stage, NS, n + 1))
                if n >= 2:
                    dve.wait_ge(added, s.count(stage, ADDS, additions(n - 2)))
                else:
                    wait(dve, added, s.count(stage, ADDS, n - 1))
                if n == 1:
                    wait(dve, y_summed, s.count(stage, 1, 0))
                dst = y_odd[:, :, :] if n == 1 else hc[:, n % 2, :, :]
                dve.tensor_tensor(out=dst, in0=h[:, n % 2, :, :],
                                  in1=c_bank[:, :].unsqueeze(1).to_broadcast([P, NH, T]),
                                  op=ALU.mult).then_inc(hc_ready, 1)
                dve.tensor_copy(carry[q][:, n, :], h[:, n % 2, :, T - 1]).then_inc(carried, 1)

            def tile_silu(s, stage, g):
                i = tile_at(g, 1)
                if i is not None:
                    dve.wait_ge(th_gate_ready, s.count(stage, NT, i + 1))
                    dve.scalar_tensor_tensor(out=th_gate[:, i % 2, :], in0=th_gate[:, i % 2, :], scalar=1.0,
                                             in1=g_bank[:, :], op0=ALU.add, op1=ALU.mult).then_inc(silu_ready, 1)

            def tile_hidden(s, stage, g):
                i = tile_at(g, 1)
                if i is not None:
                    dve.wait_ge(up_filled, s.count(stage, NT, i + 1))
                    dve.wait_ge(silu_ready, s.count(stage, NT, i + 1))
                    wait(dve, turned, s.count(stage, NT, i - 1))
                    dve.tensor_tensor(out=hid[:, i % 2, :], in0=th_gate[:, i % 2, :], in1=up_bank[:, :],
                                      op=ALU.mult).then_inc(hid_ready, 1)

            def combine(s):
                q = s.parity("E")
                dve.wait_ge(gathered, s.count("E", 16 * TOPK * NJ, 16 * TOPK * NJ))
                dve.wait_ge(acc_init, s.count("E", 1, 1))
                for c in range(TOPK):
                    if c > 0:
                        dve.wait_ge(combined, s.count("E", TOPK * NJ, c * NJ))
                    for j in range(NJ):
                        dve.scalar_tensor_tensor(out=acc[q][:, j, :], in0=y_sel[:, c, j, :], scalar=weight[q][:, c, j:j + 1],
                                                 in1=acc[q][:, j, :], op0=ALU.mult, op1=ALU.add).then_inc(combined, 1)

            def layer_norm_stats(src, st, st_ready):
                for j in range(NJ):
                    dve.bn_stats(out=st[:, j, :], in_=src[:, j, :]).then_inc(st_ready, 1)

            def layer_norm_aggregate(st, mean_var, mv_done):
                for j in range(NJ):
                    dve.bn_aggr(out=mean_var[:, j, :], in_=st[:, j, :]).then_inc(mv_done, 1)

            def route(s):
                q = s.parity("C")
                dve.wait_ge(misc_taken, s.misc("C_router") + 1)
                dve.tensor_reduce(out=top[:, :], in_=logits[:, :, :], axis=AX.X, op=ALU.max).then_inc(top_ready, 1)
                mine = logits[:, :, :].unsqueeze(3).to_broadcast([P, NJ, NE, NE])
                other = logits[:, :, :].unsqueeze(2).to_broadcast([P, NJ, NE, NE])
                flat = lambda a: a[:, :, :, :].rearrange("p j e f -> p j (e f)")
                tie_order = before[:, :, :].rearrange("p e f -> p (e f)").unsqueeze(1).to_broadcast([P, NJ, NE * NE])
                dve.tensor_tensor(out=ties[:, :, :, :], in0=other, in1=mine, op=ALU.is_equal).then_inc(route_step, 1)
                dve.tensor_tensor(out=beats[:, :, :, :], in0=other, in1=mine, op=ALU.is_gt).then_inc(route_step, 1)
                dve.wait_ge(top_ready, s.count("C", 1, 1))
                dve.tensor_tensor(out=shifted[:, :, :], in0=logits[:, :, :],
                                  in1=top[:, :].unsqueeze(2).to_broadcast([P, NJ, NE]),
                                  op=ALU.subtract).then_inc(shifted_ready, 1)
                dve.wait_ge(route_step, s.count("C", 5, 2))
                dve.tensor_tensor(out=flat(ties), in0=flat(ties), in1=tie_order, op=ALU.mult).then_inc(route_step, 1)
                dve.wait_ge(route_step, s.count("C", 5, 3))
                dve.tensor_tensor(out=flat(beats), in0=flat(beats), in1=flat(ties), op=ALU.add).then_inc(route_step, 1)
                dve.wait_ge(route_step, s.count("C", 5, 4))
                dve.tensor_reduce(out=rank[:, :, :], in_=beats[:, :, :, :], axis=AX.X, op=ALU.add).then_inc(route_step, 1)
                dve.wait_ge(route_step, s.count("C", 5, 5))
                dve.tensor_scalar(out=mask[:, :, :], in0=rank[:, :, :], scalar1=1.5, scalar2=None,
                                  op0=ALU.is_lt).then_inc(mask_ready, 1)

            def choose(s):
                for c in range(TOPK):
                    dve.tensor_scalar(out=choice[:, c, :, :], in0=rank[:, :, :], scalar1=float(c), scalar2=None,
                                      op0=ALU.is_equal).then_inc(weight_step, 1)

            def weigh(s):
                q = s.parity("C")
                dve.wait_ge(expo_ready, s.count("C", 1, 1))
                dve.tensor_reduce(out=denom[:, :], in_=expo[:, :, :], axis=AX.X, op=ALU.add).then_inc(weight_step, 1)
                dve.wait_ge(weight_step, s.count("C", 6, 2))
                dve.tensor_tensor(out=chosen[:, :, :, :], in0=choice[:, :, :, :],
                                  in1=expo[:, :, :].unsqueeze(1).to_broadcast([P, TOPK, NJ, NE]),
                                  op=ALU.mult).then_inc(weight_step, 1)
                dve.wait_ge(weight_step, s.count("C", 6, 3))
                dve.reciprocal(rdenom[:, :], denom[:, :]).then_inc(weight_step, 1)
                dve.wait_ge(weight_step, s.count("C", 6, 4))
                dve.tensor_reduce(out=chosen_w[:, :, :], in_=chosen[:, :, :, :], axis=AX.X, op=ALU.add).then_inc(weight_step, 1)
                dve.wait_ge(weight_step, s.count("C", 6, 6))
                dve.tensor_tensor(out=weight[q][:, :, :], in0=chosen_w[:, :, :],
                                  in1=rdenom[:, :].unsqueeze(1).to_broadcast([P, TOPK, NJ]),
                                  op=ALU.mult).then_inc(weight_ready, 1)

            def slots(s):
                q = s.parity("C")

                def step(n):
                    dve.wait_ge(tiles_step, s.count("C", 8, n))

                dve.wait_ge(misc_taken, s.misc("C_rank") + 1)
                dve.tensor_tensor(out=over[:, :, :], in0=place[:, NJ, :].unsqueeze(2).to_broadcast([P, NE, NJ]),
                                  in1=whole[:, :].unsqueeze(1).to_broadcast([P, NE, NJ]), op=ALU.is_gt).then_inc(tiles_step, 1)
                step(1)
                dve.tensor_reduce(out=tiles[:, :], in_=over[:, :, :], axis=AX.X, op=ALU.add).then_inc(tiles_step, 1)
                step(2)
                dve.tensor_tensor(out=tiles_b[:, :, :], in0=tiles[:, :].unsqueeze(1).to_broadcast([P, NE, NE]),
                                  in1=before[:, :, :], op=ALU.mult).then_inc(tiles_step, 1)
                step(3)
                dve.tensor_reduce(out=first_tile[:, :], in_=tiles_b[:, :, :], axis=AX.X, op=ALU.add).then_inc(tiles_step, 1)
                step(4)
                dve.scalar_tensor_tensor(out=place2[:, :, :], in0=first_tile[:, :].unsqueeze(1).to_broadcast([P, NJ, NE]),
                                         scalar=float(P), in1=place[:, 0:NJ, :], op0=ALU.mult,
                                         op1=ALU.add).then_inc(tiles_step, 1)
                dve.tensor_tensor(out=end_tile[:, :], in0=first_tile[:, :], in1=tiles[:, :],
                                  op=ALU.add).then_inc(tiles_step, 1)
                step(5)
                dve.tensor_tensor(out=picked[:, :, :, :], in0=choice[:, :, :, :],
                                  in1=place2[:, :, :].unsqueeze(1).to_broadcast([P, TOPK, NJ, NE]),
                                  op=ALU.mult).then_inc(tiles_step, 1)
                step(7)
                dve.tensor_reduce(out=slot_f[:, :, :], in_=picked[:, :, :, :], axis=AX.X, op=ALU.add).then_inc(slot_f_ready, 1)
                dve.wait_ge(slot_f_ready, s.count("C", 1, 1))
                dve.tensor_copy(slot[q][:, :, :], slot_f[:, :, :]).then_inc(slot_ready, 1)
                dve.tensor_tensor(out=passed[:, :, :], in0=tile_no[:, :].unsqueeze(2).to_broadcast([1, NT, NE]),
                                  in1=end_tile[0:1, :].unsqueeze(1).to_broadcast([1, NT, NE]),
                                  op=ALU.is_ge).then_inc(passed_ready, 1)
                dve.wait_ge(passed_ready, s.count("C", 1, 1))
                dve.tensor_reduce(out=passed_n[:, :], in_=passed[:, :, :], axis=AX.X, op=ALU.add).then_inc(tiles_step, 1)
                step(8)
                dve.tensor_scalar(out=tile_expert[q][:, :], in0=passed_n[:, :], scalar1=float(NE - 1), scalar2=None,
                                  op0=ALU.min).then_inc(expert_ready, 1)

            def stage_c(s, k):
                q = s.parity("C")
                if k == WHEN["C_gate"]:
                    dve.wait_ge(y_summed, s.count("C", 1, 1))
                    dve.tensor_tensor(out=y_even[q][:, :, :], in0=y_even[q][:, :, :], in1=gate_z[q][:, :, :],
                                      op=ALU.mult).then_inc(y_ready, 1)
                if k == TAKE["C_out"]:
                    dve.wait_ge(misc_filled, s.misc("C_out") + 1)
                    dve.tensor_tensor(out=res[:, :, :], in0=misc_tok, in1=x[q][:, :, :], op=ALU.add).then_inc(misc_taken, 1)
                if k == WHEN["C_route"]:
                    route(s)
                if k == WHEN["C_choose"]:
                    choose(s)
                if k == WHEN["C_weigh"]:
                    weigh(s)
                if k == WHEN["C_slots"]:
                    slots(s)

            def stage_a(s, k):
                q = s.parity("A")
                for tap in range(1, NTAP):
                    if k == WHEN["A_tap1" if tap == 1 else "A_taps"]:
                        for half in range(NH):
                            if tap == 1:
                                dve.wait_ge(tap0_ready, s.count("A", NH, half + 1))
                            else:
                                dve.wait_ge(tap_done, s.count("A", NH * 3, NH * (tap - 2) + half + 1))
                            dve.scalar_tensor_tensor(out=conv[:, half, :], in0=xi[:, half, tap:tap + T],
                                                     scalar=w_conv[:, half, tap:tap + 1], in1=conv[:, half, :],
                                                     op0=ALU.mult, op1=ALU.add).then_inc(tap_done, 1)
                if k == WHEN["A_silu"]:
                    for half in range(NH):
                        dve.wait_ge(th_conv_ready, s.count("A", NH, half + 1))
                        dve.scalar_tensor_tensor(out=act_x[:, half, :], in0=th_conv[:, half, :], scalar=1.0,
                                                 in1=conv[:, half, :], op0=ALU.add, op1=ALU.mult).then_inc(act_x_ready, 1)
                if k == WHEN["A_split"]:
                    dve.wait_ge(bc_ready, s.count("A", 5, 1))
                    dve.tensor_tensor(out=bc_rest, in0=bc_full, in1=bc[q][:, :], op=ALU.subtract).then_inc(rest_ready, 1)
                    dve.wait_ge(rest_ready, s.count("A", 1, 1))
                    dve.tensor_copy(bc_mid[:, :], bc_rest).then_inc(mid_ready, 1)
                    dve.wait_ge(mid_ready, s.count("A", 1, 1))
                    dve.tensor_tensor(out=bc_rest2[:, :], in0=bc_rest, in1=bc_mid[:, :],
                                      op=ALU.subtract).then_inc(rest2_ready, 1)
                    dve.tensor_copy(bc[q][2 * NS:4 * NS, :], bc_mid[2 * NS:4 * NS, :]).then_inc(bc_ready, 1)
                    dve.wait_ge(rest2_ready, s.count("A", 1, 1))
                    dve.tensor_copy(bc[q][4 * NS:6 * NS, :], bc_rest2[4 * NS:6 * NS, :]).then_inc(bc_ready, 3)
                if k == WHEN["A_delta"]:
                    dve.wait_ge(soft_ready, s.count("A", 1, 1))
                    wait(dve, decay_ready, s.count("A", NS * NH, -NS * NH))
                    dve.scalar_tensor_tensor(out=delta[q][:, :, :], in0=dt_raw[:, :, :], scalar=0.0, in1=dt_soft[:, :, :],
                                             op0=ALU.max, op1=ALU.add).then_inc(delta_ready, 1)

            def iteration(s):
                for k in range(UNITS):
                    if s.has("E") and k == WHEN["E_combine"] + 1:
                        dve.wait_ge(stats_ready, s.count("E", NJ, NJ))
                    if s.has("F") and k == TAKE["F_out"] + 1:
                        dve.wait_ge(stats2_ready, s.count("F", NJ, NJ))
                    if s.has("B") and k % 2 == 0:
                        multiply_b(s, k // 2)
                        scan(s, k // 2)
                    if s.has("tail"):
                        tile_silu(s, "tail", k + UNITS)
                    if s.has("D"):
                        tile_silu(s, "D", k)
                    if s.has("B") and k % 2 == 1:
                        multiply_c(s, "B", k // 2)
                    if s.has("tail"):
                        tile_hidden(s, "tail", k + UNITS)
                    if s.has("D"):
                        tile_hidden(s, "D", k)
                    if s.has("C"):
                        stage_c(s, k)
                    if s.has("E"):
                        q = s.parity("E")
                        if k == WHEN["E_combine"]:
                            combine(s)
                            dve.wait_ge(combined, s.count("E", TOPK * NJ, TOPK * NJ))
                            layer_norm_stats(acc[q], stats, stats_ready)
                        if k == WHEN["E_combine"] + 1:
                            layer_norm_aggregate(stats, mv, mv_ready)
                    if s.has("F"):
                        if k == TAKE["F_out"]:
                            wait(dve, stored, s.count("F", 16, 0))
                            dve.wait_ge(misc_filled, s.misc("F_out") + 1)
                            dve.tensor_tensor(out=y_out[:, :, :], in0=misc_tok, in1=x1[:, :, :], op=ALU.add).then_inc(misc_taken, 1)
                            dve.wait_ge(misc_taken, s.misc("F_out") + 1)
                            layer_norm_stats(y_out, stats2, stats2_ready)
                        if k == TAKE["F_out"] + 1:
                            layer_norm_aggregate(stats2, mv2, mv2_ready)
                    if s.has("A"):
                        stage_a(s, k)
                    if s.i0 == 0 and k in (22, 26):
                        w, half = ((w_gate, 1.0), (w_up, 0.5))[k == 26]
                        dve.wait_ge(expert_weights, 16 * N_EXPERT)
                        dve.tensor_scalar(out=w[:, :, :], in0=w[:, :, :], scalar1=w_rms2[:, 0:1], scalar2=half,
                                          op0=ALU.mult, op1=ALU.mult).then_inc(gates_scaled, 1)

            run_pipeline(dve, iteration)


_INS = ["L0_attn_hidden_states", "L0_attn_rms1_w", "L0_attn_rms2_w", "L0_attn_in_proj_w", "L0_attn_conv_w",
        "L0_attn_conv_b", "L0_attn_x_proj_w", "L0_attn_dt_proj_w", "L0_attn_dt_proj_b", "L0_attn_A_log",
        "L0_attn_D_skip", "L0_attn_out_proj_w", "L0_attn_router_w", "L0_attn_Wg", "L0_attn_Wu", "L0_attn_Wd",
        "L0_ffn_U1", "L0_ffn_V1", "L0_ffn_b1", "L0_ffn_U2", "L0_ffn_V2", "L0_ffn_b2"]


def kernel(**inputs):
    import concourse.bacc as bacc
    from concourse.bass_utils import run_bass_kernel_spmd

    nc = bacc.Bacc("TRN2", target_bir_lowering=False, num_devices=1)
    arrays, args = {}, []
    for name in _INS:
        a = np.ascontiguousarray(inputs[name])
        arrays[f"in_{name}"] = a
        args.append(nc.dram_tensor(f"in_{name}", a.shape, mybir.dt.from_np(a.dtype), kind="ExternalInput").ap())
    args.append(nc.dram_tensor("out_0", (B, L, D), F32, kind="ExternalOutput").ap())
    build(nc, *args)
    r = run_bass_kernel_spmd(nc, [arrays], core_ids=[0])
    return r.results[0]["out_0"]
```
